# Optimizing a Trainium2 kernel written in Bass

```python
import numpy as np
import jax
import jax.numpy as jnp

def _softmax(x, axis=-1):
    return jax.nn.softmax(x, axis=axis)

def _gelu(x):
    return jax.nn.gelu(x, approximate=True)

def _silu(x):
    return jax.nn.silu(x)

def _sigmoid(x):
    return jax.nn.sigmoid(x)

def _layernorm(x, axis=-1, eps=1e-05):
    m = jnp.mean(x, axis=axis, keepdims=True)
    v = jnp.var(x, axis=axis, keepdims=True)
    return (x - m) / jnp.sqrt(v + eps)

def _scatter_add(tgt, idx, src, axis=0):
    return tgt.at[idx].add(src)

def _segment_sum(src, seg, n):
    return jax.ops.segment_sum(src, seg, n)
kernel_name = 'mk_decoder_preln_d2_seqx_r4_3afa53'

def setup_inputs(seed: int=0):
    np.random.seed(seed)
    _w = jnp.asarray

    def _rec_inputs():
        import jax
        import jax.numpy as jnp
        _rk = jax.random.key(seed)
        x = 7.22e-05 + 1 * jax.random.normal(jax.random.fold_in(_rk, 1), (8, 512, 256), jnp.float32)
        _lenS = 512 - jax.random.randint(jax.random.fold_in(_rk, 7), (8,), 0, max(1, 512 // 4) + 1, jnp.int32)
        _lenS2 = 512 - jax.random.randint(jax.random.fold_in(_rk, 8), (8,), 0, max(1, 512 // 4) + 1, jnp.int32)
        _ctx_1024P = jax.random.normal(jax.random.fold_in(_rk, 11), (8, 16, 256), jnp.float32)
        _ctx_1024c = jax.random.dirichlet(jax.random.fold_in(_rk, 511), 0.3 * jnp.ones((16,), jnp.float32), (8, 512))
        _ctx_1024t = jnp.einsum('bsk,bkd->bsd', _ctx_1024c, _ctx_1024P)
        _ctx_1024t = _ctx_1024t * jax.lax.rsqrt(jnp.mean(jnp.square(_ctx_1024t)) + 1e-12) * 0.953939
        ctx_1024 = 4.13588e-05 + 0.999923 * (_ctx_1024t + 0.3 * jax.random.normal(jax.random.fold_in(_rk, 611), (8, 512, 256), jnp.float32))
        _validS = jnp.arange(512)[None, :] < _lenS[:, None]
        _validS2 = jnp.arange(512)[None, :] < _lenS2[:, None]
        _causal = jnp.tril(jnp.ones((512, 512), dtype=bool))
        mask_Bx1x1xS2_if1 = jnp.where(jnp.ones((8, 1, 1, 512), dtype=bool), 1, 0).astype(jnp.int32)
        return (x, ctx_1024, mask_Bx1x1xS2_if1)
    x, ctx_1024, mask_Bx1x1xS2_if1 = _rec_inputs()

    def _L0_attn_setup():
        import jax, jax.numpy as jnp
        import numpy as np
        D = 256
        K_LOW1 = D // 4
        K_LOW2 = D // 4

        def mix_precision_matmul(x, w):
            d = x.shape[-1]
            w1 = w[:K_LOW1]
            wh = w[K_LOW1:d - K_LOW2]
            w2 = w[d - K_LOW2:]
            y1 = jnp.matmul(x[..., :K_LOW1].astype(jnp.float16), w1.astype(jnp.float16)).astype(jnp.float32)
            yh = jnp.matmul(x[..., K_LOW1:d - K_LOW2], wh)
            y2 = jnp.matmul(x[..., d - K_LOW2:].astype(jnp.float16), w2.astype(jnp.float16)).astype(jnp.float32)
            return y1 + yh + y2
        key = jax.random.key(seed)
        k1, k2, k3, k4 = jax.random.split(key, 4)
        B, N, d = (8, 512, D)
        x = jax.random.normal(k1, (B, N, d), dtype=jnp.float32)
        weight_qkv = jax.random.normal(k2, (d, 3 * d), dtype=jnp.float32) * d ** (-0.5)
        out_w = jax.random.normal(k3, (d, d), dtype=jnp.float32) * d ** (-0.5)
        out_b = jax.random.normal(k4, (d,), dtype=jnp.float32) * 0.01
        return {'x': x, 'weight_qkv': weight_qkv, 'out_w': out_w, 'out_b': out_b}
    _L0_attn_all = _L0_attn_setup()
    _L0_attn_in = {k: v for k, v in _L0_attn_all.items() if k in ('weight_qkv', 'out_w', 'out_b')}
    del _L0_attn_all

    def _L0_xattn_setup():
        import jax, jax.numpy as jnp
        import numpy as np
        D_MODEL = 256
        HEADS = 16
        D_HEAD = D_MODEL // HEADS
        SEQ = 512
        C = 2
        K_TOP = int(C * np.log(SEQ))
        key = jax.random.key(seed)
        ks = jax.random.split(key, 5)
        s = 0.02
        return {'Q': jax.random.normal(ks[0], (4, SEQ, D_MODEL), jnp.float32), 'K': jax.random.normal(ks[1], (4, SEQ, D_MODEL), jnp.float32), 'V': jax.random.normal(ks[2], (4, SEQ, D_MODEL), jnp.float32), 'Wq': jax.random.normal(ks[3], (D_MODEL, D_HEAD), jnp.float32) * s, 'bq': jnp.zeros((D_HEAD,), jnp.float32), 'Wout': jax.random.normal(ks[4], (HEADS * D_HEAD, D_MODEL), jnp.float32) * s, 'bout': jnp.zeros((D_MODEL,), jnp.float32)}
    _L0_xattn_all = _L0_xattn_setup()
    _L0_xattn_in = {k: v for k, v in _L0_xattn_all.items() if k in ('Wq', 'bq', 'Wout', 'bout')}
    del _L0_xattn_all

    def _L0_ffn_setup():
        import jax, jax.numpy as jnp
        import numpy as np
        TOP_K = 4
        CAP_FACTOR = 4

        def swiglu(x, w1, w2, w3):
            return jax.nn.silu(x @ w1) * (x @ w3) @ w2
        key = jax.random.key(seed)
        ks = jax.random.split(key, 8)
        B, S, D, H, E = (2, 512, 256, 128, 32)
        Hs = 2 * H
        sd = lambda *sh: 1.0 / np.sqrt(sh[-2])
        x = jax.random.normal(ks[0], (B, S, D), dtype=jnp.float32)
        Wg = jax.random.normal(ks[1], (D, E), dtype=jnp.float32) * (1.0 / np.sqrt(D))
        W1 = jax.random.normal(ks[2], (E, D, H), dtype=jnp.float32) * (1.0 / np.sqrt(D))
        W3 = jax.random.normal(ks[3], (E, D, H), dtype=jnp.float32) * (1.0 / np.sqrt(D))
        W2 = jax.random.normal(ks[4], (E, H, D), dtype=jnp.float32) * (1.0 / np.sqrt(H))
        Ws1 = jax.random.normal(ks[5], (D, Hs), dtype=jnp.float32) * (1.0 / np.sqrt(D))
        Ws3 = jax.random.normal(ks[6], (D, Hs), dtype=jnp.float32) * (1.0 / np.sqrt(D))
        Ws2 = jax.random.normal(ks[7], (Hs, D), dtype=jnp.float32) * (1.0 / np.sqrt(Hs))
        return {'x': x, 'Wg': Wg, 'W1': W1, 'W2': W2, 'W3': W3, 'Ws1': Ws1, 'Ws2': Ws2, 'Ws3': Ws3}
    _L0_ffn_all = _L0_ffn_setup()
    _L0_ffn_in = {k: v for k, v in _L0_ffn_all.items() if k in ('Wg', 'W1', 'W2', 'W3', 'Ws1', 'Ws2', 'Ws3')}
    del _L0_ffn_all

    def _L1_attn_setup():
        import jax, jax.numpy as jnp
        import numpy as np
        B, S, D, O = (8, 512, 256, 256)
        key = jax.random.key(seed)
        k_in, k_a, k_bc = jax.random.split(key, 3)
        inputs = jax.random.normal(k_in, (B, S, D), dtype=jnp.float32)
        A = jax.random.uniform(k_a, (D,), minval=-0.99, maxval=0.99, dtype=jnp.float32)
        BC = jax.random.normal(k_bc, (D, O), dtype=jnp.float32) / D
        return {'inputs': inputs, 'A': A, 'BC': BC}
    _L1_attn_all = _L1_attn_setup()
    _L1_attn_in = {k: v for k, v in _L1_attn_all.items() if k in ('A', 'BC')}
    del _L1_attn_all

    def _L1_xattn_setup():
        import jax, jax.numpy as jnp
        import numpy as np
        EMBED_SIZE = 256
        HEADS = 16
        HEAD_DIM = EMBED_SIZE // HEADS
        key = jax.random.key(seed)
        ks = jax.random.split(key, 9)
        N, L = (2, 512)
        inv = 1.0 / np.sqrt(HEAD_DIM)
        return {'values': jax.random.normal(ks[0], (N, L, EMBED_SIZE), dtype=jnp.float32), 'keys': jax.random.normal(ks[1], (N, L, EMBED_SIZE), dtype=jnp.float32), 'query': jax.random.normal(ks[2], (N, L, EMBED_SIZE), dtype=jnp.float32), 'mask': jnp.ones((N, 1, 1, L), dtype=jnp.int32), 'Wv': jax.random.normal(ks[3], (HEAD_DIM, HEAD_DIM), dtype=jnp.float32) * inv, 'Wk': jax.random.normal(ks[4], (HEAD_DIM, HEAD_DIM), dtype=jnp.float32) * inv, 'Wq': jax.random.normal(ks[5], (HEAD_DIM, HEAD_DIM), dtype=jnp.float32) * inv, 'Wo': jax.random.normal(ks[6], (EMBED_SIZE, EMBED_SIZE), dtype=jnp.float32) / np.sqrt(EMBED_SIZE), 'bo': jnp.zeros((EMBED_SIZE,), dtype=jnp.float32)}
    _L1_xattn_all = _L1_xattn_setup()
    _L1_xattn_in = {k: v for k, v in _L1_xattn_all.items() if k in ('Wv', 'Wk', 'Wq', 'Wo', 'bo')}
    del _L1_xattn_all

    def _L1_ffn_setup():
        import jax, jax.numpy as jnp
        import numpy as np
        TOPK = 8
        NUM_EXPERTS = 64
        FFN = 768
        CAPACITY = 160

        def _swiglu(x, w1, w2):
            h = x @ w1.T
            x1, x2 = jnp.split(h, 2, axis=-1)
            return x1 * jax.nn.silu(x2) @ w2.T
        key = jax.random.key(seed)
        ks = jax.random.split(key, 6)
        B, S, H = (1, 128, 256)
        scale = 0.02
        return {'hidden_states': jax.random.normal(ks[0], (B, S, H), jnp.float32), 'wg': jax.random.normal(ks[1], (NUM_EXPERTS, H), jnp.float32) * scale, 'shared_w1': jax.random.normal(ks[2], (2 * FFN, H), jnp.float32) * scale, 'shared_w2': jax.random.normal(ks[3], (H, FFN), jnp.float32) * scale, 'expert_w1': jax.random.normal(ks[4], (NUM_EXPERTS, 2 * FFN, H), jnp.float32) * scale, 'expert_w2': jax.random.normal(ks[5], (NUM_EXPERTS, H, FFN), jnp.float32) * scale}
    _L1_ffn_all = _L1_ffn_setup()
    _L1_ffn_in = {k: v for k, v in _L1_ffn_all.items() if k in ('wg', 'shared_w1', 'shared_w2', 'expert_w1', 'expert_w2')}
    del _L1_ffn_all
    return {'x': x, 'ctx_1024': ctx_1024, 'mask_Bx1x1xS2_if1': mask_Bx1x1xS2_if1, 'L0_attn_weight_qkv': _L0_attn_in['weight_qkv'], 'L0_attn_out_w': _L0_attn_in['out_w'], 'L0_attn_out_b': _L0_attn_in['out_b'], 'L0_xattn_Wq': _L0_xattn_in['Wq'], 'L0_xattn_bq': _L0_xattn_in['bq'], 'L0_xattn_Wout': _L0_xattn_in['Wout'], 'L0_xattn_bout': _L0_xattn_in['bout'], 'L0_ffn_Wg': _L0_ffn_in['Wg'], 'L0_ffn_W1': _L0_ffn_in['W1'], 'L0_ffn_W2': _L0_ffn_in['W2'], 'L0_ffn_W3': _L0_ffn_in['W3'], 'L0_ffn_Ws1': _L0_ffn_in['Ws1'], 'L0_ffn_Ws2': _L0_ffn_in['Ws2'], 'L0_ffn_Ws3': _L0_ffn_in['Ws3'], 'L1_attn_A': _L1_attn_in['A'], 'L1_attn_BC': _L1_attn_in['BC'], 'L1_xattn_Wv': _L1_xattn_in['Wv'], 'L1_xattn_Wk': _L1_xattn_in['Wk'], 'L1_xattn_Wq': _L1_xattn_in['Wq'], 'L1_xattn_Wo': _L1_xattn_in['Wo'], 'L1_xattn_bo': _L1_xattn_in['bo'], 'L1_ffn_wg': _L1_ffn_in['wg'], 'L1_ffn_shared_w1': _L1_ffn_in['shared_w1'], 'L1_ffn_shared_w2': _L1_ffn_in['shared_w2'], 'L1_ffn_expert_w1': _L1_ffn_in['expert_w1'], 'L1_ffn_expert_w2': _L1_ffn_in['expert_w2']}

def reference(x, ctx_1024, mask_Bx1x1xS2_if1, L0_attn_weight_qkv, L0_attn_out_w, L0_attn_out_b, L0_xattn_Wq, L0_xattn_bq, L0_xattn_Wout, L0_xattn_bout, L0_ffn_Wg, L0_ffn_W1, L0_ffn_W2, L0_ffn_W3, L0_ffn_Ws1, L0_ffn_Ws2, L0_ffn_Ws3, L1_attn_A, L1_attn_BC, L1_xattn_Wv, L1_xattn_Wk, L1_xattn_Wq, L1_xattn_Wo, L1_xattn_bo, L1_ffn_wg, L1_ffn_shared_w1, L1_ffn_shared_w2, L1_ffn_expert_w1, L1_ffn_expert_w2):
    import jax
    import jax.numpy as jnp

    def _L0_attn_ref(x, weight_qkv, out_w, out_b):
        import jax, jax.numpy as jnp
        import numpy as np
        D = 256
        K_LOW1 = D // 4
        K_LOW2 = D // 4

        def mix_precision_matmul(x, w):
            d = x.shape[-1]
            w1 = w[:K_LOW1]
            wh = w[K_LOW1:d - K_LOW2]
            w2 = w[d - K_LOW2:]
            y1 = jnp.matmul(x[..., :K_LOW1].astype(jnp.float16), w1.astype(jnp.float16)).astype(jnp.float32)
            yh = jnp.matmul(x[..., K_LOW1:d - K_LOW2], wh)
            y2 = jnp.matmul(x[..., d - K_LOW2:].astype(jnp.float16), w2.astype(jnp.float16)).astype(jnp.float32)
            return y1 + yh + y2
        d = x.shape[-1]
        qkv = mix_precision_matmul(x, weight_qkv)
        q, k, v = jnp.split(qkv, 3, axis=-1)
        q = q / jnp.sqrt(jnp.asarray(d, dtype=q.dtype))
        qk = jnp.einsum('bqd,bkd->bqk', q, k)
        s = jax.nn.softmax(qk, axis=-1)
        y = jnp.einsum('bqk,bkd->bqd', s, v)
        return jnp.matmul(y, out_w.T) + out_b

    def _L0_xattn_ref(Q, K, V, Wq, bq, Wout, bout):
        import jax, jax.numpy as jnp
        import numpy as np
        D_MODEL = 256
        HEADS = 16
        D_HEAD = D_MODEL // HEADS
        SEQ = 512
        C = 2
        K_TOP = int(C * np.log(SEQ))
        B, L, _ = Q.shape
        q = (Q @ Wq + bq).transpose(0, 2, 1)
        k_ = (K @ Wq + bq).transpose(0, 2, 1)
        v = (V @ Wq + bq).transpose(0, 2, 1)
        Qf = jnp.fft.fft(q.astype(jnp.complex64))
        Kf = jnp.fft.fft(k_.astype(jnp.complex64))
        corr = jnp.real(jnp.fft.ifft(Qf * jnp.conj(Kf)))
        corr = corr.mean(axis=(0, 1))
        W_topk, I_topk = jax.lax.top_k(corr, K_TOP)
        W_topk = jax.nn.softmax(W_topk)

        def body(R, ws):
            w, shift = ws
            return (R + w * jnp.roll(v, -shift, axis=-1), None)
        R3, _ = jax.lax.scan(body, jnp.zeros_like(v), (W_topk, I_topk))
        R = jnp.broadcast_to(R3[:, None], (B, HEADS, D_HEAD, L)).reshape(B, L, HEADS * D_HEAD)
        return R @ Wout + bout

    def _L0_ffn_ref(x, Wg, W1, W2, W3, Ws1, Ws2, Ws3):
        import jax, jax.numpy as jnp
        import numpy as np
        TOP_K = 4
        CAP_FACTOR = 4

        def swiglu(x, w1, w2, w3):
            return jax.nn.silu(x @ w1) * (x @ w3) @ w2
        B, S, D = x.shape
        E = Wg.shape[1]
        T = B * S
        xf = x.reshape(T, D)
        scores = jax.nn.softmax(xf @ Wg, axis=-1)
        weights, indices = jax.lax.top_k(scores, TOP_K)
        P = T * TOP_K
        pair_expert = indices.reshape(-1)
        pair_token = jnp.repeat(jnp.arange(T), TOP_K)
        pair_weight = weights.reshape(-1).astype(xf.dtype)
        C = CAP_FACTOR * P // E
        y = jnp.zeros_like(xf)
        for e in range(E):
            pos = jnp.nonzero(pair_expert == e, size=C, fill_value=P)[0]
            valid = pos < P
            safe = jnp.minimum(pos, P - 1)
            tok = jnp.where(valid, pair_token[safe], 0)
            w = jnp.where(valid, pair_weight[safe], 0.0)
            xg = xf[tok]
            out = swiglu(xg, W1[e], W2[e], W3[e]) * w[:, None]
            y = y.at[tok].add(out)
        z = swiglu(xf, Ws1, Ws2, Ws3)
        return (y + z).reshape(B, S, D)

    def _L1_attn_ref(inputs, A, BC):
        import jax, jax.numpy as jnp
        import numpy as np
        B, S, D, O = (8, 512, 256, 256)
        x_tfirst = jnp.swapaxes(inputs, 0, 1)

        def step(h, x_t):
            h = h * A + x_t
            return (h, h)
        h0 = jnp.zeros((inputs.shape[0], A.shape[0]), dtype=inputs.dtype)
        _, hs = jax.lax.scan(step, h0, x_tfirst)
        out = jnp.einsum('sbd,do->bso', hs, BC)
        return out

    def _L1_xattn_ref(values, keys, query, mask, Wv, Wk, Wq, Wo, bo):
        import jax, jax.numpy as jnp
        import numpy as np
        EMBED_SIZE = 256
        HEADS = 16
        HEAD_DIM = EMBED_SIZE // HEADS
        N, q_len, E = query.shape
        k_len = keys.shape[1]
        v_len = values.shape[1]
        H, D = (HEADS, HEAD_DIM)
        v = values.reshape(N, v_len, H, D)
        k = keys.reshape(N, k_len, H, D)
        q = query.reshape(N, q_len, H, D)
        v = jnp.einsum('nlhd,ed->nlhe', v, Wv)
        k = jnp.einsum('nlhd,ed->nlhe', k, Wk)
        q = jnp.einsum('nqhd,ed->nqhe', q, Wq)
        energy = jnp.einsum('nqhd,nkhd->nhqk', q, k)
        energy = jnp.where(mask == 0, jnp.float32(-1e+20), energy)
        attention = jax.nn.softmax(energy / jnp.sqrt(jnp.float32(E)), axis=3)
        out = jnp.einsum('nhql,nlhd->nqhd', attention, v).reshape(N, q_len, H * D)
        out = out @ Wo.T + bo
        return out

    def _L1_ffn_ref(hidden_states, wg, shared_w1, shared_w2, expert_w1, expert_w2):
        import jax, jax.numpy as jnp
        import numpy as np
        TOPK = 8
        NUM_EXPERTS = 64
        FFN = 768
        CAPACITY = 160

        def _swiglu(x, w1, w2):
            h = x @ w1.T
            x1, x2 = jnp.split(h, 2, axis=-1)
            return x1 * jax.nn.silu(x2) @ w2.T
        B, S, H = hidden_states.shape
        T = B * S
        x = hidden_states.reshape(T, H)
        shared_out = _swiglu(x, shared_w1, shared_w2)
        logits = x.astype(jnp.float32) @ wg.T
        gates = jax.nn.softmax(logits, axis=-1)
        w_topk, idx_topk = jax.lax.top_k(gates, TOPK)
        denom = jnp.maximum(w_topk.sum(-1, keepdims=True), jnp.finfo(jnp.float32).eps)
        w_topk = w_topk / denom
        A = T * TOPK
        flat_e = idx_topk.reshape(A)
        flat_w = w_topk.reshape(A)
        flat_t = jnp.repeat(jnp.arange(T), TOPK)
        order = jnp.argsort(flat_e)
        se, st, sw = (flat_e[order], flat_t[order], flat_w[order])
        counts = jnp.zeros(NUM_EXPERTS, jnp.int32).at[flat_e].add(1)
        starts = jnp.cumsum(counts) - counts
        rank = jnp.arange(A) - starts[se]
        valid = rank < CAPACITY
        buf = jnp.zeros((NUM_EXPERTS, CAPACITY, H), x.dtype).at[se, rank].set(x[st], mode='drop')
        h = jnp.einsum('ech,efh->ecf', buf, expert_w1)
        x1, x2 = jnp.split(h, 2, axis=-1)
        out = jnp.einsum('ecf,ehf->ech', x1 * jax.nn.silu(x2), expert_w2)
        y = out[se, jnp.clip(rank, 0, CAPACITY - 1)]
        y = jnp.where(valid[:, None], y * sw[:, None].astype(y.dtype), 0.0)
        combined = jnp.zeros((T, H), x.dtype).at[st].add(y)
        return (shared_out + combined).reshape(B, S, H)
    x = x + _L0_attn_ref(_layernorm(x, axis=-1), L0_attn_weight_qkv, L0_attn_out_w, L0_attn_out_b)
    x = x + _L0_xattn_ref(_layernorm(x, axis=-1), ctx_1024, ctx_1024, L0_xattn_Wq, L0_xattn_bq, L0_xattn_Wout, L0_xattn_bout)
    x = x + _L0_ffn_ref(_layernorm(x, axis=-1), L0_ffn_Wg, L0_ffn_W1, L0_ffn_W2, L0_ffn_W3, L0_ffn_Ws1, L0_ffn_Ws2, L0_ffn_Ws3)
    x = x + _L1_attn_ref(_layernorm(x, axis=-1), L1_attn_A, L1_attn_BC)
    x = x + _L1_xattn_ref(ctx_1024, ctx_1024, _layernorm(x, axis=-1), mask_Bx1x1xS2_if1, L1_xattn_Wv, L1_xattn_Wk, L1_xattn_Wq, L1_xattn_Wo, L1_xattn_bo)
    x = x + _L1_ffn_ref(_layernorm(x, axis=-1), L1_ffn_wg, L1_ffn_shared_w1, L1_ffn_shared_w2, L1_ffn_expert_w1, L1_ffn_expert_w2)
    return x

_drawn_inputs = setup_inputs


def setup_inputs(seed=0):
    import zlib

    import numpy as np

    out = dict(_drawn_inputs(seed))
    spreads = {'L0_xattn_bq': (0.0, 0.1), 'L0_xattn_bout': (0.0, 0.1), 'L1_xattn_bo': (0.0, 0.1)}
    factors = {'L0_attn_out_b': 4.946,
     'L1_ffn_wg': 8.0,
     'L1_ffn_expert_w1': 8.0,
     'L1_ffn_expert_w2': 8.0,
     'L1_ffn_shared_w1': 8.0,
     'L1_ffn_shared_w2': 8.0}
    for name, (base, spread) in spreads.items():
        noise = np.random.default_rng([zlib.crc32(name.encode()), seed]).standard_normal(out[name].shape)
        drawn = base * np.exp(spread * noise) if base else spread * noise
        out[name] = jnp.asarray(drawn.astype(out[name].dtype))
    for name, factor in factors.items():
        out[name] = (out[name] * factor).astype(out[name].dtype)
    return out
```

```python
from contextlib import ExitStack

import numpy as np

import concourse.bass as bass
from concourse import mybir
from concourse.alu_op_type import AluOpType as ALU

F32 = mybir.dt.float32
F16 = mybir.dt.float16
BF16 = mybir.dt.bfloat16
I32 = mybir.dt.int32
U32 = mybir.dt.uint32
ACT = mybir.ActivationFunctionType
AX = mybir.AxisListType

P = 128
B, S, D = 8, 512, 256
NT = B * S // P
TB = S // P
DC = D // P
TURNS = B // 2
EPS = 1e-5


class Kit:

    def __init__(self, nc, ctx, prefix):
        self.nc, self.ctx, self.prefix, self.sems = nc, ctx, prefix, []

    def sb(self, name, shape, dtype=F32):
        return self.ctx.enter_context(self.nc.sbuf_tensor(self.prefix + name, shape, dtype))

    def ps(self, name, shape, dtype=F32):
        return self.ctx.enter_context(self.nc.psum_tensor(self.prefix + name, shape, dtype))

    def sem(self, name):
        self.sems.append(self.ctx.enter_context(self.nc.semaphore(self.prefix + name)))
        return self.sems[-1]

    def clear(self):
        with self.nc.Block() as block:
            @block.sync
            def _(sp):
                for sem in self.sems:
                    sp.sem_clear(sem)


class Chain:

    def __init__(self, eng, sem):
        self.eng, self.sem, self.base, self.n = eng, sem, 0, 0

    def turn(self, base):
        self.base, self.n = base, 0

    def tick(self, ins):
        ins.then_inc(self.sem, 1)
        self.n += 1

    def wait(self):
        self.eng.wait_ge(self.sem, self.base + self.n)

    def link(self, ins):
        self.tick(ins)
        self.wait()


def identity_stage(nc, ctx, ident, ident_bf):
    k = Kit(nc, ctx, "id_")
    zero_done, ident_done = k.sem("zero_done"), k.sem("ident_done")
    with nc.Block() as block:
        @block.gpsimd
        def _(pool):
            nc.gpsimd.memset(ident[:], 0.0).then_inc(zero_done, 1)
            pool.wait_ge(zero_done, 1)
            nc.gpsimd.affine_select(out=ident[:], in_=ident[:], compare_op=ALU.not_equal, fill=1.0, base=0,
                                    pattern=[[-1, P]], channel_multiplier=1).then_inc(ident_done, 1)
            pool.wait_ge(ident_done, 1)
            nc.gpsimd.tensor_copy(ident_bf[:], ident[:]).then_inc(ident_done, 1)
            pool.wait_ge(ident_done, 2)


def norm_stats(nc, ctx, name, x, mean, rstd):
    with ExitStack() as own:
        k = Kit(nc, own, name + "_st_")
        s = Kit(nc, own, name + "_st_")
        stats = k.sb("stats", [P, NT, 6])
        half_diff = k.sb("half_diff", [P, NT])
        var = k.sb("var", [P, NT])
        dev = k.sb("dev", [P, NT])
        dve_done, dev_done, stats_done, var_done = s.sem("dve_done"), s.sem("dev_done"), s.sem("stats_done"), s.sem("var_done")
        with nc.Block() as block:
            @block.vector
            def _(dve):
                with dve.Fori(0, NT // 4) as i:
                    for j in range(4):
                        nc.vector.bn_stats(stats[:, i * 4 + j, :], x[:, i * 4 + j, :]).then_inc(stats_done, 1)
                dve.wait_ge(stats_done, NT)
                chain = Chain(dve, dve_done)
                me, mo = stats[:, :, 1], stats[:, :, 4]
                chain.link(nc.vector.tensor_tensor(mean[:], me, mo, ALU.add))
                chain.link(nc.vector.tensor_scalar(mean[:], mean[:], 0.5, None, ALU.mult))
                chain.link(nc.vector.tensor_tensor(half_diff[:], me, mo, ALU.subtract))
                chain.link(nc.vector.scalar_tensor_tensor(half_diff[:], half_diff[:], 0.25, half_diff[:], ALU.mult, ALU.mult))
                chain.link(nc.vector.tensor_tensor(var[:], stats[:, :, 2], stats[:, :, 5], ALU.add))
                chain.link(nc.vector.scalar_tensor_tensor(var[:], var[:], 1.0 / D, half_diff[:], ALU.mult, ALU.add))
                nc.vector.tensor_scalar(var[:], var[:], EPS, None, ALU.add).then_inc(var_done, 1)
                dve.wait_ge(dev_done, 1)
                chain.link(nc.vector.reciprocal(rstd[:], dev[:]))

            @block.scalar
            def _(act):
                act.wait_ge(var_done, 1)
                nc.scalar.activation(dev[:], var[:], ACT.Sqrt).then_inc(dev_done, 1)
        s.clear()


def mix_attention(nc, ctx, x, ident, ident_bf, mean, rstd, w_qkv, out_wT, out_b):
    with ExitStack() as own:
        k = Kit(nc, own, "at_")
        s = Kit(nc, own, "at_")
        Q4 = D // 4
        xn = k.sb("xn", [P, 2, TB, D])
        xT_low = k.sb("xT_low", [P, 2, S], F16)
        xT_high = k.sb("xT_high", [P, 2, S])
        w_low32 = k.sb("w_low32", [P, 3 * D])
        w_low = k.sb("w_low", [P, 3 * D], F16)
        w_high = k.sb("w_high", [P, 3 * D])
        w_out = k.sb("w_out", [P, DC, D])
        bias = k.sb("bias", [P, D])
        qT = k.sb("qT", [P, 2, DC, S])
        kT = k.sb("kT", [P, 2, DC, S])
        v = k.sb("v", [P, 2, TB, D])
        prob = k.sb("prob", [P, 2, TB, S])
        probT = k.sb("probT", [P, 2, TB, S])
        yT = k.sb("yT", [P, 2, DC, S])
        nmax = k.sb("nmax", [P, 2, TB])
        total = k.sb("total", [P, 2, TB])
        rtotal = k.sb("rtotal", [P, 2, TB])
        turned = k.ps("turned", [P, 2, S])
        proj = k.ps("proj", [P, 2, S])
        score = k.ps("score", [P, 2, S])
        outp = k.ps("outp", [P, 2, S])
        loaded, w_ready = s.sem("loaded"), s.sem("w_ready")
        xn_ready, batch_done = s.sem("xn_ready"), s.sem("batch_done")
        turned_full, turned_free = s.sem("turned_full"), s.sem("turned_free")
        proj_full, proj_free = s.sem("proj_full"), s.sem("proj_free")
        score_full, score_free = s.sem("score_full"), s.sem("score_free")
        out_full, out_free = s.sem("out_full"), s.sem("out_free")
        nmax_ready, rtot_ready, bias_added = s.sem("nmax_ready"), s.sem("rtot_ready"), s.sem("bias_added")
        NSC, NOUT = 4, 2
        NTURN, NPROJ = 12, 16

        with nc.Block() as block:
            @block.sync
            def _(sp):
                sp.dma_start(w_low32[0:Q4, :], w_qkv[0:Q4, :]).then_inc(loaded, 16)
                sp.dma_start(w_low32[Q4:P, :], w_qkv[D - Q4:D, :]).then_inc(loaded, 16)
                sp.dma_start(w_high[:], w_qkv[Q4:D - Q4, :]).then_inc(loaded, 16)
                sp.dma_start(w_out[:], out_wT.rearrange("(c p) n -> p c n", p=P)).then_inc(loaded, 16)
                sp.dma_start(bias[:], out_b.rearrange("(a n) -> a n", a=1).to_broadcast([P, D])).then_inc(loaded, 16)

            @block.gpsimd
            def _(pool):
                pool.wait_ge(loaded, 80)
                with pool.Fori(0, B) as b:
                    pool.wait_ge(xn_ready, b * TB + TB)
                    for j in range(TB):
                        last = nc.gpsimd.tensor_tensor(x[:, b * TB + j, :], x[:, b * TB + j, :], bias[:], ALU.add)
                    last.then_inc(bias_added, 1)

            @block.tensor
            def _(pe):
                pe.sem_inc(batch_done, 2)
                pe.wait_ge(w_ready, 1)
                with pe.Fori(0, TURNS) as i:
                    for sl in range(2):
                        b = i * 2 + sl
                        pe.wait_ge(xn_ready, b * TB + TB)
                        for half in range(2):
                            pe.wait_ge(turned_free, i * NTURN + 2 * sl + half + 1)
                            for j in range(TB):
                                last = nc.tensor.transpose(turned[:, half, j * P:(j + 1) * P],
                                                           xn[:, sl, j, half * P:(half + 1) * P], ident[:])
                            last.then_inc(turned_full, 1)
                        pe.wait_ge(turned_free, i * NTURN + 2 * sl + 2 + 2)
                        for m in range(4):
                            pe.wait_ge(proj_free, i * NPROJ + 6 * sl + m + 1)
                            cols = slice(m * P, (m + 1) * P)
                            nc.tensor.matmul(proj[:, m % 2, :], w_high[:, cols], xT_high[:, sl, :], start=True, stop=False)
                            nc.tensor.matmul(proj[:, m % 2, :], w_low[:, cols], xT_low[:, sl, :], start=False, stop=True)\
                                .then_inc(proj_full, 1)
                        for m in range(2):
                            pe.wait_ge(proj_free, i * NPROJ + 6 * sl + 4 + m + 1)
                            for j in range(2):
                                t = slice((2 * m + j) * P, (2 * m + j + 1) * P)
                                o = proj[:, m, j * D:(j + 1) * D]
                                nc.tensor.matmul(o, xT_high[:, sl, t], w_high[:, 2 * D:3 * D], start=True, stop=False)
                                last = nc.tensor.matmul(o, xT_low[:, sl, t], w_low[:, 2 * D:3 * D], start=False, stop=True)
                            last.then_inc(proj_full, 1)
                    for sl in range(2):
                        b = i * 2 + sl
                        pe.wait_ge(proj_free, i * NPROJ + 6 * sl + 4 + 2)
                        for qc in range(TB):
                            pe.wait_ge(score_free, b * NSC + qc + 1)
                            for c in range(DC):
                                last = nc.tensor.matmul(score[:, qc % 2, :], qT[:, sl, c, qc * P:(qc + 1) * P],
                                                        kT[:, sl, c, :], start=(c == 0), stop=(c == DC - 1))
                            last.then_inc(score_full, 1)
                    for sl in range(2):
                        b = i * 2 + sl
                        pe.wait_ge(score_free, b * NSC + TB + 2)
                        for kc in range(TB):
                            pe.wait_ge(turned_free, i * NTURN + 4 + TB * sl + kc + 1)
                            for qc in range(TB):
                                last = nc.tensor.transpose(turned[:, kc % 2, qc * P:(qc + 1) * P],
                                                           prob[:, sl, qc, kc * P:(kc + 1) * P], ident[:])
                            last.then_inc(turned_full, 1)
                        pe.wait_ge(turned_free, i * NTURN + 4 + TB * sl + TB + 2)
                        for c in range(DC):
                            pe.wait_ge(proj_free, i * NPROJ + 12 + 2 * sl + c + 1)
                            for kc in range(TB):
                                last = nc.tensor.matmul(proj[:, c, :], v[:, sl, kc, c * P:(c + 1) * P], probT[:, sl, kc, :],
                                                        start=(kc == 0), stop=(kc == TB - 1))
                            last.then_inc(proj_full, 1)
                        pe.wait_ge(proj_free, i * NPROJ + 12 + 2 * sl + 2 + 2)
                        for m in range(2):
                            pe.wait_ge(out_free, b * NOUT + m + 1)
                            for j in range(2):
                                t = slice((2 * m + j) * P, (2 * m + j + 1) * P)
                                for c in range(DC):
                                    last = nc.tensor.matmul(outp[:, m, j * D:(j + 1) * D], yT[:, sl, c, t], w_out[:, c, :],
                                                            start=(c == 0), stop=(c == DC - 1))
                            last.then_inc(out_full, 1)
                        pe.wait_ge(out_full, b * NOUT + 2)
                        pe.sem_inc(batch_done, 1)

            @block.scalar
            def _(act):
                act.sem_inc(turned_free, 2)
                act.sem_inc(score_free, 2)
                with act.Fori(0, TURNS) as i:
                    for sl in range(2):
                        b = i * 2 + sl
                        act.wait_ge(batch_done, b + 1)
                        for half in range(2):
                            act.wait_ge(turned_full, i * NTURN + 2 * sl + half + 1)
                            dst = xT_low[:, sl, :] if half == 0 else xT_high[:, sl, :]
                            nc.scalar.activation(dst, turned[:, half, :], ACT.Copy).then_inc(turned_free, 1)
                    for sl in range(2):
                        b = i * 2 + sl
                        for qc in range(TB):
                            act.wait_ge(nmax_ready, b * NSC + qc + 1)
                            nc.scalar.activation(prob[:, sl, qc, :], score[:, qc % 2, :], ACT.Exp,
                                                 bias=nmax[:, sl, qc:qc + 1],
                                                 accum_out=total[:, sl, qc:qc + 1]).then_inc(score_free, 1)
                    for sl in range(2):
                        b = i * 2 + sl
                        for kc in range(TB):
                            act.wait_ge(turned_full, i * NTURN + 4 + TB * sl + kc + 1)
                            nc.scalar.activation(probT[:, sl, kc, :], turned[:, kc % 2, :], ACT.Copy).then_inc(turned_free, 1)

            @block.vector
            def _(dve):
                dve.wait_ge(loaded, 80)
                nc.vector.tensor_copy(w_low[:], w_low32[:]).then_inc(w_ready, 1)
                dve.sem_inc(proj_free, 2)
                dve.sem_inc(out_free, 2)
                with dve.Fori(0, TURNS) as i:
                    for sl in range(2):
                        b = i * 2 + sl
                        dve.wait_ge(batch_done, b + 1)
                        for j in range(TB):
                            t = b * TB + j
                            for half, cols in enumerate((slice(0, 4, 3), slice(1, 3))):
                                last = nc.vector.tensor_scalar(
                                    xn[:, sl, j, half * P:(half + 1) * P].rearrange("p (a c) -> p a c", a=2),
                                    x[:, t, :].rearrange("p (a c) -> p a c", a=4)[:, cols, :],
                                    mean[:, bass.ds(t, 1)], rstd[:, bass.ds(t, 1)], ALU.subtract, ALU.mult)
                            last.then_inc(xn_ready, 1)
                    for sl in range(2):
                        b = i * 2 + sl
                        for m in range(6):
                            dve.wait_ge(proj_full, i * NPROJ + 6 * sl + m + 1)
                            if m < 2:
                                nc.vector.tensor_scalar(qT[:, sl, m, :], proj[:, m % 2, :], D ** -0.5, None, ALU.mult)\
                                    .then_inc(proj_free, 1)
                            elif m < 4:
                                nc.vector.tensor_copy(kT[:, sl, m - 2, :], proj[:, m % 2, :]).then_inc(proj_free, 1)
                            else:
                                j = 2 * (m - 4)
                                nc.vector.tensor_copy(v[:, sl, j:j + 2, :].rearrange("p j n -> p (j n)"), proj[:, m % 2, :])\
                                    .then_inc(proj_free, 1)
                    for sl in range(2):
                        b = i * 2 + sl
                        for qc in range(TB):
                            dve.wait_ge(score_full, b * NSC + qc + 1)
                            nc.vector.tensor_reduce(nmax[:, sl, qc:qc + 1], score[:, qc % 2, :], AX.X, ALU.max, negate=True)\
                                .then_inc(nmax_ready, 1)
                    for sl in range(2):
                        b = i * 2 + sl
                        dve.wait_ge(score_free, b * NSC + TB + 2)
                        nc.vector.reciprocal(rtotal[:, sl, :], total[:, sl, :]).then_inc(rtot_ready, 1)
                        for c in range(DC):
                            dve.wait_ge(proj_full, i * NPROJ + 12 + 2 * sl + c + 1)
                            nc.vector.tensor_copy(yT[:, sl, c, :], proj[:, c, :]).then_inc(proj_free, 1)
                        dve.wait_ge(rtot_ready, b + 1)
                        dve.wait_ge(bias_added, b + 1)
                        for m in range(2):
                            dve.wait_ge(out_full, b * NOUT + m + 1)
                            for j in range(2):
                                qc = 2 * m + j
                                t = b * TB + qc
                                last = nc.vector.scalar_tensor_tensor(x[:, t, :], outp[:, m, j * D:(j + 1) * D],
                                                                      rtotal[:, sl, qc:qc + 1], x[:, t, :], ALU.mult, ALU.add)
                            last.then_inc(out_free, 1)
                dve.wait_ge(out_free, B * NOUT + 2)
        s.clear()


def mix_correlation(nc, ctx, x, ident, mean, rstd, ctx_in, w_q, b_q, w_out, b_out, h_dram, c_dram):
    with ExitStack() as own:
        k = Kit(nc, own, "xa_")
        s = Kit(nc, own, "xa_")
        DH = 16
        TOP = int(2 * np.log(S))
        NCOL = B * DH
        LIST = S + 8
        PAD, TAKEN = -3.2e38, -3.3e38
        xn = k.sb("xn", [P, 2, TB, D])
        cx = k.sb("cx", [P, 2, TB, D])
        xT = k.sb("xT", [P, 2, DC, S])
        cT = k.sb("cT", [P, 2, DC, S])
        wq = k.sb("wq", [P, DC, DH])
        bq = k.sb("bq", [P, TB, DH])
        wo = k.sb("wo", [P, DC, D])
        bo = k.sb("bo", [1, D])
        ones = k.sb("ones", [P, P])
        q_tok = k.sb("q_tok", [P, TB, NCOL])
        k_tok = k.sb("k_tok", [P, TB, NCOL])
        qT = k.sb("qT", [P, 2 * S])
        kT = k.sb("kT", [P, S])
        h = k.sb("h", [P, 2 * S])
        h_skew = k.sb("h_skew", [P, S])
        corr = k.sb("corr", [1, LIST])
        left = k.sb("left", [1, LIST])
        left2 = k.sb("left2", [1, LIST])
        top = k.sb("top", [1, 16])
        ntop = k.sb("ntop", [1, 1])
        weight = k.sb("weight", [1, S])
        wsum = k.sb("wsum", [1, 1])
        wr = k.sb("wr", [1, 1])
        c3 = k.sb("c3", [1, 3, S])
        hankel = k.sb("hankel", [P, TB, S + 1])
        circ = k.sb("circ", [P, TB, S])
        z = k.sb("z", [P, DC, B, P])
        tp = k.ps("tp", [P, 4, S])
        proj = k.ps("proj", [P, 2, S])
        misc = k.ps("misc", [P, 2, S])
        loaded, ctx_loaded = s.sem("loaded"), [s.sem("ctx_loaded0"), s.sem("ctx_loaded1")]
        xn_ready, batch_done = s.sem("xn_ready"), s.sem("batch_done")
        tp_full, tp_free = s.sem("tp_full"), s.sem("tp_free")
        proj_full, proj_free = s.sem("proj_full"), s.sem("proj_free")
        ones_ready, dve_done = s.sem("ones_ready"), s.sem("dve_done")
        turned, turned_out, h_full, h_out = s.sem("turned"), s.sem("turned_out"), s.sem("h_full"), s.sem("h_out")
        h_stored, h_back, corr_full, ntop_ready = s.sem("h_stored"), s.sem("h_back"), s.sem("corr_full"), s.sem("ntop_ready")
        weight_ready, c_ready, c_stored, c_back = s.sem("weight_ready"), s.sem("c_ready"), s.sem("c_stored"), s.sem("c_back")
        circ_ready = s.sem("circ_ready")
        r_full, z_ready, y_full, y_free = s.sem("r_full"), s.sem("z_ready"), s.sem("y_full"), s.sem("y_free")
        ctx_tok = ctx_in.rearrange("b (j p) d -> b p j d", p=P)

        with nc.Block() as block:
            @block.sync
            def _(sp):
                sp.dma_start(wq[:], w_q.rearrange("(c p) n -> p c n", p=P)).then_inc(loaded, 16)
                sp.dma_start(bq[:, 0, :], b_q.rearrange("(a n) -> a n", a=1).to_broadcast([P, DH])).then_inc(loaded, 16)
                sp.dma_start(wo[:], w_out.rearrange("(c p) n -> p c n", p=P)).then_inc(loaded, 16)
                sp.dma_start(bo[:], b_out.rearrange("(a n) -> a n", a=1)).then_inc(loaded, 16)
                with sp.Fori(0, TURNS) as i:
                    for sl in range(2):
                        sp.wait_ge(batch_done, i * 2 + sl + 1)
                        sp.dma_start(cx[:, sl, :, :], ctx_tok[bass.ds(i * 2 + sl, 1), :, :, :].rearrange("a p j d -> p (a j) d"))\
                            .then_inc(ctx_loaded[sl], 16)
                sp.wait_ge(h_out, 2)
                sp.dma_start(h_dram[:, :], h[:]).then_inc(h_stored, 16)
                sp.wait_ge(h_stored, 16)
                skewed = h_dram.rearrange("p n -> (p n)")[0:P * (2 * S + 1) - P].rearrange("(p n) -> p n", p=P)
                skewed = bass.AP(tensor=h_dram.tensor, offset=0, ap=[[2 * S + 1, P], [1, S]])
                sp.dma_start(h_skew[:], skewed).then_inc(h_back, 16)
                sp.wait_ge(c_ready, 3)
                sp.dma_start(c_dram[:, :], c3[:].rearrange("a n m -> a (n m)")).then_inc(c_stored, 16)
                sp.wait_ge(c_stored, 16)
                for j in range(TB):
                    sp.dma_start(hankel[:, j, :], bass.AP(tensor=c_dram.tensor, offset=j * P, ap=[[1, P], [1, S + 1]]))\
                        .then_inc(c_back, 16)

            @block.gpsimd
            def _(pool):
                nc.gpsimd.memset(ones[:], 1.0).then_inc(ones_ready, 1)

            @block.tensor
            def _(pe):
                pe.sem_inc(batch_done, 2)
                pe.wait_ge(loaded, 64)
                with pe.Fori(0, TURNS) as i:
                    for sl in range(2):
                        b = i * 2 + sl
                        pe.wait_ge(xn_ready, b * TB + TB)
                        pe.wait_ge(ctx_loaded[sl], i * 16 + 16)
                        for c in range(4):
                            pe.wait_ge(tp_free, b * 4 + c + 1)
                            src = xn if c < 2 else cx
                            for j in range(TB):
                                last = nc.tensor.transpose(tp[:, c, j * P:(j + 1) * P],
                                                           src[:, sl, j, (c % 2) * P:(c % 2 + 1) * P], ident[:])
                            last.then_inc(tp_full, 1)
                    for sl in range(2):
                        b = i * 2 + sl
                        pe.wait_ge(tp_free, (b + 1) * 4 + 4)
                        for n, src in enumerate((xT, cT)):
                            pe.wait_ge(proj_free, b * 2 + n + 1)
                            for j in range(TB):
                                for c in range(DC):
                                    last = nc.tensor.matmul(proj[:, n, j * DH:(j + 1) * DH], src[:, sl, c, j * P:(j + 1) * P],
                                                            wq[:, c, :], start=(c == 0), stop=(c == DC - 1))
                            last.then_inc(proj_full, 1)
                        pe.wait_ge(proj_full, b * 2 + 2)
                        pe.sem_inc(batch_done, 1)
                pe.wait_ge(proj_free, B * 2 + 2)
                for n, src in enumerate((q_tok, k_tok)):
                    for j in range(TB):
                        last = nc.tensor.transpose(misc[:, n, j * P:(j + 1) * P], src[:, j, :], ident[:])
                    last.then_inc(turned, 1)
                pe.wait_ge(turned_out, 3)
                for j in range(TB):
                    last = nc.tensor.matmul(misc[:, 0, :], kT[:, j * P:(j + 1) * P], qT[:, j * P:j * P + S],
                                            start=(j == 0), stop=(j == TB - 1))
                last.then_inc(h_full, 1)
                pe.wait_ge(h_back, 16)
                pe.wait_ge(ones_ready, 1)
                nc.tensor.matmul(misc[0:1, 1, :], ones[:, 0:1], h_skew[:], start=True, stop=True).then_inc(corr_full, 1)
                pe.wait_ge(circ_ready, 1)
                for t in range(TB):
                    for j in range(TB):
                        last = nc.tensor.matmul(misc[:, 0, t * P:(t + 1) * P], circ[:, j, t * P:(t + 1) * P],
                                                k_tok[:, j, :], start=(j == 0), stop=(j == TB - 1))
                last.then_inc(r_full, 1)
                pe.wait_ge(z_ready, 2)
                for b in range(B):
                    if b >= 2:
                        pe.wait_ge(y_free, b - 1)
                    o = proj[:, b % 2, 0:D]
                    for c in range(DC):
                        nc.tensor.matmul(o, z[:, c, b, :], wo[:, c, :], start=(c == 0), stop=False)
                    nc.tensor.matmul(o, ones[0:1, :], bo[:], start=False, stop=True).then_inc(y_full, 1)

            @block.scalar
            def _(act):
                act.sem_inc(tp_free, 4)
                with act.Fori(0, TURNS) as i:
                    for sl in range(2):
                        b = i * 2 + sl
                        act.wait_ge(batch_done, b + 1)
                        for c in range(4):
                            act.wait_ge(tp_full, b * 4 + c + 1)
                            dst = (xT if c < 2 else cT)[:, sl, c % 2, :]
                            nc.scalar.activation(dst, tp[:, c, :], ACT.Copy).then_inc(tp_free, 1)
                act.wait_ge(ntop_ready, 1)
                nc.scalar.activation(weight[:], corr[:, 0:S], ACT.Exp, bias=ntop[:]).then_inc(weight_ready, 1)

            @block.vector
            def _(dve):
                dve.wait_ge(loaded, 64)
                dve.sem_inc(proj_free, 2)
                chain = Chain(dve, dve_done)
                for j in range(1, TB):
                    chain.tick(nc.vector.tensor_copy(bq[:, j, :], bq[:, 0, :]))
                chain.wait()
                with dve.Fori(0, TURNS) as i:
                    for sl in range(2):
                        b = i * 2 + sl
                        dve.wait_ge(batch_done, b + 1)
                        for j in range(TB):
                            t = b * TB + j
                            nc.vector.tensor_scalar(xn[:, sl, j, :], x[:, t, :], mean[:, bass.ds(t, 1)], rstd[:, bass.ds(t, 1)],
                                                    ALU.subtract, ALU.mult).then_inc(xn_ready, 1)
                    for sl in range(2):
                        b = i * 2 + sl
                        for n, dst in enumerate((q_tok, k_tok)):
                            dve.wait_ge(proj_full, b * 2 + n + 1)
                            nc.vector.tensor_tensor(dst[:, :, bass.ds(b * DH, DH)],
                                                    proj[:, n, 0:TB * DH].rearrange("p (j n) -> p j n", j=TB),
                                                    bq[:], ALU.add).then_inc(proj_free, 1)
                dve.wait_ge(turned, 1)
                nc.vector.tensor_copy(qT[:, 0:S], misc[:, 0, :]).then_inc(turned_out, 1)
                nc.vector.tensor_copy(qT[:, S:2 * S], misc[:, 0, :]).then_inc(turned_out, 1)
                dve.wait_ge(turned, 2)
                nc.vector.tensor_copy(kT[:], misc[:, 1, :]).then_inc(turned_out, 1)
                dve.wait_ge(h_full, 1)
                nc.vector.tensor_copy(h[:, 0:S], misc[:, 0, :]).then_inc(h_out, 1)
                nc.vector.tensor_copy(h[:, S:2 * S], misc[:, 0, :]).then_inc(h_out, 1)
                chain.link(nc.vector.memset(corr[:], PAD))
                dve.wait_ge(corr_full, 1)
                chain.link(nc.vector.tensor_scalar(corr[:, 0:S], misc[0:1, 1, :], 1.0 / NCOL, None, ALU.mult))
                chain.link(nc.vector.max(top[:, 0:8], corr[:, 0:S]))
                nc.vector.tensor_scalar(ntop[:], top[:, 0:1], -1.0, None, ALU.mult).then_inc(ntop_ready, 1)
                chain.link(nc.vector.match_replace(left[:], top[:, 0:8], corr[:], TAKEN))
                chain.link(nc.vector.max(top[:, 8:16], left[:, 0:S]))
                chain.link(nc.vector.memset(top[:, TOP:16], PAD))
                chain.link(nc.vector.match_replace(left2[:], top[:, 8:16], left[:], TAKEN))
                chain.link(nc.vector.tensor_scalar(left[:, 0:S], left2[:, 0:S], TAKEN, None, ALU.is_equal))
                dve.wait_ge(weight_ready, 1)
                chain.link(nc.vector.tensor_tensor(weight[:], weight[:], left[:, 0:S], ALU.mult))
                chain.link(nc.vector.tensor_reduce(wsum[:], weight[:], AX.X, ALU.add))
                chain.link(nc.vector.reciprocal(wr[:], wsum[:]))
                for n in range(3):
                    nc.vector.tensor_scalar(c3[:, n, :], weight[:], wr[:], None, ALU.mult).then_inc(c_ready, 1)
                dve.wait_ge(c_back, 16 * TB)
                nc.vector.tensor_copy(circ[:], hankel[:, :, S:0:-1]).then_inc(circ_ready, 1)
                dve.wait_ge(r_full, 1)
                rv = misc[:, 0, :].rearrange("p (h c b d) -> p c b d h", h=2, c=DC, b=B)
                for c in range(DC):
                    for rep in range(4):
                        last = nc.vector.tensor_copy(z[:, c, :, rep * 32:(rep + 1) * 32].rearrange("p b (d h) -> p b d h", h=2),
                                                     rv[:, c])
                    last.then_inc(z_ready, 1)
                for b in range(B):
                    dve.wait_ge(y_full, b + 1)
                    for j in range(TB):
                        last = nc.vector.tensor_tensor(x[:, b * TB + j, :], x[:, b * TB + j, :], proj[:, b % 2, 0:D], ALU.add)
                    last.then_inc(y_free, 1)
                dve.wait_ge(y_free, B)
        s.clear()


def mix_recurrence(nc, ctx, x, ident, mean, rstd, decay_in, w_bc):
    with ExitStack() as own:
        k = Kit(nc, own, "rc_")
        s = Kit(nc, own, "rc_")
        xn = k.sb("xn", [P, 2, TB, D])
        wbc = k.sb("wbc", [P, DC, D])
        decay = k.sb("decay", [P, DC, S])
        decay_col = k.sb("decay_col", [P, DC])
        hid = k.sb("hid", [P, 2, DC, S])
        tp = k.ps("tp", [P, 2, DC, S])
        outp = k.ps("outp", [P, 4, S])
        loaded, decay_ready = s.sem("loaded"), s.sem("decay_ready")
        xn_ready, tp_full, tp_free = s.sem("xn_ready"), s.sem("tp_full"), s.sem("tp_free")
        out_full, out_free = s.sem("out_full"), s.sem("out_free")

        with nc.Block() as block:
            @block.sync
            def _(sp):
                sp.dma_start(wbc[:], w_bc.rearrange("(c p) n -> p c n", p=P)).then_inc(loaded, 16)
                sp.dma_start(decay_col[:], decay_in.rearrange("(c p) -> p c", p=P),
                             allow_slow_non_contiguous=True).then_inc(loaded, 16)

            @block.tensor
            def _(pe):
                pe.wait_ge(loaded, 32)
                with pe.Fori(0, TURNS) as i:
                    for sl in range(2):
                        b = i * 2 + sl
                        pe.wait_ge(xn_ready, b * TB + TB)
                        pe.wait_ge(tp_free, b + 1)
                        for c in range(DC):
                            for j in range(TB):
                                last = nc.tensor.transpose(tp[:, sl, c, j * P:(j + 1) * P],
                                                           xn[:, sl, j, c * P:(c + 1) * P], ident[:])
                        last.then_inc(tp_full, 1)
                    for sl in range(2):
                        b = i * 2 + sl
                        pe.wait_ge(tp_free, b + 1 + 2)
                        pe.wait_ge(out_free, b + 1)
                        for j in range(TB):
                            for c in range(DC):
                                last = nc.tensor.matmul(outp[:, 2 * sl + j // 2, (j % 2) * D:(j % 2 + 1) * D],
                                                        hid[:, sl, c, j * P:(j + 1) * P], wbc[:, c, :],
                                                        start=(c == 0), stop=(c == DC - 1))
                        last.then_inc(out_full, 1)

            @block.vector
            def _(dve):
                dve.sem_inc(tp_free, 2)
                dve.sem_inc(out_free, 2)
                dve.wait_ge(loaded, 32)
                nc.vector.memset(decay[:], 0.0).then_inc(decay_ready, 1)
                dve.wait_ge(decay_ready, 1)
                for c in range(DC):
                    nc.vector.tensor_scalar(decay[:, c, :], decay[:, c, :], decay_col[:, c:c + 1], None, ALU.add)\
                        .then_inc(decay_ready, 1)
                dve.wait_ge(decay_ready, 3)
                with dve.Fori(0, TURNS) as i:
                    for sl in range(2):
                        b = i * 2 + sl
                        dve.wait_ge(out_free, b + 1)
                        for j in range(TB):
                            t = b * TB + j
                            nc.vector.tensor_scalar(xn[:, sl, j, :], x[:, t, :], mean[:, bass.ds(t, 1)], rstd[:, bass.ds(t, 1)],
                                                    ALU.subtract, ALU.mult).then_inc(xn_ready, 1)
                    for sl in range(2):
                        b = i * 2 + sl
                        dve.wait_ge(tp_full, b + 1)
                        for c in range(DC):
                            last = nc.vector.tensor_tensor_scan(hid[:, sl, c, :], decay[:, c, :], tp[:, sl, c, :], 0.0,
                                                                ALU.mult, ALU.add)
                        last.then_inc(tp_free, 1)
                    for sl in range(2):
                        b = i * 2 + sl
                        dve.wait_ge(out_full, b + 1)
                        for m in range(2):
                            o = x[:, bass.ds(b * TB + 2 * m, 2), :].rearrange("p j n -> p (j n)")
                            last = nc.vector.tensor_tensor(o, o, outp[:, 2 * sl + m, :], ALU.add)
                        last.then_inc(out_free, 1)
                dve.wait_ge(out_free, B + 2)
        s.clear()


class Batch:

    def __init__(self, b, slot, earlier, first=False, last=False):
        self.b, self.slot, self.earlier, self.first, self.last = b, slot, earlier, first, last


def all_batches(eng, one):
    one(Batch(0, 0, 0, first=True), Batch(1, 1, 0))
    with eng.Fori(0, TURNS - 1) as i:
        one(Batch(i * 2 + 1, 1, i), Batch(i * 2 + 2, 0, i + 1))
        one(Batch(i * 2 + 2, 0, i + 1), Batch(i * 2 + 3, 1, i + 1))
    one(Batch(B - 1, 1, TURNS - 1, last=True), None)


def mix_heads(nc, ctx, x, ident, ident_bf, mean, rstd, ctx_in, mask_in, w_vT, w_kT, w_qT, w_oT, b_o, parts_dram, mask_dram):
    with ExitStack() as own:
        k = Kit(nc, own, "hd_")
        s = Kit(nc, own, "hd_")
        H, DH = 16, 16
        GH = 4
        NG = H // GH
        Q_PARTS, K_PARTS = (0, 0, 0, 1, 1, 2), (0, 1, 2, 0, 1, 0)
        NPAIR = len(Q_PARTS)
        MASK_ROW = NPAIR * DH
        FIRST_ROWS, ROWS = MASK_ROW + 1, MASK_ROW + 4
        MASKED = -1e20
        NUNIT = GH * TB
        NRING = 8
        xn = k.sb("xn", [P, TB, D])
        cx = k.sb("cx", [P, 2, TB, D])
        xT = k.sb("xT", [P, DC, S])
        cT = k.sb("cT", [P, DC, S])
        wk = k.sb("wk", [P, P])
        wq = k.sb("wq", [P, P])
        wv = k.sb("wv", [P, P])
        wo = k.sb("wo", [P, DC, D])
        bo = k.sb("bo", [1, D])
        ones = k.sb("ones", [1, P])
        parts = k.sb("parts", [P, 2, 3, DC, S], BF16)
        rest = k.sb("rest", [P, 2, DC, S])
        k_stack = k.sb("k_stack", [ROWS, 2, H, S], BF16)
        q_stack = k.sb("q_stack", [ROWS, 2, H, S], BF16)
        mask = k.sb("mask", [B, S], I32)
        zero = k.sb("zero", [P, 1])
        mask_bf = k.sb("mask_bf", [B, S], BF16)
        v = k.sb("v", [P, 2, TB, H, 2 * DH])
        nmax = k.sb("nmax", [P, 2, GH, TB])
        nrest = k.sb("nrest", [P, GH, TB])
        nparts = k.sb("nparts", [P, 2, P // (GH * TB), GH * TB], BF16)
        nrows = k.sb("nrows", [3 * GH * TB, 2, P], BF16)
        prob = k.sb("prob", [P, NRING, S])
        oT = k.sb("oT", [P, S])
        rsum = k.sb("rsum", [P, TB, GH])
        o = k.sb("o", [P, 2, TB, D])
        oT2 = k.sb("oT2", [P, DC, S])
        first = k.ps("first", [P, 2, 2, S])
        second = k.ps("second", [P, 2, S])
        pv = k.ps("pv", [P, S])
        misc = k.ps("misc", [P, S])
        zeroed, loaded = s.sem("zeroed"), s.sem("loaded")
        ctx_loaded = [s.sem("ctx_loaded0"), s.sem("ctx_loaded1")]
        xn_ready, first_full, first_free = s.sem("xn_ready"), s.sem("first_full"), s.sem("first_free")
        part0_ready, rest_ready, part1_ready, parts_ready = s.sem("part0_ready"), s.sem("rest_ready"), s.sem("part1_ready"), s.sem("parts_ready")
        parts_stored, stack_loaded, mask_ready = s.sem("parts_stored"), s.sem("stack_loaded"), s.sem("mask_ready")
        nmax_ready, nstep, nparts_ready = s.sem("nmax_ready"), s.sem("nstep"), s.sem("nparts_ready")
        nrows_ready, nrows_loaded = s.sem("nrows_ready"), [s.sem("nrows_loaded0"), s.sem("nrows_loaded1")]
        second_full, second_free = s.sem("second_full"), s.sem("second_free")
        pv_done, pv_free, misc_full, misc_free = s.sem("pv_done"), s.sem("pv_free"), s.sem("misc_full"), s.sem("misc_free")
        rsum_ready, mask_stored = s.sem("rsum_ready"), s.sem("mask_stored")
        NLOAD = 2 * NPAIR + 1
        NPREP, NSTEP = 5, GH * TB // 2
        PER_BATCH = NG * NSTEP + NPREP
        ctx_tok = ctx_in.rearrange("b (j p) d -> b p j d", p=P)

        def use_first(bt, g):
            return NPREP + NSTEP + PER_BATCH * bt.b + g * NSTEP + (NPREP if g and not bt.last else 0)

        def pair_of(bt, g, n):
            return (NPREP + NSTEP + PER_BATCH * bt.slot + g * NSTEP + (NPREP if g and not bt.last else 0) + n) % 2

        def use_prep(bt):
            return NPREP + NSTEP + PER_BATCH * bt.b + NSTEP

        def prep_pair(bt, n):
            return (NPREP + NSTEP + PER_BATCH * bt.slot + NSTEP + n) % 2

        NFIN = 4

        def use_misc(bt, g, what):
            if bt.first:
                return 1 + (2 * g - 1 if g else 0) + (1 if g and what == "rows" else 0)
            base = 1 + 2 * NG - 1 + (2 * NG + NFIN) * (bt.b - 1)
            return base + 2 * g + (NFIN if g > 1 or (g == 1 and what == "rows") else 0) + (0 if what == "turn" else 1)

        def wait(eng, sem, n):
            if not isinstance(n, int) or n > 0:
                eng.wait_ge(sem, n)

        with nc.Block() as block:
            @block.sync
            def _(sp):
                sp.wait_ge(zeroed, 3)
                for dst, src in ((wk, w_kT), (wq, w_qT), (wv, w_vT)):
                    for a in range(P // DH):
                        sp.dma_start(dst[a * DH:(a + 1) * DH, a * DH:(a + 1) * DH], src[:, :],
                                     allow_slow_non_contiguous=True).then_inc(loaded, 16)
                sp.dma_start(mask[:], mask_in.rearrange("b x y s -> (b x y) s")).then_inc(loaded, 16)
                sp.dma_start(wo[:], w_oT.rearrange("(c p) n -> p c n", p=P)).then_inc(loaded, 16)
                sp.dma_start(bo[:], b_o.rearrange("(a n) -> a n", a=1)).then_inc(loaded, 16)

                def load_ctx(b, slot):
                    sp.dma_start(cx[:, slot, :, :], ctx_tok[bass.ds(b, 1), :, :, :].rearrange("a p j d -> p (a j) d"))\
                        .then_inc(ctx_loaded[slot], 16)

                def stacks(b, slot):
                    wait(sp, stack_loaded, b * NLOAD * 16)
                    sp.wait_ge(parts_ready, b * 2 + 2)
                    sp.dma_start(parts_dram.rearrange("a n (c p) s -> p (a n c) s", p=P),
                                 parts[:].rearrange("p a n c s -> p (a n c) s")).then_inc(parts_stored, 16)
                    sp.wait_ge(parts_stored, b * 16 + 16)
                    for a, (stack, which) in enumerate(((k_stack, K_PARTS), (q_stack, Q_PARTS))):
                        for n, part in enumerate(which):
                            sp.dma_start(stack[n * DH:(n + 1) * DH, slot, :, :],
                                         parts_dram[a, part].rearrange("(h e) s -> e h s", e=DH)).then_inc(stack_loaded, 16)
                    sp.dma_start(k_stack[MASK_ROW:MASK_ROW + 1, slot, :, :],
                                 mask_dram[bass.ds(b, 1), :].rearrange("p (a s) -> p a s", a=1).to_broadcast([1, H, S]))\
                        .then_inc(stack_loaded, 16)

                def max_rows(bt, g):
                    wait(sp, nrows_ready, bt.b * NG + g + 1)
                    sp.dma_start(q_stack[MASK_ROW + 1:ROWS, bt.slot, g * GH:(g + 1) * GH, :]
                                 .rearrange("a h (c p) -> a (h c) p", p=P),
                                 nrows[:, g % 2, :]).then_inc(nrows_loaded[g % 2], 16)

                load_ctx(0, 0)
                sp.wait_ge(zeroed, 7)
                sp.wait_ge(mask_ready, 1)
                sp.dma_start(mask_dram[:, :], mask_bf[:]).then_inc(mask_stored, 16)
                sp.wait_ge(mask_stored, 16)
                stacks(0, 0)
                max_rows(Batch(0, 0, 0), 0)

                def batch(bt, nxt):
                    if nxt is not None:
                        load_ctx(nxt.b, nxt.slot)
                    for g in range(NG):
                        if g < NG - 1:
                            max_rows(bt, g + 1)
                        if g == 0 and nxt is not None:
                            stacks(nxt.b, nxt.slot)
                        if g == NG - 1 and nxt is not None:
                            max_rows(nxt, 0)

                all_batches(sp, batch)
                for sem in nrows_loaded:
                    sp.wait_ge(sem, 16 * B * NG // 2)
                sp.wait_ge(stack_loaded, 16 * NLOAD * B)

            @block.gpsimd
            def _(pool):
                for n, (t, value) in enumerate(((wk[:], 0.0), (wq[:], 0.0), (wv[:], 0.0), (k_stack[MASK_ROW:ROWS], 1.0),
                                                (q_stack[MASK_ROW:FIRST_ROWS], 1.0), (nparts[:], 0.0), (zero[:], 0.0))):
                    if n:
                        pool.wait_ge(zeroed, n)
                    nc.gpsimd.memset(t, value).then_inc(zeroed, 1)
                pool.wait_ge(zeroed, 7)

                def split(bt):
                    for a in range(2):
                        pool.wait_ge(rest_ready, bt.b * 2 + a + 1)
                        wait(pool, parts_stored, bt.b * 16)
                        nc.gpsimd.tensor_tensor(parts[:, a, 1], rest[:, a], zero[:].unsqueeze(2).to_broadcast([P, DC, S]), ALU.add).then_inc(part1_ready, 1)
                        pool.wait_ge(part1_ready, bt.b * 2 + a + 1)
                        nc.gpsimd.tensor_tensor(parts[:, a, 2], rest[:, a], parts[:, a, 1], ALU.subtract).then_inc(parts_ready, 1)

                def split_max(bt, g):
                    m, p = nmax[:, g % 2], nparts[:, g % 2].rearrange("p n (h c) -> p n h c", h=GH)
                    at = (bt.b * NG + g) * 3
                    z = zero[:].unsqueeze(2).to_broadcast([P, GH, TB])
                    pool.wait_ge(nmax_ready, (bt.b * NG + g) * NSTEP + NSTEP)
                    nc.gpsimd.tensor_tensor(p[:, 0], m, z, ALU.add).then_inc(nstep, 1)
                    pool.wait_ge(nstep, at + 1)
                    nc.gpsimd.tensor_tensor(nrest[:], m, p[:, 0], ALU.subtract).then_inc(nstep, 1)
                    pool.wait_ge(nstep, at + 2)
                    nc.gpsimd.tensor_tensor(p[:, 1], nrest[:], z, ALU.add).then_inc(nstep, 1)
                    pool.wait_ge(nstep, at + 3)
                    nc.gpsimd.tensor_tensor(p[:, 2], nrest[:], p[:, 1], ALU.subtract).then_inc(nparts_ready, 1)

                def batch(bt, nxt):
                    for g in range(NG):
                        if g < NG - 1:
                            split_max(bt, g + 1)
                        elif nxt is not None:
                            split_max(nxt, 0)
                        if g == 0 and nxt is not None:
                            split(nxt)

                split(Batch(0, 0, 0))
                split_max(Batch(0, 0, 0), 0)
                all_batches(pool, batch)

            @block.tensor
            def _(pe):
                def prep(bt, uses, pair):
                    pe.wait_ge(ctx_loaded[bt.slot], bt.earlier * 16 + 16)
                    pe.wait_ge(xn_ready, bt.b * TB + TB)
                    for n in range(2):
                        pe.wait_ge(first_free, uses + n + 1)
                        for c in range(DC):
                            for j in range(TB):
                                cols = slice(c * P, (c + 1) * P)
                                src = xn[:, j, cols] if n else cx[:, bt.slot, j, cols]
                                last = nc.tensor.transpose(first[:, pair(n), c, j * P:(j + 1) * P], src, ident[:])
                        last.then_inc(first_full, 1)
                    for n, (w, src) in enumerate(((wk, cT), (wq, xT))):
                        pe.wait_ge(first_free, uses + n + 1 + 2)
                        for c in range(DC):
                            last = nc.tensor.matmul(first[:, pair(2 + n), c, :], w[:], src[:, c, :], start=True, stop=True)
                        last.then_inc(first_full, 1)
                    pe.wait_ge(first_free, uses + 4 + 1)
                    for j in range(TB):
                        for c in range(DC):
                            at = (j % 2) * D + c * P
                            last = nc.tensor.matmul(first[:, pair(4), j // 2, at:at + P], cT[:, c, j * P:(j + 1) * P], wv[:],
                                                    start=True, stop=True)
                    last.then_inc(first_full, 1)

                def first_energies(bt, g, n, uses, pair):
                    h = g * GH + n // 2
                    if g == 0 and n == 0:
                        pe.wait_ge(stack_loaded, (bt.b + 1) * NLOAD * 16)
                    pe.wait_ge(first_free, uses + n + 1)
                    for j in range(2):
                        qc = (n % 2) * 2 + j
                        last = nc.tensor.matmul(first[:, pair, j, :], q_stack[0:FIRST_ROWS, bt.slot, h, qc * P:(qc + 1) * P],
                                                k_stack[0:FIRST_ROWS, bt.slot, h, :], start=True, stop=True)
                    last.then_inc(first_full, 1)

                def second_energies(bt, g, u):
                    kc, h = u // GH, g * GH + u % GH
                    if u == 0:
                        pe.wait_ge(nrows_loaded[g % 2], (bt.b * (NG // 2) + g // 2 + 1) * 16)
                    pe.wait_ge(second_free, (bt.b * NG + g) * NUNIT + u + 1)
                    nc.tensor.matmul(second[:, u % 2, :], k_stack[:, bt.slot, h, kc * P:(kc + 1) * P], q_stack[:, bt.slot, h, :],
                                     start=True, stop=True).then_inc(second_full, 1)

                def values(bt, g, kc):
                    at = bt.b * NG + g
                    pe.wait_ge(second_free, at * NUNIT + (kc + 1) * GH + 2)
                    if kc == 0:
                        pe.wait_ge(pv_free, at + 1)
                    for j in range(GH):
                        last = nc.tensor.matmul(pv[32 * j:32 * j + 32, :], v[:, bt.slot, kc, g * GH + j, :],
                                                prob[:, (kc * GH + j) % NRING, :], start=(kc == 0), stop=(kc == TB - 1),
                                                skip_group_check=True)
                    last.then_inc(pv_done, 1)

                def rows(bt, g, uses):
                    pe.wait_ge(nparts_ready, bt.b * NG + g + 1)
                    pe.wait_ge(misc_free, uses + 1)
                    nc.tensor.transpose(misc[:, 0:P // 2].bitcast(BF16), nparts[:, g % 2].rearrange("p n m -> p (n m)"),
                                        ident_bf[:]).then_inc(misc_full, 1)

                def turn(groups, uses):
                    pe.wait_ge(pv_free, groups + 1)
                    pe.wait_ge(misc_free, uses + 1)
                    for qc in range(TB):
                        last = nc.tensor.transpose(misc[:, qc * P:(qc + 1) * P], oT[:, qc * P:(qc + 1) * P], ident[:])
                    last.then_inc(misc_full, 1)

                def finish(slot, n, uses):
                    pe.wait_ge(misc_free, uses + n + 1)
                    if n < 2:
                        for qc in range(TB):
                            last = nc.tensor.transpose(misc[:, qc * P:(qc + 1) * P], o[:, slot, qc, n * P:(n + 1) * P], ident[:])
                    else:
                        for j in range(2):
                            qc, out = 2 * (n - 2) + j, misc[:, j * D:(j + 1) * D]
                            for c in range(DC):
                                nc.tensor.matmul(out, oT2[:, c, qc * P:(qc + 1) * P], wo[:, c, :], start=(c == 0), stop=False)
                            last = nc.tensor.matmul(out, ones[:], bo[:], start=False, stop=True)
                    last.then_inc(misc_full, 1)

                def group(bt, g, nbt, ng):
                    for n in range(NSTEP):
                        if nbt is not None:
                            first_energies(nbt, ng, n, use_first(bt, g), pair_of(bt, g, n))
                        second_energies(bt, g, 2 * n)
                        second_energies(bt, g, 2 * n + 1)
                        if n == 2 and not (bt.first and g == 0):
                            turn(bt.b * NG + g, use_misc(bt, g, "turn"))
                        if g == 1 and 3 <= n < 7 and not bt.first:
                            finish(1 - bt.slot, n - 3, use_misc(bt, g, "fin"))
                        if n >= 3 and n % 2 == 1:
                            values(bt, g, (n - 3) // 2)
                    values(bt, g, TB - 1)
                    if nbt is not None:
                        rows(nbt, ng, use_misc(bt, g, "rows"))

                def batch(bt, nxt):
                    for g in range(NG):
                        nbt, ng = (bt, g + 1) if g < NG - 1 else (nxt, 0)
                        group(bt, g, nbt, ng)
                        if g == 0 and nxt is not None:
                            prep(nxt, use_prep(bt), lambda n: prep_pair(bt, n))

                pe.wait_ge(loaded, (3 * (P // DH) + 3) * 16)
                b0 = Batch(0, 0, 0)
                prep(b0, 0, lambda n: n % 2)
                for n in range(NSTEP):
                    first_energies(b0, 0, n, NPREP, (NPREP + n) % 2)
                rows(b0, 0, 0)
                all_batches(pe, batch)
                turn(B * NG, 1 + 2 * NG - 1 + (2 * NG + NFIN) * (B - 1) - 1)
                for n in range(NFIN):
                    finish(1, n, 1 + 2 * NG - 1 + (2 * NG + NFIN) * (B - 1))

            @block.scalar
            def _(act):
                act.sem_inc(second_free, 2)
                act.sem_inc(pv_free, 1)

                def copy_out(groups):
                    act.wait_ge(pv_done, groups * TB + 2)
                    nc.scalar.activation(oT[:], pv[:], ACT.Copy).then_inc(pv_free, 1)

                def batch(bt, nxt):
                    for g in range(NG):
                        at = bt.b * NG + g
                        for u in range(NUNIT):
                            if u % GH == 0:
                                act.wait_ge(pv_done, at * TB + u // GH + 1)
                            act.wait_ge(second_full, at * NUNIT + u + 1)
                            nc.scalar.activation(prob[:, u % NRING, :], second[:, u % 2, :], ACT.Exp, scale=D ** -0.5)\
                                .then_inc(second_free, 1)
                            if u == 1 and not (bt.first and g == 0):
                                copy_out(at)

                all_batches(act, batch)
                copy_out(B * NG)

            @block.vector
            def _(dve):
                dve.sem_inc(first_free, 2)
                dve.sem_inc(misc_free, 1)
                dve.sem_inc(pv_done, 2)
                nc.vector.memset(ones[:], 1.0)
                nc.vector.memset(v[:], 0.0).then_inc(rsum_ready, 1)
                dve.wait_ge(rsum_ready, 1)
                nc.vector.memset(v[:, :, :, :, DH:DH + 1].rearrange("p a j h n -> p (a j h) n"), 1.0)
                dve.wait_ge(loaded, (3 * (P // DH) + 3) * 16)
                nc.vector.tensor_scalar(mask_bf[:], mask[:], 0.0, MASKED, ALU.is_equal, ALU.mult).then_inc(mask_ready, 1)

                def normed(bt):
                    for j in range(TB):
                        t = bt.b * TB + j
                        nc.vector.tensor_scalar(xn[:, j, :], x[:, t, :], mean[:, bass.ds(t, 1)], rstd[:, bass.ds(t, 1)],
                                                ALU.subtract, ALU.mult).then_inc(xn_ready, 1)

                def prep(bt, uses, pair):
                    for n, dst in enumerate((cT, xT)):
                        dve.wait_ge(first_full, uses + n + 1)
                        nc.vector.tensor_copy(dst[:], first[:, pair(n)]).then_inc(first_free, 1)
                    for a in range(2):
                        dve.wait_ge(first_full, uses + 2 + a + 1)
                        wait(dve, parts_stored, bt.b * 16)
                        nc.vector.tensor_copy(parts[:, a, 0], first[:, pair(2 + a)]).then_inc(part0_ready, 1)
                        dve.wait_ge(part0_ready, bt.b * 2 + a + 1)
                        nc.vector.tensor_tensor(rest[:, a], first[:, pair(2 + a)], parts[:, a, 0], ALU.subtract)\
                            .then_inc(rest_ready, 1)
                        dve.wait_ge(rest_ready, bt.b * 2 + a + 1)
                        dve.sem_inc(first_free, 1)
                    dve.wait_ge(first_full, uses + 4 + 1)
                    nc.vector.tensor_copy(v[:, bt.slot, :, :, 0:DH].rearrange("p j h e -> p (j h) e"),
                                          first[:, pair(4)].rearrange("p a (m e) -> p (a m) e", e=DH)).then_inc(first_free, 1)

                def maxima(bt, g, n, uses, pair):
                    dve.wait_ge(first_full, uses + n + 1)
                    c = (n % 2) * 2
                    nc.vector.tensor_reduce(nmax[:, g % 2, n // 2, c:c + 2], first[:, pair], AX.X, ALU.max, negate=True)\
                        .then_inc(nmax_ready, 1)
                    dve.wait_ge(nmax_ready, (bt.b * NG + g) * NSTEP + n + 1)
                    dve.sem_inc(first_free, 1)

                def rows(bt, g, uses):
                    dve.wait_ge(misc_full, uses + 1)
                    wait(dve, nrows_loaded[g % 2], (bt.b * (NG // 2) + g // 2) * 16)
                    nc.vector.tensor_copy(nrows[:, g % 2, :], misc[0:3 * GH * TB, 0:P // 2].bitcast(BF16))\
                        .then_inc(nrows_ready, 1)
                    dve.wait_ge(nrows_ready, bt.b * NG + g + 1)
                    dve.sem_inc(misc_free, 1)

                def turn(groups, slot, g, uses):
                    m = misc[:].rearrange("p (c h n) -> p c h n", c=TB, n=2 * DH)
                    dve.wait_ge(misc_full, uses + 1)
                    nc.vector.reciprocal(rsum[:], m[:, :, :, DH]).then_inc(rsum_ready, 1)
                    dve.wait_ge(rsum_ready, groups + 1)
                    nc.vector.tensor_tensor(o[:, slot, :, g * GH * DH:(g + 1) * GH * DH].rearrange("p c (h e) -> p c h e", e=DH),
                                            m[:, :, :, 0:DH], rsum[:].unsqueeze(3).to_broadcast([P, TB, GH, DH]), ALU.mult)\
                        .then_inc(misc_free, 1)

                def finish(b, n, uses):
                    dve.wait_ge(misc_full, uses + n + 1)
                    if n < 2:
                        nc.vector.tensor_copy(oT2[:, n, :], misc[:]).then_inc(misc_free, 1)
                    else:
                        xs = x[:, bass.ds(b * TB + 2 * (n - 2), 2), :].rearrange("p j n -> p (j n)")
                        nc.vector.tensor_tensor(xs, xs, misc[:], ALU.add).then_inc(misc_free, 1)

                def batch(bt, nxt):
                    for g in range(NG):
                        nbt, ng = (bt, g + 1) if g < NG - 1 else (nxt, 0)
                        if g == 0 and nxt is not None:
                            normed(nxt)
                        for n in range(NSTEP):
                            if nbt is not None:
                                maxima(nbt, ng, n, use_first(bt, g), pair_of(bt, g, n))
                            if n == 2 and not (bt.first and g == 0):
                                turn(bt.b * NG + g, bt.slot if g else 1 - bt.slot, (g - 1) % NG, use_misc(bt, g, "turn"))
                            if g == 1 and 3 <= n < 7 and not bt.first:
                                finish(bt.b - 1, n - 3, use_misc(bt, g, "fin"))
                        if nbt is not None:
                            rows(nbt, ng, use_misc(bt, g, "rows"))
                        if g == 0 and nxt is not None:
                            prep(nxt, use_prep(bt), lambda n: prep_pair(bt, n))

                b0 = Batch(0, 0, 0)
                normed(b0)
                prep(b0, 0, lambda n: n % 2)
                for n in range(NSTEP):
                    maxima(b0, 0, n, NPREP, (NPREP + n) % 2)
                rows(b0, 0, 0)
                all_batches(dve, batch)
                turn(B * NG, 1, NG - 1, 1 + 2 * NG - 1 + (2 * NG + NFIN) * (B - 1) - 1)
                for n in range(NFIN):
                    finish(B - 1, n, 1 + 2 * NG - 1 + (2 * NG + NFIN) * (B - 1))
                dve.wait_ge(misc_free, 1 + 2 * NG + (2 * NG + NFIN) * (B - 1) + NFIN)
        s.clear()


def normed_and_logits(nc, ctx, name, x, ident, mean, rstd, w_gate, n_exp, xnT, logits, rows=None):
    with ExitStack() as own:
        k = Kit(nc, own, name + "_nl_")
        s = Kit(nc, own, name + "_nl_")
        xn = k.sb("xn", [P, 2, TB, D])
        wg = k.sb("wg", [P, DC, n_exp])
        lgT = k.sb("lgT", [P, 2, S])
        tp = k.ps("tp", [P, 2, DC, S])
        lp = k.ps("lp", [n_exp, 2, S])
        lt = k.ps("lt", [P, 2, S])
        loaded, xn_ready, xn_free = s.sem("loaded"), s.sem("xn_ready"), s.sem("xn_free")
        tp_full, tp_free, lp_full, lp_free = s.sem("tp_full"), s.sem("tp_free"), s.sem("lp_full"), s.sem("lp_free")
        lt_full, lt_free, stored = s.sem("lt_full"), s.sem("lt_free"), [s.sem("stored0"), s.sem("stored1")]

        with nc.Block() as block:
            @block.sync
            def _(sp):
                sp.dma_start(wg[:], w_gate.rearrange("(c p) n -> p c n", p=P)).then_inc(loaded, 16)
                if rows is not None:
                    for sem in stored:
                        sp.sem_inc(sem, 16)
                    with sp.Fori(0, TURNS) as i:
                        for sl in range(2):
                            b = i * 2 + sl
                            sp.wait_ge(xn_ready, b * TB + TB)
                            sp.dma_start(rows[bass.ds(b * S, S), 0:D].rearrange("(j p) d -> p j d", p=P), xn[:, sl])\
                                .then_inc(stored[sl], 16)
                    for sem in stored:
                        sp.wait_ge(sem, 16 * TURNS + 16)

            @block.tensor
            def _(pe):
                pe.sem_inc(xn_free, 2)
                pe.wait_ge(loaded, 16)
                with pe.Fori(0, TURNS) as i:
                    for sl in range(2):
                        b = i * 2 + sl
                        pe.wait_ge(xn_ready, b * TB + TB)
                        pe.wait_ge(tp_free, b + 1)
                        for c in range(DC):
                            for j in range(TB):
                                last = nc.tensor.transpose(tp[:, sl, c, j * P:(j + 1) * P],
                                                           xn[:, sl, j, c * P:(c + 1) * P], ident[:])
                        last.then_inc(tp_full, 1)
                        pe.wait_ge(tp_full, b + 1)
                        pe.sem_inc(xn_free, 1)
                    for sl in range(2):
                        b = i * 2 + sl
                        pe.wait_ge(tp_free, b + 1 + 2)
                        pe.wait_ge(lp_free, b + 1)
                        for c in range(DC):
                            last = nc.tensor.matmul(lp[:, sl, :], wg[:, c, :], xnT[:, c, bass.ds(b * S, S)],
                                                    start=(c == 0), stop=(c == DC - 1))
                        last.then_inc(lp_full, 1)
                    for sl in range(2):
                        b = i * 2 + sl
                        pe.wait_ge(lp_free, b + 1 + 2)
                        pe.wait_ge(lt_free, b + 1)
                        for j in range(TB):
                            last = nc.tensor.transpose(lt[:, sl, j * P:(j + 1) * P], lgT[:, sl, j * P:(j + 1) * P], ident[:])
                        last.then_inc(lt_full, 1)

            @block.scalar
            def _(act):
                act.sem_inc(tp_free, 2)
                with act.Fori(0, TURNS) as i:
                    for sl in range(2):
                        b = i * 2 + sl
                        act.wait_ge(tp_full, b + 1)
                        nc.scalar.activation(xnT[:, :, bass.ds(b * S, S)], tp[:, sl], ACT.Copy).then_inc(tp_free, 1)

            @block.vector
            def _(dve):
                nc.vector.memset(lgT[:], 0.0).then_inc(lp_free, 2)
                dve.wait_ge(lp_free, 2)
                dve.sem_inc(lt_free, 2)
                with dve.Fori(0, TURNS) as i:
                    for sl in range(2):
                        b = i * 2 + sl
                        dve.wait_ge(xn_free, b + 1)
                        if rows is not None:
                            dve.wait_ge(stored[sl], i * 16 + 16)
                        for j in range(TB):
                            t = b * TB + j
                            nc.vector.tensor_scalar(xn[:, sl, j, :], x[:, t, :], mean[:, bass.ds(t, 1)], rstd[:, bass.ds(t, 1)],
                                                    ALU.subtract, ALU.mult).then_inc(xn_ready, 1)
                    for sl in range(2):
                        b = i * 2 + sl
                        dve.wait_ge(lp_full, b + 1)
                        nc.vector.tensor_copy(lgT[0:n_exp, sl, :], lp[:, sl, :]).then_inc(lp_free, 1)
                    for sl in range(2):
                        b = i * 2 + sl
                        dve.wait_ge(lt_full, b + 1)
                        nc.vector.tensor_copy(logits[:, bass.ds(b * TB, TB), :],
                                              lt[:, sl, :].rearrange("p (j n) -> p j n", j=TB)[:, :, 0:n_exp]).then_inc(lt_free, 1)
                dve.wait_ge(lt_free, B + 2)
                dve.wait_ge(tp_free, B + 2)
        s.clear()


def softmax_scores(nc, dve, chain, logits, nmax, total, exp_ready, exp_go):
    n = logits.shape[2]
    chain.link(nc.vector.tensor_reduce(nmax[:], logits[:], AX.X, ALU.max))
    nc.vector.tensor_tensor(logits[:], logits[:], nmax[:].unsqueeze(2).to_broadcast([P, NT, n]), ALU.subtract).then_inc(exp_go, 1)
    dve.wait_ge(exp_ready, 1)
    chain.link(nc.vector.tensor_reduce(total[:], logits[:], AX.X, ALU.add))
    chain.link(nc.vector.reciprocal(total[:], total[:]))
    chain.link(nc.vector.tensor_tensor(logits[:], logits[:], total[:].unsqueeze(2).to_broadcast([P, NT, n]), ALU.mult))


def mix_experts_dense(nc, ctx, x, ident, mean, rstd, w_gate, w_in, w_out, n_shared):
    with ExitStack() as own:
        k = Kit(nc, own, "mo_")
        s = Kit(nc, own, "mo_")
        E, TOP, CAP = 32, 4, 2048
        NE = w_in.shape[0]
        F = 128
        xnT = k.sb("xnT", [P, DC, B * S])
        gates = k.sb("gates", [P, NT, NE])
        with ExitStack() as own2:
            k2 = Kit(nc, own2, "mo_r_")
            PAD, TAKEN = -2.0, -1.0
            logits = k2.sb("logits", [P, NT, E])
            normed_and_logits(nc, ctx, "mo", x, ident, mean, rstd, w_gate, E, xnT, logits)
            nmax = k2.sb("nmax", [P, NT])
            total = k2.sb("total", [P, NT])
            padded = k2.sb("padded", [P, NT, E + 8])
            left = k2.sb("left", [P, NT, E + 8])
            top = k2.sb("top", [P, NT, 8])
            before = k2.sb("before", [P, NT, E])
            tri = k2.sb("tri", [P, P])
            ones = k2.sb("ones", [P, P])
            rank = k2.ps("rank", [P, 2, 512])
            exp_go, exp_ready, chained = s.sem("exp_go"), s.sem("exp_ready"), s.sem("chained")
            top_done, tri_ready, sel_ready, rank_full = s.sem("top_done"), s.sem("tri_ready"), s.sem("sel_ready"), s.sem("rank_full")
            with nc.Block() as block:
                @block.gpsimd
                def _(pool):
                    nc.gpsimd.memset(ones[:], 1.0).then_inc(tri_ready, 1)
                    pool.wait_ge(tri_ready, 1)
                    nc.gpsimd.affine_select(out=tri[:], in_=ones[:], compare_op=ALU.is_ge, fill=0.0, base=0,
                                            pattern=[[1, P]], channel_multiplier=-1).then_inc(tri_ready, 1)

                @block.scalar
                def _(act):
                    act.wait_ge(exp_go, 1)
                    nc.scalar.activation(logits[:], logits[:], ACT.Exp).then_inc(exp_ready, 1)

                @block.tensor
                def _(pe):
                    pe.wait_ge(tri_ready, 2)
                    pe.wait_ge(sel_ready, 2)
                    for t in range(NT):
                        o = rank[:, t // 16, (t % 16) * E:(t % 16 + 1) * E]
                        nc.tensor.matmul(o, ones[:], before[:, t, :], start=True, stop=False)
                        last = nc.tensor.matmul(o, tri[:], gates[:, t, 0:E], start=False, stop=True)
                    last.then_inc(rank_full, 1)

                @block.vector
                def _(dve):
                    chain = Chain(dve, chained)
                    chain.link(nc.vector.memset(padded[:], PAD))
                    chain.link(nc.vector.memset(gates[:], 1.0))
                    softmax_scores(nc, dve, chain, logits, nmax, total, exp_ready, exp_go)
                    chain.link(nc.vector.tensor_copy(padded[:, :, 0:E], logits[:]))
                    for t in range(NT):
                        nc.vector.max(top[:, t, :], logits[:, t, :]).then_inc(top_done, 1)
                    dve.wait_ge(top_done, NT)
                    chain.link(nc.vector.memset(top[:, :, TOP:8], PAD))
                    for t in range(NT):
                        nc.vector.match_replace(left[:, t, :], top[:, t, :], padded[:, t, :], TAKEN).then_inc(top_done, 1)
                    dve.wait_ge(top_done, 2 * NT)
                    chain.link(nc.vector.tensor_scalar(gates[:, :, 0:E], left[:, :, 0:E], TAKEN, None, ALU.is_equal))
                    chain.link(nc.vector.memset(before[:, 0, :], 0.0))
                    for t in range(1, NT):
                        chain.link(nc.vector.tensor_tensor(before[:, t, :], before[:, t - 1, :], gates[:, t - 1, 0:E], ALU.add))
                    dve.sem_inc(sel_ready, 2)
                    dve.wait_ge(rank_full, 1)
                    r = rank[:].rearrange("p a (t e) -> p (a t) e", e=E)
                    chain.link(nc.vector.tensor_scalar(before[:], r, float(CAP), None, ALU.is_le))
                    chain.link(nc.vector.tensor_tensor(gates[:, :, 0:E], gates[:, :, 0:E], before[:], ALU.mult))
                    chain.link(nc.vector.tensor_tensor(gates[:, :, 0:E], gates[:, :, 0:E], logits[:], ALU.mult))

        w = k.sb("w", [P, 2, DC, 2 * F])
        w2 = k.sb("w2", [P, 2, D])
        act_out = k.sb("act_out", [P, 2, S])
        hid = k.sb("hid", [P, 2, S])
        hp = k.ps("hp", [P, 2, 2, S])
        yp = k.ps("yp", [P, 2, 2, S])
        w_loaded, w_free = [s.sem("w_loaded0"), s.sem("w_loaded1")], s.sem("w_free")
        h_full, silu_done, h_free = s.sem("h_full"), s.sem("silu_done"), s.sem("h_free")
        y_full, y_free = s.sem("y_full"), s.sem("y_free")
        NG = B * S // S
        with nc.Block() as block:
            @block.sync
            def _(sp):
                with sp.Fori(0, NE // 2) as i:
                    for sl in range(2):
                        sp.wait_ge(w_free, i * 2 + sl + 1)
                        sp.dma_start(w[:, sl].rearrange("p c n -> p (c n)"), w_in[bass.ds(i * 2 + sl, 1)].rearrange("a p n -> p (a n)"))\
                            .then_inc(w_loaded[sl], 16)
                        sp.dma_start(w2[:, sl], w_out[bass.ds(i * 2 + sl, 1)].rearrange("a p n -> p (a n)"))\
                            .then_inc(w_loaded[sl], 16)

            @block.tensor
            def _(pe):
                def y(pe, sl, at, g):
                    pe.wait_ge(h_free, at + 2)
                    pe.wait_ge(y_free, at)
                    for j in range(TB):
                        last = nc.tensor.matmul(yp[:, g % 2, j // 2, (j % 2) * D:(j % 2 + 1) * D], hid[:, g % 2, j * P:(j + 1) * P],
                                                w2[:, sl, :], start=True, stop=True)
                    last.then_inc(y_full, 1)

                pe.sem_inc(w_free, 2)
                with pe.Fori(0, NE // 2) as i:
                    for sl in range(2):
                        pe.wait_ge(w_loaded[sl], i * 32 + 32)
                        for g in range(NG):
                            at = (i * 2 + sl) * NG + g
                            for half in range(2):
                                pe.wait_ge(h_free, at + 1)
                                for c in range(DC):
                                    last = nc.tensor.matmul(hp[:, g % 2, half, :], w[:, sl, c, half * F:(half + 1) * F],
                                                            xnT[:, c, g * S:(g + 1) * S], start=(c == 0), stop=(c == DC - 1))
                            last.then_inc(h_full, 1)
                            if g:
                                y(pe, sl, at, g - 1)
                        y(pe, sl, (i * 2 + sl) * NG + NG, NG - 1)
                        pe.wait_ge(y_full, (i * 2 + sl) * NG + NG)
                        pe.sem_inc(w_free, 1)

            @block.scalar
            def _(act):
                with act.Fori(0, NE // 2) as i:
                    for sl in range(2):
                        for g in range(NG):
                            at = (i * 2 + sl) * NG + g
                            act.wait_ge(h_full, at + 1)
                            act.wait_ge(h_free, at + 1)
                            nc.scalar.activation(act_out[:, g % 2, :], hp[:, g % 2, 0, :], ACT.Silu).then_inc(silu_done, 1)

            @block.vector
            def _(dve):
                dve.sem_inc(h_free, 2)
                dve.sem_inc(y_free, 2)

                def add(e, at, g):
                    dve.wait_ge(y_full, at)
                    for j in range(TB):
                        t = g * TB + j
                        last = nc.vector.scalar_tensor_tensor(x[:, t, :], yp[:, g % 2, j // 2, (j % 2) * D:(j % 2 + 1) * D],
                                                              gates[:, t, bass.ds(e, 1)], x[:, t, :], ALU.mult, ALU.add)
                    last.then_inc(y_free, 1)

                with dve.Fori(0, NE // 2) as i:
                    for sl in range(2):
                        for g in range(NG):
                            at = (i * 2 + sl) * NG + g
                            dve.wait_ge(silu_done, at + 1)
                            nc.vector.tensor_tensor(hid[:, g % 2, :], act_out[:, g % 2, :], hp[:, g % 2, 1, :], ALU.mult)\
                                .then_inc(h_free, 1)
                            if g:
                                add(i * 2 + sl, at, g - 1)
                        add(i * 2 + sl, (i * 2 + sl) * NG + NG, NG - 1)
                dve.wait_ge(y_free, NE * NG + 2)
        s.clear()


def experts_in_turn(eng, n, one):
    one(0, 0, 0, True)
    with eng.Fori(0, n // 2 - 1) as i:
        one(i * 2 + 1, 1, i, False)
        one(i * 2 + 2, 0, i + 1, False)
    one(n - 1, 1, n // 2 - 1, False)


def mix_experts_sparse(nc, ctx, x, ident, mean, rstd, w_gate, w_exp, sw_in, sw_out, rows, y_dram, out):
    with ExitStack() as own:
        k = Kit(nc, own, "me_")
        s = Kit(nc, own, "me_")
        E, TOP, CAP, F = 64, 8, 160, 768
        T = B * S
        FC = F // P
        HALF = NT // 2
        TH = T // 2
        TAIL = CAP - P
        ROUNDS = CAP // 8
        passed = s.sem("passed")
        lists = k.sb("lists", [P, CAP])
        index_a = k.sb("index_a", [P, E], I32)
        index_b = k.sb("index_b", [TAIL, E], I32)
        with ExitStack() as own2:
            k2 = Kit(nc, own2, "me_r_")
            xnT = k2.sb("xnT", [P, DC, T])
            key = k2.sb("key", [P, TH])
            with ExitStack() as own3:
                k3 = Kit(nc, own3, "me_g_")
                gates = k3.sb("gates", [P, NT, E])
                normed_and_logits(nc, ctx, "me", x, ident, mean, rstd, w_gate, E, xnT, gates, rows)
                left = k3.sb("left", [P, NT, E])
                sel = k3.sb("sel", [P, HALF, 2, E])
                top = k3.sb("top", [P, NT, 8])
                nmax = k3.sb("nmax", [P, NT])
                total = k3.sb("total", [P, NT])
                ones = k3.sb("ones", [P, TH])
                selT = k3.sb("selT", [P, TH])
                count = k3.sb("count", [P, TH])
                before = k3.sb("before", [P, 1])
                order = k3.sb("order", [P, TH])
                zero = k3.sb("zero", [P, D + E])
                sp4 = k3.ps("sp4", [P, TH])
                exp_go, exp_ready, chained, top_done = s.sem("exp_go"), s.sem("exp_ready"), s.sem("chained"), s.sem("top_done")
                sel_ready, selT_full, counted, moved = s.sem("sel_ready"), s.sem("selT_full"), s.sem("counted"), s.sem("moved")
                gates_ready, stored, order_ready, zero_ready = s.sem("gates_ready"), s.sem("stored"), s.sem("order_ready"), s.sem("zero_ready")
                with nc.Block() as block:
                    @block.gpsimd
                    def _(pool):
                        nc.gpsimd.iota(order[:], pattern=[[-1, TH]], base=TH, channel_multiplier=0,
                                       allow_small_or_imprecise_dtypes=True).then_inc(order_ready, 1)

                    @block.sync
                    def _(sp):
                        sp.wait_ge(zero_ready, 1)
                        sp.dma_start(rows[T:T + P, :], zero[:]).then_inc(stored, 16)
                        sp.dma_start(rows[T + P:T + CAP, :], zero[0:TAIL, :]).then_inc(stored, 16)
                        sp.dma_start(y_dram[T:T + P, :], zero[:, 0:D]).then_inc(stored, 16)
                        sp.dma_start(y_dram[T + P:T + CAP, :], zero[0:TAIL, 0:D]).then_inc(stored, 16)
                        sp.wait_ge(counted, 1)
                        sp.dma_start(before[P // 2:P, :], count[0:P // 2, TH - 1:TH]).then_inc(moved, 16)
                        sp.wait_ge(gates_ready, 1)
                        sp.dma_start(rows[0:T, D:D + E].rearrange("(j p) e -> p j e", p=P), gates[:]).then_inc(stored, 16)
                        sp.wait_ge(stored, 80)
                        sp.wait_ge(moved, 16)

                    @block.scalar
                    def _(act):
                        act.wait_ge(exp_go, 1)
                        nc.scalar.activation(gates[:], gates[:], ACT.Exp).then_inc(exp_ready, 1)

                    @block.tensor
                    def _(pe):
                        pe.wait_ge(sel_ready, 1)
                        for j in range(HALF):
                            last = nc.tensor.transpose(sp4[:, j * P:(j + 1) * P], sel[:, j].rearrange("p a e -> p (a e)"), ident[:])
                        last.then_inc(selT_full, 1)

                    @block.vector
                    def _(dve):
                        chain = Chain(dve, chained)
                        nc.vector.memset(zero[:], 0.0).then_inc(zero_ready, 1)
                        chain.link(nc.vector.memset(before[:], 0.0))
                        chain.link(nc.vector.memset(ones[:], 1.0))
                        softmax_scores(nc, dve, chain, gates, nmax, total, exp_ready, exp_go)
                        for t in range(NT):
                            nc.vector.max(top[:, t, :], gates[:, t, :]).then_inc(top_done, 1)
                        dve.wait_ge(top_done, NT)
                        for t in range(NT):
                            nc.vector.match_replace(left[:, t, :], top[:, t, :], gates[:, t, :], -1.0).then_inc(top_done, 1)
                        dve.wait_ge(top_done, 2 * NT)
                        chain.link(nc.vector.tensor_scalar(left[:], left[:], -1.0, None, ALU.is_equal))
                        for a in range(2):
                            last = nc.vector.tensor_copy(sel[:, :, a, :], left[:, a * HALF:(a + 1) * HALF, :])
                            chain.tick(last)
                        chain.wait()
                        dve.sem_inc(sel_ready, 1)
                        chain.link(nc.vector.tensor_reduce(total[:], top[:], AX.X, ALU.add))
                        chain.link(nc.vector.tensor_scalar(total[:], total[:], float(np.finfo(np.float32).eps), None, ALU.max))
                        chain.link(nc.vector.reciprocal(total[:], total[:]))
                        chain.link(nc.vector.tensor_tensor(gates[:], gates[:], left[:], ALU.mult))
                        nc.vector.tensor_tensor(gates[:], gates[:], total[:].unsqueeze(2).to_broadcast([P, NT, E]), ALU.mult)\
                            .then_inc(gates_ready, 1)
                        dve.wait_ge(selT_full, 1)
                        chain.link(nc.vector.tensor_copy(selT[:], sp4[:]))
                        nc.vector.tensor_tensor_scan(count[:], ones[:], selT[:], 0.0, ALU.mult, ALU.add).then_inc(counted, 1)
                        dve.wait_ge(moved, 16)
                        chain.link(nc.vector.tensor_scalar(count[:], count[:], before[:], float(CAP), ALU.add, ALU.is_le))
                        chain.link(nc.vector.tensor_tensor(selT[:], selT[:], count[:], ALU.mult))
                        dve.wait_ge(order_ready, 1)
                        chain.link(nc.vector.tensor_tensor(key[:], selT[:], order[:], ALU.mult))

            sw1 = k2.sb("sw1", [P, DC, 2 * F])
            sw2 = k2.sb("sw2", [P, FC, D])
            act_out = k2.sb("act_out", [P, 2, S])
            hid = k2.sb("hid", [P, FC, S])
            best = k2.sb("best", [P, ROUNDS // TURNS, 8])
            hp = k2.ps("hp", [P, 2, 2, S])
            yp = k2.ps("yp", [P, 4, S])
            loaded, h_full, silu_done, h_free = s.sem("sh_loaded"), s.sem("sh_h_full"), s.sem("sh_silu_done"), s.sem("sh_h_free")
            y_full, y_free, listed, y_stored, x_ready = s.sem("sh_y_full"), s.sem("sh_y_free"), s.sem("listed"), s.sem("y_stored"), s.sem("x_ready")
            lists_ready = s.sem("lists_ready")
            with nc.Block() as block:
                @block.sync
                def _(sp):
                    sp.dma_start(sw1[:], sw_in.rearrange("(c p) n -> p c n", p=P)).then_inc(loaded, 16)
                    sp.dma_start(sw2[:], sw_out.rearrange("(c p) n -> p c n", p=P)).then_inc(loaded, 16)
                    sp.wait_ge(x_ready, B)
                    sp.dma_start(y_dram[0:T, :].rearrange("(j p) d -> p j d", p=P), x[:]).then_inc(y_stored, 16)
                    sp.wait_ge(y_stored, 16)

                @block.tensor
                def _(pe):
                    pe.wait_ge(loaded, 32)
                    with pe.Fori(0, TURNS) as i:
                        for sl in range(2):
                            b = i * 2 + sl
                            for f in range(FC):
                                pe.wait_ge(h_free, b * FC + f + 1)
                                for half in range(2):
                                    for c in range(DC):
                                        at = half * F + f * P
                                        last = nc.tensor.matmul(hp[:, f % 2, half, :], sw1[:, c, at:at + P],
                                                                xnT[:, c, bass.ds(b * S, S)], start=(c == 0), stop=(c == DC - 1))
                                last.then_inc(h_full, 1)
                            pe.wait_ge(h_free, b * FC + FC + 2)
                            pe.wait_ge(y_free, b + 1)
                            for j in range(TB):
                                for f in range(FC):
                                    last = nc.tensor.matmul(yp[:, 2 * sl + j // 2, (j % 2) * D:(j % 2 + 1) * D],
                                                            hid[:, f, j * P:(j + 1) * P], sw2[:, f, :],
                                                            start=(f == 0), stop=(f == FC - 1))
                            last.then_inc(y_full, 1)

                @block.scalar
                def _(act):
                    with act.Fori(0, TURNS) as i:
                        for sl in range(2):
                            for f in range(FC):
                                at = (i * 2 + sl) * FC + f
                                act.wait_ge(h_full, at + 1)
                                act.wait_ge(h_free, at + 1)
                                nc.scalar.activation(act_out[:, f % 2, :], hp[:, f % 2, 1, :], ACT.Silu).then_inc(silu_done, 1)

                @block.vector
                def _(dve):
                    dve.sem_inc(h_free, 2)
                    dve.sem_inc(y_free, 2)
                    with dve.Fori(0, TURNS) as i:
                        for sl in range(2):
                            b = i * 2 + sl
                            for f in range(FC):
                                dve.wait_ge(silu_done, b * FC + f + 1)
                                nc.vector.tensor_tensor(hid[:, f, :], act_out[:, f % 2, :], hp[:, f % 2, 0, :], ALU.mult)\
                                    .then_inc(h_free, 1)
                                r = sl * 3 + f - 1
                                if 1 <= f < 4 and r < ROUNDS // TURNS:
                                    at = (i * (ROUNDS // TURNS) + r) * 2
                                    nc.vector.max(best[:, r, :], key[:]).then_inc(listed, 1)
                                    dve.wait_ge(listed, at + 1)
                                    dve.sem_inc(passed, 1)
                                    nc.vector.match_replace(key[:], best[:, r, :], key[:], 0.0).then_inc(listed, 1)
                                    dve.wait_ge(listed, at + 2)
                            dve.wait_ge(y_full, b + 1)
                            for m in range(2):
                                xs = x[:, bass.ds(b * TB + 2 * m, 2), :].rearrange("p j n -> p (j n)")
                                last = nc.vector.tensor_tensor(xs, xs, yp[:, 2 * sl + m, :], ALU.add)
                            last.then_inc(x_ready, 1)
                            dve.wait_ge(x_ready, b + 1)
                            dve.sem_inc(y_free, 1)
                        nc.vector.tensor_copy(lists[:, bass.ds(i * (CAP // TURNS), CAP // TURNS)],
                                              best[:].rearrange("p r n -> p (r n)")).then_inc(lists_ready, 1)
                        dve.wait_ge(lists_ready, i + 1)

        with ExitStack() as own2:
            k2 = Kit(nc, own2, "me_i_")
            start = k2.sb("start", [P, 1])
            found = k2.sb("found", [P, CAP])
            token = k2.sb("token", [P, CAP])
            flipped = k2.sb("flipped", [P, CAP])
            place = k2.sb("place", [P, 1])
            spare = k2.sb("spare", [P, 2, 1])
            both = k2.sb("both", [P, 2, E])
            empty = k2.sb("empty", [P, 2, E])
            tT = k2.ps("tT", [P, 2, P])
            chained, ready, turned, iota_done = s.sem("i_chained"), s.sem("i_ready"), s.sem("i_turned"), s.sem("i_iota_done")
            with nc.Block() as block:
                @block.gpsimd
                def _(pool):
                    nc.gpsimd.iota(place[:], pattern=[[0, 1]], base=T + 1, channel_multiplier=1,
                                   allow_small_or_imprecise_dtypes=True).then_inc(iota_done, 1)

                @block.tensor
                def _(pe):
                    pe.wait_ge(ready, 1)
                    nc.tensor.transpose(tT[:, 0, :], flipped[:, 0:P], ident[:])
                    nc.tensor.transpose(tT[0:TAIL, 1, :], flipped[:, P:CAP], ident[:]).then_inc(turned, 1)

                @block.vector
                def _(dve):
                    chain = Chain(dve, chained)
                    chain.tick(nc.vector.memset(start[0:P // 2, :], float(TH + 1)))
                    chain.link(nc.vector.memset(start[P // 2:P, :], float(T + 1)))
                    chain.link(nc.vector.tensor_scalar(found[:], lists[:], 0.0, None, ALU.is_gt))
                    chain.link(nc.vector.tensor_scalar(token[:], lists[:], -1.0, start[:], ALU.mult, ALU.add))
                    chain.link(nc.vector.tensor_tensor(token[:], token[:], found[:], ALU.mult))
                    chain.tick(nc.vector.tensor_copy(flipped[0:P // 2, :], token[0:P // 2, :]))
                    chain.tick(nc.vector.tensor_copy(flipped[P // 2:P, :], token[P // 2:P, ::-1]))
                    chain.wait()
                    dve.sem_inc(ready, 1)
                    dve.wait_ge(iota_done, 1)
                    chain.tick(nc.vector.tensor_copy(spare[:, 0, :], place[:]))
                    chain.tick(nc.vector.tensor_scalar(spare[:, 1, :], place[:], float(P), None, ALU.add))
                    chain.wait()
                    dve.wait_ge(turned, 1)
                    for a, (n, index) in enumerate(((P, index_a), (TAIL, index_b))):
                        t, e = both[0:n, a, :], empty[0:n, a, :]
                        chain.link(nc.vector.tensor_copy(t, tT[0:n, a, 0:E]))
                        chain.link(nc.vector.tensor_tensor(t, t, tT[0:n, a, E:2 * E], ALU.add))
                        chain.link(nc.vector.tensor_scalar(e, t, 0.0, spare[0:n, a, :], ALU.is_equal, ALU.mult))
                        chain.link(nc.vector.scalar_tensor_tensor(t, t, -1.0, e, ALU.add, ALU.add))
                        chain.link(nc.vector.tensor_copy(index[:], t))

        w = k.sb("w", [P, 2, DC * 2 * F + FC * D])
        w1 = w[:, :, 0:DC * 2 * F].rearrange("p a (c n) -> p a c n", c=DC)
        w2 = w[:, :, DC * 2 * F:].rearrange("p a (c n) -> p a c n", c=FC)
        xa = k.sb("xa", [P, 2, D + E])
        xb = k.sb("xb", [TAIL, 2, D + E])
        now_a = k.sb("now_a", [P, 2, 1], I32)
        now_b = k.sb("now_b", [TAIL, 2, 1], I32)
        index_ready = s.sem("index_ready")
        xgT = k.sb("xgT", [P, DC, CAP])
        act_out = k.sb("act_out", [P, 2, CAP])
        hid = k.sb("hid", [P, 2, FC, CAP])
        oT = k.sb("oT", [P, DC, CAP])
        oa = k.sb("oa", [P, 2, D])
        ob = k.sb("ob", [TAIL, 2, D])
        xp = k.ps("xp", [P, S])
        hp = k.ps("hp", [P, 3, S])
        op = k.ps("op", [P, DC, S])
        tp = k.ps("tp", [P, 2, S // 2])
        w_loaded, g_loaded = [s.sem("w_loaded0"), s.sem("w_loaded1")], [s.sem("g_loaded0"), s.sem("g_loaded1")]
        e_done, xp_full, xp_free = s.sem("e_done"), s.sem("xp_full"), s.sem("xp_free")
        h_full, silu_done, h_free = s.sem("h_full"), s.sem("silu_done"), s.sem("h_free")
        o_full, o_free, t_full, t_free, added = s.sem("o_full"), s.sem("o_free"), s.sem("t_full"), s.sem("t_free"), s.sem("added")
        rows_free = s.sem("rows_free")
        o_ready, final = s.sem("o_ready"), s.sem("final")

        with nc.Block() as block:
            @block.sync
            def _(sp):
                with sp.Fori(0, E // 2) as i:
                    for sl in range(2):
                        sp.wait_ge(e_done, i * 2 + sl + 1)
                        sp.dma_start(w[:, sl, :], w_exp[bass.ds(i * 2 + sl, 1)].rearrange("a p n -> p (a n)")).then_inc(w_loaded[sl], 16)
                sp.wait_ge(added, 32 * E)
                sp.dma_start(out[:, :], y_dram[0:T, :]).then_inc(final, 16)
                sp.wait_ge(final, 16)

            @block.gpsimd
            def _(pool):
                def gather(e, sl):
                    nc.gpsimd.tensor_copy(now_a[:, sl, :], index_a[:, bass.ds(e, 1)]).then_inc(index_ready, 1)
                    nc.gpsimd.tensor_copy(now_b[:, sl, :], index_b[:, bass.ds(e, 1)]).then_inc(index_ready, 1)
                    pool.wait_ge(index_ready, e * 2 + 2)
                    pool.sem_inc(passed, 1)
                    for dst, index in ((xa, now_a), (xb, now_b)):
                        nc.gpsimd.indirect_dma_start(out=dst[:, sl, :], out_offset=None, in_=rows[:, :],
                                                     in_offset=bass.IndirectOffsetOnAxis(ap=index[:, sl, :], axis=0))\
                            .then_inc(g_loaded[sl], 16)

                def scatter(e, sl):
                    pool.wait_ge(o_ready, e + 1)
                    pool.sem_inc(passed, 1)
                    for src, index in ((oa, now_a), (ob, now_b)):
                        nc.gpsimd.indirect_dma_start(out=y_dram[:, :],
                                                     out_offset=bass.IndirectOffsetOnAxis(ap=index[:, sl, :], axis=0),
                                                     in_=src[:, sl, :], in_offset=None, compute_op=ALU.add).then_inc(added, 16)
                    pool.wait_ge(added, e * 32 + 32)
                    pool.sem_inc(rows_free, 1)

                pool.sem_inc(rows_free, 2)
                gather(0, 0)
                gather(1, 1)
                with pool.Fori(0, E // 2 - 1) as i:
                    for sl in range(2):
                        scatter(i * 2 + sl, sl)
                        gather(i * 2 + sl + 2, sl)
                scatter(E - 2, 0)
                scatter(E - 1, 1)

            @block.tensor
            def _(pe):
                pe.sem_inc(e_done, 2)

                def turn_in(e, sl, earlier):
                    pe.wait_ge(g_loaded[sl], earlier * 32 + 32)
                    pe.wait_ge(xp_free, e + 1)
                    for c in range(DC):
                        cols = slice(c * P, (c + 1) * P)
                        nc.tensor.transpose(xp[:, c * CAP:c * CAP + P], xa[:, sl, cols], ident[:])
                        last = nc.tensor.transpose(xp[:, c * CAP + P:(c + 1) * CAP], xb[:, sl, cols], ident[0:TAIL, 0:TAIL])
                    last.then_inc(xp_full, 1)

                def turn_out(e):
                    pe.wait_ge(o_free, e + 2)
                    pe.wait_ge(t_free, e + 1)
                    for c in range(DC):
                        cols = slice(c * P, (c + 1) * P)
                        nc.tensor.transpose(tp[:, 0, cols], oT[:, c, 0:P], ident[:])
                        last = nc.tensor.transpose(tp[0:TAIL, 1, cols], oT[:, c, P:CAP], ident[:])
                    last.then_inc(t_full, 1)

                def one(e, sl, earlier, first):
                    turn_in(e, sl, earlier)
                    pe.wait_ge(xp_free, e + 2)
                    pe.wait_ge(w_loaded[sl], earlier * 16 + 16)
                    for f in range(FC):
                        at = e * FC + f
                        pe.wait_ge(h_free, at + 1)
                        for half in range(2):
                            for c in range(DC):
                                cols = slice(half * F + f * P, half * F + (f + 1) * P)
                                last = nc.tensor.matmul(hp[:, f % 3, half * CAP:(half + 1) * CAP], w1[:, sl, c, cols], xgT[:, c, :],
                                                        start=(c == 0), stop=(c == DC - 1))
                        last.then_inc(h_full, 1)
                        if f == 1 and not first:
                            turn_out(e - 1)
                    pe.wait_ge(o_free, e + 1)
                    for f in range(FC):
                        pe.wait_ge(h_free, e * FC + f + 1 + 3)
                        for c in range(DC):
                            last = nc.tensor.matmul(op[:, c, 0:CAP], w2[:, sl, f, c * P:(c + 1) * P], hid[:, sl, f, :],
                                                    start=(f == 0), stop=(f == FC - 1))
                    last.then_inc(o_full, 1)
                    pe.wait_ge(o_full, e + 1)
                    pe.sem_inc(e_done, 1)

                experts_in_turn(pe, E, one)
                turn_out(E - 1)

            @block.scalar
            def _(act):
                act.sem_inc(o_free, 1)

                def one(e, sl, earlier, first):
                    for f in range(FC):
                        at = e * FC + f
                        act.wait_ge(h_full, at + 1)
                        act.wait_ge(h_free, at + 2)
                        nc.scalar.activation(act_out[:, f % 2, :], hp[:, f % 3, CAP:2 * CAP], ACT.Silu).then_inc(silu_done, 1)
                    act.wait_ge(o_full, e + 1)
                    nc.scalar.activation(oT[:], op[:, :, 0:CAP], ACT.Copy).then_inc(o_free, 1)

                experts_in_turn(act, E, one)

            @block.vector
            def _(dve):
                dve.sem_inc(xp_free, 1)
                dve.sem_inc(h_free, 3)
                dve.sem_inc(t_free, 1)

                def weigh(e, sl):
                    dve.wait_ge(t_full, e + 1)
                    dve.wait_ge(rows_free, e + 1)
                    nc.vector.tensor_scalar(oa[:, sl, :], tp[:, 0, :], xa[:, sl, bass.ds(e + D, 1)], None, ALU.mult).then_inc(t_free, 1)
                    nc.vector.tensor_scalar(ob[:, sl, :], tp[0:TAIL, 1, :], xb[:, sl, bass.ds(e + D, 1)], None, ALU.mult)\
                        .then_inc(o_ready, 1)

                def one(e, sl, earlier, first):
                    dve.wait_ge(xp_full, e + 1)
                    nc.vector.tensor_copy(xgT[:], xp[:, 0:DC * CAP].rearrange("p (c n) -> p c n", c=DC)).then_inc(xp_free, 1)
                    for f in range(FC):
                        dve.wait_ge(silu_done, e * FC + f + 1)
                        nc.vector.tensor_tensor(hid[:, sl, f, :], act_out[:, f % 2, :], hp[:, f % 3, 0:CAP], ALU.mult).then_inc(h_free, 1)
                        if f == 1 and not first:
                            weigh(e - 1, 1 - sl)

                experts_in_turn(dve, E, one)
                weigh(E - 1, 1)
        s.clear()


def program(nc, a, out):
    scratch = {name: nc.dram_tensor(name, shape, dtype).ap() for name, shape, dtype in (
        ("lag_products", [P, 2 * S], F32), ("lag_weights", [1, 3 * S], F32),
        ("part_rows", [2, 3, D, S], BF16), ("mask_rows", [B, S], BF16),
        ("token_rows", [B * S + 160, D + 64], F32), ("sums", [B * S + 160, D], F32))}
    with ExitStack() as ctx:
        k = Kit(nc, ctx, "all_")
        x = k.sb("x", [P, NT, D])
        ident = k.sb("ident", [P, P])
        ident_bf = k.sb("ident_bf", [P, P], BF16)
        mean = k.sb("mean", [P, NT])
        rstd = k.sb("rstd", [P, NT])
        x_loaded = k.sem("x_loaded")
        identity_stage(nc, ctx, ident, ident_bf)
        with nc.Block() as block:
            @block.sync
            def _(sp):
                sp.dma_start(x[:], a["x"].rearrange("b (j p) d -> p (b j) d", p=P)).then_inc(x_loaded, 16)
                sp.wait_ge(x_loaded, 16)
        norm_stats(nc, ctx, "l0a", x, mean, rstd)
        mix_attention(nc, ctx, x, ident, ident_bf, mean, rstd, a["L0_attn_weight_qkv"], a["L0_attn_out_wT"], a["L0_attn_out_b"])
        norm_stats(nc, ctx, "l0x", x, mean, rstd)
        mix_correlation(nc, ctx, x, ident, mean, rstd, a["ctx_1024"], a["L0_xattn_Wq"], a["L0_xattn_bq"], a["L0_xattn_Wout"],
                        a["L0_xattn_bout"], scratch["lag_products"], scratch["lag_weights"])
        norm_stats(nc, ctx, "l0f", x, mean, rstd)
        mix_experts_dense(nc, ctx, x, ident, mean, rstd, a["L0_ffn_Wg"], a["L0_ffn_w_in"], a["L0_ffn_w_out"], 2)
        norm_stats(nc, ctx, "l1a", x, mean, rstd)
        mix_recurrence(nc, ctx, x, ident, mean, rstd, a["L1_attn_A"], a["L1_attn_BC"])
        norm_stats(nc, ctx, "l1x", x, mean, rstd)
        mix_heads(nc, ctx, x, ident, ident_bf, mean, rstd, a["ctx_1024"], a["mask"], a["L1_xattn_WvT"], a["L1_xattn_WkT"],
                  a["L1_xattn_WqT"], a["L1_xattn_WoT"], a["L1_xattn_bo"], scratch["part_rows"], scratch["mask_rows"])
        norm_stats(nc, ctx, "l1f", x, mean, rstd)
        mix_experts_sparse(nc, ctx, x, ident, mean, rstd, a["L1_ffn_wgT"], a["L1_ffn_w_exp"], a["L1_ffn_shared_w1T"],
                           a["L1_ffn_shared_w2T"], scratch["token_rows"], scratch["sums"], out)


def laid_out(i):
    i = {name: np.asarray(v) for name, v in i.items()}

    def by_partition(w):
        n, c, m = w.shape[0], w.shape[1] // P, w.shape[2]
        return w.reshape(n, c, P, m).transpose(0, 2, 1, 3).reshape(n, P, c * m)

    def slices(w, axis):
        return np.stack(np.split(w, w.shape[axis] // P, axis=axis))

    w1, w3, w2 = (np.concatenate([i[f"L0_ffn_W{n}"], slices(i[f"L0_ffn_Ws{n}"], axis)]) for n, axis in ((1, 1), (3, 1), (2, 0)))
    a = {name: i[name] for name in ("x", "ctx_1024", "L0_attn_weight_qkv", "L0_attn_out_b", "L0_xattn_Wq", "L0_xattn_bq",
                                    "L0_xattn_Wout", "L0_xattn_bout", "L0_ffn_Wg", "L1_attn_A", "L1_attn_BC", "L1_xattn_bo")}
    a["mask"] = i["mask_Bx1x1xS2_if1"]
    a["L0_ffn_w_in"] = by_partition(np.concatenate([w1, w3], axis=2))
    a["L0_ffn_w_out"] = w2
    a["L1_ffn_w_exp"] = np.concatenate([by_partition(i["L1_ffn_expert_w1"].transpose(0, 2, 1)),
                                        by_partition(i["L1_ffn_expert_w2"].transpose(0, 2, 1))], axis=2)
    for name in ("L0_attn_out_w", "L1_xattn_Wv", "L1_xattn_Wk", "L1_xattn_Wq", "L1_xattn_Wo", "L1_ffn_wg",
                 "L1_ffn_shared_w1", "L1_ffn_shared_w2"):
        a[name + "T"] = i[name].T
    return {name: np.ascontiguousarray(v) for name, v in a.items()}


def kernel(**inputs):
    import concourse.bacc as bacc
    from concourse.bass_utils import run_bass_kernel_spmd

    nc = bacc.Bacc("TRN2", target_bir_lowering=False, num_devices=1)
    arrays = laid_out(inputs)
    aps = {name: nc.dram_tensor("in_" + name, v.shape, mybir.dt.from_np(v.dtype), kind="ExternalInput").ap()
           for name, v in arrays.items()}
    out = nc.dram_tensor("out_x", (B * S, D), F32, kind="ExternalOutput").ap()
    program(nc, aps, out)
    r = run_bass_kernel_spmd(nc, [{"in_" + name: v for name, v in arrays.items()}], core_ids=[0])
    return r.results[0]["out_x"].reshape(B, S, D)
```

```python
from contextlib import ExitStack

import numpy as np

import concourse.bass as bass
from concourse import mybir
from concourse.alu_op_type import AluOpType as ALU

F32 = mybir.dt.float32
F16 = mybir.dt.float16
BF16 = mybir.dt.bfloat16
I32 = mybir.dt.int32
U32 = mybir.dt.uint32
ACT = mybir.ActivationFunctionType
AX = mybir.AxisListType

P = 128
B, S, D = 8, 512, 256
NT = B * S // P
TB = S // P
DC = D // P
TURNS = B // 2
EPS = 1e-5


class Kit:

    def __init__(self, nc, ctx, prefix):
        self.nc, self.ctx, self.prefix, self.sems = nc, ctx, prefix, []

    def sb(self, name, shape, dtype=F32):
        return self.ctx.enter_context(self.nc.sbuf_tensor(self.prefix + name, shape, dtype))

    def ps(self, name, shape, dtype=F32):
        return self.ctx.enter_context(self.nc.psum_tensor(self.prefix + name, shape, dtype))

    def sem(self, name):
        self.sems.append(self.ctx.enter_context(self.nc.semaphore(self.prefix + name)))
        return self.sems[-1]

    def clear(self):
        with self.nc.Block() as block:
            @block.sync
            def _(sp):
                for sem in self.sems:
                    sp.sem_clear(sem)


class Chain:

    def __init__(self, eng, sem):
        self.eng, self.sem, self.base, self.n = eng, sem, 0, 0

    def turn(self, base):
        self.base, self.n = base, 0

    def tick(self, ins):
        ins.then_inc(self.sem, 1)
        self.n += 1

    def wait(self):
        self.eng.wait_ge(self.sem, self.base + self.n)

    def link(self, ins):
        self.tick(ins)
        self.wait()


def identity_stage(nc, ctx, ident, ident_bf):
    k = Kit(nc, ctx, "id_")
    zero_done, ident_done = k.sem("zero_done"), k.sem("ident_done")
    with nc.Block() as block:
        @block.gpsimd
        def _(pool):
            nc.gpsimd.memset(ident[:], 0.0).then_inc(zero_done, 1)
            pool.wait_ge(zero_done, 1)
            nc.gpsimd.affine_select(out=ident[:], in_=ident[:], compare_op=ALU.not_equal, fill=1.0, base=0,
                                    pattern=[[-1, P]], channel_multiplier=1).then_inc(ident_done, 1)
            pool.wait_ge(ident_done, 1)
            nc.gpsimd.tensor_copy(ident_bf[:], ident[:]).then_inc(ident_done, 1)
            pool.wait_ge(ident_done, 2)


def norm_stats(nc, ctx, name, x, mean, rstd):
    with ExitStack() as own:
        k = Kit(nc, own, name + "_st_")
        s = Kit(nc, own, name + "_st_")
        stats = k.sb("stats", [P, NT, 6])
        half_diff = k.sb("half_diff", [P, NT])
        var = k.sb("var", [P, NT])
        dev = k.sb("dev", [P, NT])
        dve_done, dev_done, stats_done, var_done = s.sem("dve_done"), s.sem("dev_done"), s.sem("stats_done"), s.sem("var_done")
        with nc.Block() as block:
            @block.vector
            def _(dve):
                with dve.Fori(0, NT // 4) as i:
                    for j in range(4):
                        nc.vector.bn_stats(stats[:, i * 4 + j, :], x[:, i * 4 + j, :]).then_inc(stats_done, 1)
                dve.wait_ge(stats_done, NT)
                chain = Chain(dve, dve_done)
                me, mo = stats[:, :, 1], stats[:, :, 4]
                chain.link(nc.vector.tensor_tensor(mean[:], me, mo, ALU.add))
                chain.link(nc.vector.tensor_scalar(mean[:], mean[:], 0.5, None, ALU.mult))
                chain.link(nc.vector.tensor_tensor(half_diff[:], me, mo, ALU.subtract))
                chain.link(nc.vector.scalar_tensor_tensor(half_diff[:], half_diff[:], 0.25, half_diff[:], ALU.mult, ALU.mult))
                chain.link(nc.vector.tensor_tensor(var[:], stats[:, :, 2], stats[:, :, 5], ALU.add))
                chain.link(nc.vector.scalar_tensor_tensor(var[:], var[:], 1.0 / D, half_diff[:], ALU.mult, ALU.add))
                nc.vector.tensor_scalar(var[:], var[:], EPS, None, ALU.add).then_inc(var_done, 1)
                dve.wait_ge(dev_done, 1)
                chain.link(nc.vector.reciprocal(rstd[:], dev[:]))

            @block.scalar
            def _(act):
                act.wait_ge(var_done, 1)
                nc.scalar.activation(dev[:], var[:], ACT.Sqrt).then_inc(dev_done, 1)
        s.clear()


def mix_attention(nc, ctx, x, ident, ident_bf, mean, rstd, w_qkv, out_wT, out_b):
    with ExitStack() as own:
        k = Kit(nc, own, "at_")
        s = Kit(nc, own, "at_")
        Q4 = D // 4
        xn = k.sb("xn", [P, 2, TB, D])
        xT_low = k.sb("xT_low", [P, 2, S], F16)
        xT_high = k.sb("xT_high", [P, 2, S])
        w_low32 = k.sb("w_low32", [P, 3 * D])
        w_low = k.sb("w_low", [P, 3 * D], F16)
        w_high = k.sb("w_high", [P, 3 * D])
        w_out = k.sb("w_out", [P, DC, D])
        bias = k.sb("bias", [P, D])
        qT = k.sb("qT", [P, 2, DC, S])
        kT = k.sb("kT", [P, 2, DC, S])
        v = k.sb("v", [P, 2, TB, D])
        prob = k.sb("prob", [P, 2, TB, S])
        probT = k.sb("probT", [P, 2, TB, S])
        yT = k.sb("yT", [P, 2, DC, S])
        nmax = k.sb("nmax", [P, 2, TB])
        total = k.sb("total", [P, 2, TB])
        rtotal = k.sb("rtotal", [P, 2, TB])
        turned = k.ps("turned", [P, 2, S])
        proj = k.ps("proj", [P, 2, S])
        score = k.ps("score", [P, 2, S])
        outp = k.ps("outp", [P, 2, S])
        loaded, w_ready = s.sem("loaded"), s.sem("w_ready")
        xn_ready, batch_done = s.sem("xn_ready"), s.sem("batch_done")
        turned_full, turned_free = s.sem("turned_full"), s.sem("turned_free")
        proj_full, proj_free = s.sem("proj_full"), s.sem("proj_free")
        score_full, score_free = s.sem("score_full"), s.sem("score_free")
        out_full, out_free = s.sem("out_full"), s.sem("out_free")
        nmax_ready, rtot_ready, bias_added = s.sem("nmax_ready"), s.sem("rtot_ready"), s.sem("bias_added")
        NSC, NOUT = 4, 2
        NTURN, NPROJ = 12, 16

        with nc.Block() as block:
            @block.sync
            def _(sp):
                sp.dma_start(w_low32[0:Q4, :], w_qkv[0:Q4, :]).then_inc(loaded, 16)
                sp.dma_start(w_low32[Q4:P, :], w_qkv[D - Q4:D, :]).then_inc(loaded, 16)
                sp.dma_start(w_high[:], w_qkv[Q4:D - Q4, :]).then_inc(loaded, 16)
                sp.dma_start(w_out[:], out_wT.rearrange("(c p) n -> p c n", p=P)).then_inc(loaded, 16)
                sp.dma_start(bias[:], out_b.rearrange("(a n) -> a n", a=1).to_broadcast([P, D])).then_inc(loaded, 16)

            @block.gpsimd
            def _(pool):
                pool.wait_ge(loaded, 80)
                with pool.Fori(0, B) as b:
                    pool.wait_ge(xn_ready, b * TB + TB)
                    for j in range(TB):
                        last = nc.gpsimd.tensor_tensor(x[:, b * TB + j, :], x[:, b * TB + j, :], bias[:], ALU.add)
                    last.then_inc(bias_added, 1)

            @block.tensor
            def _(pe):
                pe.sem_inc(batch_done, 2)
                pe.wait_ge(w_ready, 1)
                with pe.Fori(0, TURNS) as i:
                    for sl in range(2):
                        b = i * 2 + sl
                        pe.wait_ge(xn_ready, b * TB + TB)
                        for half in range(2):
                            pe.wait_ge(turned_free, i * NTURN + 2 * sl + half + 1)
                            for j in range(TB):
                                last = nc.tensor.transpose(turned[:, half, j * P:(j + 1) * P],
                                                           xn[:, sl, j, half * P:(half + 1) * P], ident[:])
                            last.then_inc(turned_full, 1)
                        pe.wait_ge(turned_free, i * NTURN + 2 * sl + 2 + 2)
                        for m in range(4):
                            pe.wait_ge(proj_free, i * NPROJ + 6 * sl + m + 1)
                            cols = slice(m * P, (m + 1) * P)
                            nc.tensor.matmul(proj[:, m % 2, :], w_high[:, cols], xT_high[:, sl, :], start=True, stop=False)
                            nc.tensor.matmul(proj[:, m % 2, :], w_low[:, cols], xT_low[:, sl, :], start=False, stop=True)\
                                .then_inc(proj_full, 1)
                        for m in range(2):
                            pe.wait_ge(proj_free, i * NPROJ + 6 * sl + 4 + m + 1)
                            for j in range(2):
                                t = slice((2 * m + j) * P, (2 * m + j + 1) * P)
                                o = proj[:, m, j * D:(j + 1) * D]
                                nc.tensor.matmul(o, xT_high[:, sl, t], w_high[:, 2 * D:3 * D], start=True, stop=False)
                                last = nc.tensor.matmul(o, xT_low[:, sl, t], w_low[:, 2 * D:3 * D], start=False, stop=True)
                            last.then_inc(proj_full, 1)
                    for sl in range(2):
                        b = i * 2 + sl
                        pe.wait_ge(proj_free, i * NPROJ + 6 * sl + 4 + 2)
                        for qc in range(TB):
                            pe.wait_ge(score_free, b * NSC + qc + 1)
                            for c in range(DC):
                                last = nc.tensor.matmul(score[:, qc % 2, :], qT[:, sl, c, qc * P:(qc + 1) * P],
                                                        kT[:, sl, c, :], start=(c == 0), stop=(c == DC - 1))
                            last.then_inc(score_full, 1)
                    for sl in range(2):
                        b = i * 2 + sl
                        pe.wait_ge(score_free, b * NSC + TB + 2)
                        for kc in range(TB):
                            pe.wait_ge(turned_free, i * NTURN + 4 + TB * sl + kc + 1)
                            for qc in range(TB):
                                last = nc.tensor.transpose(turned[:, kc % 2, qc * P:(qc + 1) * P],
                                                           prob[:, sl, qc, kc * P:(kc + 1) * P], ident[:])
                            last.then_inc(turned_full, 1)
                        pe.wait_ge(turned_free, i * NTURN + 4 + TB * sl + TB + 2)
                        for c in range(DC):
                            pe.wait_ge(proj_free, i * NPROJ + 12 + 2 * sl + c + 1)
                            for kc in range(TB):
                                last = nc.tensor.matmul(proj[:, c, :], v[:, sl, kc, c * P:(c + 1) * P], probT[:, sl, kc, :],
                                                        start=(kc == 0), stop=(kc == TB - 1))
                            last.then_inc(proj_full, 1)
                        pe.wait_ge(proj_free, i * NPROJ + 12 + 2 * sl + 2 + 2)
                        for m in range(2):
                            pe.wait_ge(out_free, b * NOUT + m + 1)
                            for j in range(2):
                                t = slice((2 * m + j) * P, (2 * m + j + 1) * P)
                                for c in range(DC):
                                    last = nc.tensor.matmul(outp[:, m, j * D:(j + 1) * D], yT[:, sl, c, t], w_out[:, c, :],
                                                            start=(c == 0), stop=(c == DC - 1))
                            last.then_inc(out_full, 1)
                        pe.wait_ge(out_full, b * NOUT + 2)
                        pe.sem_inc(batch_done, 1)

            @block.scalar
            def _(act):
                act.sem_inc(turned_free, 2)
                act.sem_inc(score_free, 2)
                with act.Fori(0, TURNS) as i:
                    for sl in range(2):
                        b = i * 2 + sl
                        act.wait_ge(batch_done, b + 1)
                        for half in range(2):
                            act.wait_ge(turned_full, i * NTURN + 2 * sl + half + 1)
                            dst = xT_low[:, sl, :] if half == 0 else xT_high[:, sl, :]
                            nc.scalar.activation(dst, turned[:, half, :], ACT.Copy).then_inc(turned_free, 1)
                    for sl in range(2):
                        b = i * 2 + sl
                        for qc in range(TB):
                            act.wait_ge(nmax_ready, b * NSC + qc + 1)
                            nc.scalar.activation(prob[:, sl, qc, :], score[:, qc % 2, :], ACT.Exp,
                                                 bias=nmax[:, sl, qc:qc + 1],
                                                 accum_out=total[:, sl, qc:qc + 1]).then_inc(score_free, 1)
                    for sl in range(2):
                        b = i * 2 + sl
                        for kc in range(TB):
                            act.wait_ge(turned_full, i * NTURN + 4 + TB * sl + kc + 1)
                            nc.scalar.activation(probT[:, sl, kc, :], turned[:, kc % 2, :], ACT.Copy).then_inc(turned_free, 1)

            @block.vector
            def _(dve):
                dve.wait_ge(loaded, 80)
                nc.vector.tensor_copy(w_low[:], w_low32[:]).then_inc(w_ready, 1)
                dve.sem_inc(proj_free, 2)
                dve.sem_inc(out_free, 2)
                with dve.Fori(0, TURNS) as i:
                    for sl in range(2):
                        b = i * 2 + sl
                        dve.wait_ge(batch_done, b + 1)
                        for j in range(TB):
                            t = b * TB + j
                            for half, cols in enumerate((slice(0, 4, 3), slice(1, 3))):
                                last = nc.vector.tensor_scalar(
                                    xn[:, sl, j, half * P:(half + 1) * P].rearrange("p (a c) -> p a c", a=2),
                                    x[:, t, :].rearrange("p (a c) -> p a c", a=4)[:, cols, :],
                                    mean[:, bass.ds(t, 1)], rstd[:, bass.ds(t, 1)], ALU.subtract, ALU.mult)
                            last.then_inc(xn_ready, 1)
                    for sl in range(2):
                        b = i * 2 + sl
                        for m in range(6):
                            dve.wait_ge(proj_full, i * NPROJ + 6 * sl + m + 1)
                            if m < 2:
                                nc.vector.tensor_scalar(qT[:, sl, m, :], proj[:, m % 2, :], D ** -0.5, None, ALU.mult)\
                                    .then_inc(proj_free, 1)
                            elif m < 4:
                                nc.vector.tensor_copy(kT[:, sl, m - 2, :], proj[:, m % 2, :]).then_inc(proj_free, 1)
                            else:
                                j = 2 * (m - 4)
                                nc.vector.tensor_copy(v[:, sl, j:j + 2, :].rearrange("p j n -> p (j n)"), proj[:, m % 2, :])\
                                    .then_inc(proj_free, 1)
                    for sl in range(2):
                        b = i * 2 + sl
                        for qc in range(TB):
                            dve.wait_ge(score_full, b * NSC + qc + 1)
                            nc.vector.tensor_reduce(nmax[:, sl, qc:qc + 1], score[:, qc % 2, :], AX.X, ALU.max, negate=True)\
                                .then_inc(nmax_ready, 1)
                    for sl in range(2):
                        b = i * 2 + sl
                        dve.wait_ge(score_free, b * NSC + TB + 2)
                        nc.vector.reciprocal(rtotal[:, sl, :], total[:, sl, :]).then_inc(rtot_ready, 1)
                        for c in range(DC):
                            dve.wait_ge(proj_full, i * NPROJ + 12 + 2 * sl + c + 1)
                            nc.vector.tensor_copy(yT[:, sl, c, :], proj[:, c, :]).then_inc(proj_free, 1)
                        dve.wait_ge(rtot_ready, b + 1)
                        dve.wait_ge(bias_added, b + 1)
                        for m in range(2):
                            dve.wait_ge(out_full, b * NOUT + m + 1)
                            for j in range(2):
                                qc = 2 * m + j
                                t = b * TB + qc
                                last = nc.vector.scalar_tensor_tensor(x[:, t, :], outp[:, m, j * D:(j + 1) * D],
                                                                      rtotal[:, sl, qc:qc + 1], x[:, t, :], ALU.mult, ALU.add)
                            last.then_inc(out_free, 1)
                dve.wait_ge(out_free, B * NOUT + 2)
        s.clear()


def mix_correlation(nc, ctx, x, ident, mean, rstd, ctx_in, w_q, b_q, w_out, b_out, h_dram, c_dram):
    with ExitStack() as own:
        k = Kit(nc, own, "xa_")
        s = Kit(nc, own, "xa_")
        DH = 16
        TOP = int(2 * np.log(S))
        NCOL = B * DH
        LIST = S + 8
        PAD, TAKEN = -3.2e38, -3.3e38
        xn = k.sb("xn", [P, 2, TB, D])
        cx = k.sb("cx", [P, 2, TB, D])
        xT = k.sb("xT", [P, 2, DC, S])
        cT = k.sb("cT", [P, 2, DC, S])
        wq = k.sb("wq", [P, DC, DH])
        bq = k.sb("bq", [P, TB, DH])
        wo = k.sb("wo", [P, DC, D])
        bo = k.sb("bo", [1, D])
        ones = k.sb("ones", [P, P])
        q_tok = k.sb("q_tok", [P, TB, NCOL])
        k_tok = k.sb("k_tok", [P, TB, NCOL])
        qT = k.sb("qT", [P, 2 * S])
        kT = k.sb("kT", [P, S])
        h = k.sb("h", [P, 2 * S])
        h_skew = k.sb("h_skew", [P, S])
        corr = k.sb("corr", [1, LIST])
        left = k.sb("left", [1, LIST])
        left2 = k.sb("left2", [1, LIST])
        top = k.sb("top", [1, 16])
        ntop = k.sb("ntop", [1, 1])
        weight = k.sb("weight", [1, S])
        wsum = k.sb("wsum", [1, 1])
        wr = k.sb("wr", [1, 1])
        c3 = k.sb("c3", [1, 3, S])
        hankel = k.sb("hankel", [P, TB, S + 1])
        circ = k.sb("circ", [P, TB, S])
        z = k.sb("z", [P, DC, B, P])
        tp = k.ps("tp", [P, 4, S])
        proj = k.ps("proj", [P, 2, S])
        misc = k.ps("misc", [P, 2, S])
        loaded, ctx_loaded = s.sem("loaded"), [s.sem("ctx_loaded0"), s.sem("ctx_loaded1")]
        xn_ready, batch_done = s.sem("xn_ready"), s.sem("batch_done")
        tp_full, tp_free = s.sem("tp_full"), s.sem("tp_free")
        proj_full, proj_free = s.sem("proj_full"), s.sem("proj_free")
        ones_ready, dve_done = s.sem("ones_ready"), s.sem("dve_done")
        turned, turned_out, h_full, h_out = s.sem("turned"), s.sem("turned_out"), s.sem("h_full"), s.sem("h_out")
        h_stored, h_back, corr_full, ntop_ready = s.sem("h_stored"), s.sem("h_back"), s.sem("corr_full"), s.sem("ntop_ready")
        weight_ready, c_ready, c_stored, c_back = s.sem("weight_ready"), s.sem("c_ready"), s.sem("c_stored"), s.sem("c_back")
        circ_ready = s.sem("circ_ready")
        r_full, z_ready, y_full, y_free = s.sem("r_full"), s.sem("z_ready"), s.sem("y_full"), s.sem("y_free")
        ctx_tok = ctx_in.rearrange("b (j p) d -> b p j d", p=P)

        with nc.Block() as block:
            @block.sync
            def _(sp):
                sp.dma_start(wq[:], w_q.rearrange("(c p) n -> p c n", p=P)).then_inc(loaded, 16)
                sp.dma_start(bq[:, 0, :], b_q.rearrange("(a n) -> a n", a=1).to_broadcast([P, DH])).then_inc(loaded, 16)
                sp.dma_start(wo[:], w_out.rearrange("(c p) n -> p c n", p=P)).then_inc(loaded, 16)
                sp.dma_start(bo[:], b_out.rearrange("(a n) -> a n", a=1)).then_inc(loaded, 16)
                with sp.Fori(0, TURNS) as i:
                    for sl in range(2):
                        sp.wait_ge(batch_done, i * 2 + sl + 1)
                        sp.dma_start(cx[:, sl, :, :], ctx_tok[bass.ds(i * 2 + sl, 1), :, :, :].rearrange("a p j d -> p (a j) d"))\
                            .then_inc(ctx_loaded[sl], 16)
                sp.wait_ge(h_out, 2)
                sp.dma_start(h_dram[:, :], h[:]).then_inc(h_stored, 16)
                sp.wait_ge(h_stored, 16)
                skewed = h_dram.rearrange("p n -> (p n)")[0:P * (2 * S + 1) - P].rearrange("(p n) -> p n", p=P)
                skewed = bass.AP(tensor=h_dram.tensor, offset=0, ap=[[2 * S + 1, P], [1, S]])
                sp.dma_start(h_skew[:], skewed).then_inc(h_back, 16)
                sp.wait_ge(c_ready, 3)
                sp.dma_start(c_dram[:, :], c3[:].rearrange("a n m -> a (n m)")).then_inc(c_stored, 16)
                sp.wait_ge(c_stored, 16)
                for j in range(TB):
                    sp.dma_start(hankel[:, j, :], bass.AP(tensor=c_dram.tensor, offset=j * P, ap=[[1, P], [1, S + 1]]))\
                        .then_inc(c_back, 16)

            @block.gpsimd
            def _(pool):
                nc.gpsimd.memset(ones[:], 1.0).then_inc(ones_ready, 1)

            @block.tensor
            def _(pe):
                pe.sem_inc(batch_done, 2)
                pe.wait_ge(loaded, 64)
                with pe.Fori(0, TURNS) as i:
                    for sl in range(2):
                        b = i * 2 + sl
                        pe.wait_ge(xn_ready, b * TB + TB)
                        pe.wait_ge(ctx_loaded[sl], i * 16 + 16)
                        for c in range(4):
                            pe.wait_ge(tp_free, b * 4 + c + 1)
                            src = xn if c < 2 else cx
                            for j in range(TB):
                                last = nc.tensor.transpose(tp[:, c, j * P:(j + 1) * P],
                                                           src[:, sl, j, (c % 2) * P:(c % 2 + 1) * P], ident[:])
                            last.then_inc(tp_full, 1)
                    for sl in range(2):
                        b = i * 2 + sl
                        pe.wait_ge(tp_free, (b + 1) * 4 + 4)
                        for n, src in enumerate((xT, cT)):
                            pe.wait_ge(proj_free, b * 2 + n + 1)
                            for j in range(TB):
                                for c in range(DC):
                                    last = nc.tensor.matmul(proj[:, n, j * DH:(j + 1) * DH], src[:, sl, c, j * P:(j + 1) * P],
                                                            wq[:, c, :], start=(c == 0), stop=(c == DC - 1))
                            last.then_inc(proj_full, 1)
                        pe.wait_ge(proj_full, b * 2 + 2)
                        pe.sem_inc(batch_done, 1)
                pe.wait_ge(proj_free, B * 2 + 2)
                for n, src in enumerate((q_tok, k_tok)):
                    for j in range(TB):
                        last = nc.tensor.transpose(misc[:, n, j * P:(j + 1) * P], src[:, j, :], ident[:])
                    last.then_inc(turned, 1)
                pe.wait_ge(turned_out, 3)
                for j in range(TB):
                    last = nc.tensor.matmul(misc[:, 0, :], kT[:, j * P:(j + 1) * P], qT[:, j * P:j * P + S],
                                            start=(j == 0), stop=(j == TB - 1))
                last.then_inc(h_full, 1)
                pe.wait_ge(h_back, 16)
                pe.wait_ge(ones_ready, 1)
                nc.tensor.matmul(misc[0:1, 1, :], ones[:, 0:1], h_skew[:], start=True, stop=True).then_inc(corr_full, 1)
                pe.wait_ge(circ_ready, 1)
                for t in range(TB):
                    for j in range(TB):
                        last = nc.tensor.matmul(misc[:, 0, t * P:(t + 1) * P], circ[:, j, t * P:(t + 1) * P],
                                                k_tok[:, j, :], start=(j == 0), stop=(j == TB - 1))
                last.then_inc(r_full, 1)
                pe.wait_ge(z_ready, 2)
                for b in range(B):
                    if b >= 2:
                        pe.wait_ge(y_free, b - 1)
                    o = proj[:, b % 2, 0:D]
                    for c in range(DC):
                        nc.tensor.matmul(o, z[:, c, b, :], wo[:, c, :], start=(c == 0), stop=False)
                    nc.tensor.matmul(o, ones[0:1, :], bo[:], start=False, stop=True).then_inc(y_full, 1)

            @block.scalar
            def _(act):
                act.sem_inc(tp_free, 4)
                with act.Fori(0, TURNS) as i:
                    for sl in range(2):
                        b = i * 2 + sl
                        act.wait_ge(batch_done, b + 1)
                        for c in range(4):
                            act.wait_ge(tp_full, b * 4 + c + 1)
                            dst = (xT if c < 2 else cT)[:, sl, c % 2, :]
                            nc.scalar.activation(dst, tp[:, c, :], ACT.Copy).then_inc(tp_free, 1)
                act.wait_ge(ntop_ready, 1)
                nc.scalar.activation(weight[:], corr[:, 0:S], ACT.Exp, bias=ntop[:]).then_inc(weight_ready, 1)

            @block.vector
            def _(dve):
                dve.wait_ge(loaded, 64)
                dve.sem_inc(proj_free, 2)
                chain = Chain(dve, dve_done)
                for j in range(1, TB):
                    chain.tick(nc.vector.tensor_copy(bq[:, j, :], bq[:, 0, :]))
                chain.wait()
                with dve.Fori(0, TURNS) as i:
                    for sl in range(2):
                        b = i * 2 + sl
                        dve.wait_ge(batch_done, b + 1)
                        for j in range(TB):
                            t = b * TB + j
                            nc.vector.tensor_scalar(xn[:, sl, j, :], x[:, t, :], mean[:, bass.ds(t, 1)], rstd[:, bass.ds(t, 1)],
                                                    ALU.subtract, ALU.mult).then_inc(xn_ready, 1)
                    for sl in range(2):
                        b = i * 2 + sl
                        for n, dst in enumerate((q_tok, k_tok)):
                            dve.wait_ge(proj_full, b * 2 + n + 1)
                            nc.vector.tensor_tensor(dst[:, :, bass.ds(b * DH, DH)],
                                                    proj[:, n, 0:TB * DH].rearrange("p (j n) -> p j n", j=TB),
                                                    bq[:], ALU.add).then_inc(proj_free, 1)
                dve.wait_ge(turned, 1)
                nc.vector.tensor_copy(qT[:, 0:S], misc[:, 0, :]).then_inc(turned_out, 1)
                nc.vector.tensor_copy(qT[:, S:2 * S], misc[:, 0, :]).then_inc(turned_out, 1)
                dve.wait_ge(turned, 2)
                nc.vector.tensor_copy(kT[:], misc[:, 1, :]).then_inc(turned_out, 1)
                dve.wait_ge(h_full, 1)
                nc.vector.tensor_copy(h[:, 0:S], misc[:, 0, :]).then_inc(h_out, 1)
                nc.vector.tensor_copy(h[:, S:2 * S], misc[:, 0, :]).then_inc(h_out, 1)
                chain.link(nc.vector.memset(corr[:], PAD))
                dve.wait_ge(corr_full, 1)
                chain.link(nc.vector.tensor_scalar(corr[:, 0:S], misc[0:1, 1, :], 1.0 / NCOL, None, ALU.mult))
                chain.link(nc.vector.max(top[:, 0:8], corr[:, 0:S]))
                nc.vector.tensor_scalar(ntop[:], top[:, 0:1], -1.0, None, ALU.mult).then_inc(ntop_ready, 1)
                chain.link(nc.vector.match_replace(left[:], top[:, 0:8], corr[:], TAKEN))
                chain.link(nc.vector.max(top[:, 8:16], left[:, 0:S]))
                chain.link(nc.vector.memset(top[:, TOP:16], PAD))
                chain.link(nc.vector.match_replace(left2[:], top[:, 8:16], left[:], TAKEN))
                chain.link(nc.vector.tensor_scalar(left[:, 0:S], left2[:, 0:S], TAKEN, None, ALU.is_equal))
                dve.wait_ge(weight_ready, 1)
                chain.link(nc.vector.tensor_tensor(weight[:], weight[:], left[:, 0:S], ALU.mult))
                chain.link(nc.vector.tensor_reduce(wsum[:], weight[:], AX.X, ALU.add))
                chain.link(nc.vector.reciprocal(wr[:], wsum[:]))
                for n in range(3):
                    nc.vector.tensor_scalar(c3[:, n, :], weight[:], wr[:], None, ALU.mult).then_inc(c_ready, 1)
                dve.wait_ge(c_back, 16 * TB)
                nc.vector.tensor_copy(circ[:], hankel[:, :, S:0:-1]).then_inc(circ_ready, 1)
                dve.wait_ge(r_full, 1)
                rv = misc[:, 0, :].rearrange("p (h c b d) -> p c b d h", h=2, c=DC, b=B)
                for c in range(DC):
                    for rep in range(4):
                        last = nc.vector.tensor_copy(z[:, c, :, rep * 32:(rep + 1) * 32].rearrange("p b (d h) -> p b d h", h=2),
                                                     rv[:, c])
                    last.then_inc(z_ready, 1)
                for b in range(B):
                    dve.wait_ge(y_full, b + 1)
                    for j in range(TB):
                        last = nc.vector.tensor_tensor(x[:, b * TB + j, :], x[:, b * TB + j, :], proj[:, b % 2, 0:D], ALU.add)
                    last.then_inc(y_free, 1)
                dve.wait_ge(y_free, B)
        s.clear()


def mix_recurrence(nc, ctx, x, ident, mean, rstd, decay_in, w_bc):
    with ExitStack() as own:
        k = Kit(nc, own, "rc_")
        s = Kit(nc, own, "rc_")
        xn = k.sb("xn", [P, 2, TB, D])
        wbc = k.sb("wbc", [P, DC, D])
        decay = k.sb("decay", [P, DC, S])
        decay_col = k.sb("decay_col", [P, DC])
        hid = k.sb("hid", [P, 2, DC, S])
        tp = k.ps("tp", [P, 2, DC, S])
        outp = k.ps("outp", [P, 4, S])
        loaded, decay_ready = s.sem("loaded"), s.sem("decay_ready")
        xn_ready, tp_full, tp_free = s.sem("xn_ready"), s.sem("tp_full"), s.sem("tp_free")
        out_full, out_free = s.sem("out_full"), s.sem("out_free")

        with nc.Block() as block:
            @block.sync
            def _(sp):
                sp.dma_start(wbc[:], w_bc.rearrange("(c p) n -> p c n", p=P)).then_inc(loaded, 16)
                sp.dma_start(decay_col[:], decay_in.rearrange("(c p) -> p c", p=P),
                             allow_slow_non_contiguous=True).then_inc(loaded, 16)

            @block.tensor
            def _(pe):
                pe.wait_ge(loaded, 32)
                with pe.Fori(0, TURNS) as i:
                    for sl in range(2):
                        b = i * 2 + sl
                        pe.wait_ge(xn_ready, b * TB + TB)
                        pe.wait_ge(tp_free, b + 1)
                        for c in range(DC):
                            for j in range(TB):
                                last = nc.tensor.transpose(tp[:, sl, c, j * P:(j + 1) * P],
                                                           xn[:, sl, j, c * P:(c + 1) * P], ident[:])
                        last.then_inc(tp_full, 1)
                    for sl in range(2):
                        b = i * 2 + sl
                        pe.wait_ge(tp_free, b + 1 + 2)
                        pe.wait_ge(out_free, b + 1)
                        for j in range(TB):
                            for c in range(DC):
                                last = nc.tensor.matmul(outp[:, 2 * sl + j // 2, (j % 2) * D:(j % 2 + 1) * D],
                                                        hid[:, sl, c, j * P:(j + 1) * P], wbc[:, c, :],
                                                        start=(c == 0), stop=(c == DC - 1))
                        last.then_inc(out_full, 1)

            @block.vector
            def _(dve):
                dve.sem_inc(tp_free, 2)
                dve.sem_inc(out_free, 2)
                dve.wait_ge(loaded, 32)
                nc.vector.memset(decay[:], 0.0).then_inc(decay_ready, 1)
                dve.wait_ge(decay_ready, 1)
                for c in range(DC):
                    nc.vector.tensor_scalar(decay[:, c, :], decay[:, c, :], decay_col[:, c:c + 1], None, ALU.add)\
                        .then_inc(decay_ready, 1)
                dve.wait_ge(decay_ready, 3)
                with dve.Fori(0, TURNS) as i:
                    for sl in range(2):
                        b = i * 2 + sl
                        dve.wait_ge(out_free, b + 1)
                        for j in range(TB):
                            t = b * TB + j
                            nc.vector.tensor_scalar(xn[:, sl, j, :], x[:, t, :], mean[:, bass.ds(t, 1)], rstd[:, bass.ds(t, 1)],
                                                    ALU.subtract, ALU.mult).then_inc(xn_ready, 1)
                    for sl in range(2):
                        b = i * 2 + sl
                        dve.wait_ge(tp_full, b + 1)
                        for c in range(DC):
                            last = nc.vector.tensor_tensor_scan(hid[:, sl, c, :], decay[:, c, :], tp[:, sl, c, :], 0.0,
                                                                ALU.mult, ALU.add)
                        last.then_inc(tp_free, 1)
                    for sl in range(2):
                        b = i * 2 + sl
                        dve.wait_ge(out_full, b + 1)
                        for m in range(2):
                            o = x[:, bass.ds(b * TB + 2 * m, 2), :].rearrange("p j n -> p (j n)")
                            last = nc.vector.tensor_tensor(o, o, outp[:, 2 * sl + m, :], ALU.add)
                        last.then_inc(out_free, 1)
                dve.wait_ge(out_free, B + 2)
        s.clear()


class Batch:

    def __init__(self, b, slot, earlier, first=False, last=False):
        self.b, self.slot, self.earlier, self.first, self.last = b, slot, earlier, first, last


def all_batches(eng, one):
    one(Batch(0, 0, 0, first=True), Batch(1, 1, 0))
    with eng.Fori(0, TURNS - 1) as i:
        one(Batch(i * 2 + 1, 1, i), Batch(i * 2 + 2, 0, i + 1))
        one(Batch(i * 2 + 2, 0, i + 1), Batch(i * 2 + 3, 1, i + 1))
    one(Batch(B - 1, 1, TURNS - 1, last=True), None)


def mix_heads(nc, ctx, x, ident, ident_bf, mean, rstd, ctx_in, mask_in, w_vT, w_kT, w_qT, w_oT, b_o, parts_dram, mask_dram):
    with ExitStack() as own:
        k = Kit(nc, own, "hd_")
        s = Kit(nc, own, "hd_")
        H, DH = 16, 16
        GH = 4
        NG = H // GH
        Q_PARTS, K_PARTS = (0, 0, 0, 1, 1, 2), (0, 1, 2, 0, 1, 0)
        NPAIR = len(Q_PARTS)
        MASK_ROW = NPAIR * DH
        FIRST_ROWS, ROWS = MASK_ROW + 1, MASK_ROW + 4
        MASKED = -1e20
        NUNIT = GH * TB
        NRING = 8
        xn = k.sb("xn", [P, TB, D])
        cx = k.sb("cx", [P, 2, TB, D])
        xT = k.sb("xT", [P, DC, S])
        cT = k.sb("cT", [P, DC, S])
        wk = k.sb("wk", [P, P])
        wq = k.sb("wq", [P, P])
        wv = k.sb("wv", [P, P])
        wo = k.sb("wo", [P, DC, D])
        bo = k.sb("bo", [1, D])
        ones = k.sb("ones", [1, P])
        parts = k.sb("parts", [P, 2, 3, DC, S], BF16)
        rest = k.sb("rest", [P, 2, DC, S])
        k_stack = k.sb("k_stack", [ROWS, 2, H, S], BF16)
        q_stack = k.sb("q_stack", [ROWS, 2, H, S], BF16)
        mask = k.sb("mask", [B, S], I32)
        zero = k.sb("zero", [P, 1])
        mask_bf = k.sb("mask_bf", [B, S], BF16)
        v = k.sb("v", [P, 2, TB, H, 2 * DH])
        nmax = k.sb("nmax", [P, 2, GH, TB])
        nrest = k.sb("nrest", [P, GH, TB])
        nparts = k.sb("nparts", [P, 2, P // (GH * TB), GH * TB], BF16)
        nrows = k.sb("nrows", [3 * GH * TB, 2, P], BF16)
        prob = k.sb("prob", [P, NRING, S])
        oT = k.sb("oT", [P, S])
        rsum = k.sb("rsum", [P, TB, GH])
        o = k.sb("o", [P, 2, TB, D])
        oT2 = k.sb("oT2", [P, DC, S])
        first = k.ps("first", [P, 2, 2, S])
        second = k.ps("second", [P, 2, S])
        pv = k.ps("pv", [P, S])
        misc = k.ps("misc", [P, S])
        zeroed, loaded = s.sem("zeroed"), s.sem("loaded")
        ctx_loaded = [s.sem("ctx_loaded0"), s.sem("ctx_loaded1")]
        xn_ready, first_full, turned_ready, v_ready = s.sem("xn_ready"), s.sem("first_full"), s.sem("turned_ready"), s.sem("v_ready")
        part0_ready, rest_ready, part1_ready, parts_ready = s.sem("part0_ready"), s.sem("rest_ready"), s.sem("part1_ready"), s.sem("parts_ready")
        parts_stored, stack_loaded, mask_ready = s.sem("parts_stored"), s.sem("stack_loaded"), s.sem("mask_ready")
        nmax_ready, nstep, nparts_ready = s.sem("nmax_ready"), s.sem("nstep"), s.sem("nparts_ready")
        nrows_ready, nrows_loaded = s.sem("nrows_ready"), [s.sem("nrows_loaded0"), s.sem("nrows_loaded1")]
        second_full, second_free = s.sem("second_full"), s.sem("second_free")
        pv_done, pv_free, misc_full, misc_free = s.sem("pv_done"), s.sem("pv_free"), s.sem("misc_full"), s.sem("misc_free")
        rsum_ready, mask_stored = s.sem("rsum_ready"), s.sem("mask_stored")
        NLOAD = 2 * NPAIR + 1
        NPREP, NSTEP = 5, GH * TB // 2
        LEAD = NSTEP // 2
        ctx_tok = ctx_in.rearrange("b (j p) d -> b p j d", p=P)

        BEFORE = [("prep", 0, n) for n in range(NPREP)] + [("energy", 0, n // NSTEP, n % NSTEP) for n in range(NSTEP + LEAD)]
        PREP_AT = (0, 1, 3, 5, 7)

        def ahead(g, n):
            m = (g + 1) * NSTEP + n + LEAD
            return ("energy", m // (NG * NSTEP), m // NSTEP % NG, m % NSTEP)

        def schedule(last):
            items = []
            for g in range(NG):
                for n in range(NSTEP):
                    items.append(ahead(g, n))
                    if g == 0 and n in PREP_AT:
                        items.append(("prep", 1, PREP_AT.index(n)))
            return [item for item in items if not (last and item[1])]

        PER_BATCH = len(schedule(False))

        def use(bt, item):
            return len(BEFORE) + PER_BATCH * bt.b + schedule(bt.last).index(item)

        def pair(bt, item):
            return (len(BEFORE) + PER_BATCH * bt.slot + schedule(bt.last).index(item)) % 2

        def freed(eng, bt, item):
            items = BEFORE[-2:] + schedule(bt.last)
            read(eng, bt, items[items.index(item, 2) - 2])

        def read(eng, bt, item):
            b, n = bt.b + item[1], item[-1]
            if item[0] == "energy":
                eng.wait_ge(nmax_ready, (b * NG + item[2]) * NSTEP + n + 1)
            elif n < 2:
                eng.wait_ge(turned_ready, b * 2 + n + 1)
            elif n < 4:
                eng.wait_ge(rest_ready, b * 2 + n - 2 + 1)
            else:
                eng.wait_ge(v_ready, b + 1)

        NFIN, TURN_AT, ROWS_AT = 4, 2, 5

        def misc_schedule(first, last):
            items = []
            for g in range(NG):
                if not (first and g == 0):
                    items.append(("turn", g))
                if not (last and g == NG - 1):
                    items.append(("rows", g))
                if g in (1, 2) and not first:
                    items += [("fin", 2 * g - 2), ("fin", 2 * g - 1)]
            return items

        def use_misc(bt, what, n):
            base = 1 if bt.first else 1 + len(misc_schedule(True, False)) + len(misc_schedule(False, False)) * (bt.b - 1)
            return base + misc_schedule(bt.first, bt.last).index((what, n))

        MISC_END = 1 + len(misc_schedule(True, False)) + len(misc_schedule(False, False)) * (B - 2) + len(misc_schedule(False, True))

        def wait(eng, sem, n):
            if not isinstance(n, int) or n > 0:
                eng.wait_ge(sem, n)

        with nc.Block() as block:
            @block.sync
            def _(sp):
                sp.wait_ge(zeroed, 3)
                for dst, src in ((wk, w_kT), (wq, w_qT), (wv, w_vT)):
                    for a in range(P // DH):
                        sp.dma_start(dst[a * DH:(a + 1) * DH, a * DH:(a + 1) * DH], src[:, :],
                                     allow_slow_non_contiguous=True).then_inc(loaded, 16)
                sp.dma_start(mask[:], mask_in.rearrange("b x y s -> (b x y) s")).then_inc(loaded, 16)
                sp.dma_start(wo[:], w_oT.rearrange("(c p) n -> p c n", p=P)).then_inc(loaded, 16)
                sp.dma_start(bo[:], b_o.rearrange("(a n) -> a n", a=1)).then_inc(loaded, 16)

                def load_ctx(b, slot):
                    sp.dma_start(cx[:, slot, :, :], ctx_tok[bass.ds(b, 1), :, :, :].rearrange("a p j d -> p (a j) d"))\
                        .then_inc(ctx_loaded[slot], 16)

                def stacks(b, slot):
                    wait(sp, stack_loaded, b * NLOAD * 16)
                    sp.wait_ge(parts_ready, b * 2 + 2)
                    sp.dma_start(parts_dram.rearrange("a n (c p) s -> p (a n c) s", p=P),
                                 parts[:].rearrange("p a n c s -> p (a n c) s")).then_inc(parts_stored, 16)
                    sp.wait_ge(parts_stored, b * 16 + 16)
                    for a, (stack, which) in enumerate(((k_stack, K_PARTS), (q_stack, Q_PARTS))):
                        for n, part in enumerate(which):
                            sp.dma_start(stack[n * DH:(n + 1) * DH, slot, :, :],
                                         parts_dram[a, part].rearrange("(h e) s -> e h s", e=DH)).then_inc(stack_loaded, 16)
                    sp.dma_start(k_stack[MASK_ROW:MASK_ROW + 1, slot, :, :],
                                 mask_dram[bass.ds(b, 1), :].rearrange("p (a s) -> p a s", a=1).to_broadcast([1, H, S]))\
                        .then_inc(stack_loaded, 16)

                def max_rows(bt, g):
                    wait(sp, nrows_ready, bt.b * NG + g + 1)
                    sp.dma_start(q_stack[MASK_ROW + 1:ROWS, bt.slot, g * GH:(g + 1) * GH, :]
                                 .rearrange("a h (c p) -> a (h c) p", p=P),
                                 nrows[:, g % 2, :]).then_inc(nrows_loaded[g % 2], 16)

                load_ctx(0, 0)
                sp.wait_ge(zeroed, 7)
                sp.wait_ge(mask_ready, 1)
                sp.dma_start(mask_dram[:, :], mask_bf[:]).then_inc(mask_stored, 16)
                sp.wait_ge(mask_stored, 16)
                stacks(0, 0)
                max_rows(Batch(0, 0, 0), 0)

                def batch(bt, nxt):
                    if nxt is not None:
                        load_ctx(nxt.b, nxt.slot)
                    for g in range(NG):
                        if g < NG - 1:
                            max_rows(bt, g + 1)
                        if g == 0 and nxt is not None:
                            stacks(nxt.b, nxt.slot)
                        if g == NG - 1 and nxt is not None:
                            max_rows(nxt, 0)

                all_batches(sp, batch)
                for sem in nrows_loaded:
                    sp.wait_ge(sem, 16 * B * NG // 2)
                sp.wait_ge(stack_loaded, 16 * NLOAD * B)

            @block.gpsimd
            def _(pool):
                for n, (t, value) in enumerate(((wk[:], 0.0), (wq[:], 0.0), (wv[:], 0.0), (k_stack[MASK_ROW:ROWS], 1.0),
                                                (q_stack[MASK_ROW:FIRST_ROWS], 1.0), (nparts[:], 0.0), (zero[:], 0.0))):
                    if n:
                        pool.wait_ge(zeroed, n)
                    nc.gpsimd.memset(t, value).then_inc(zeroed, 1)
                pool.wait_ge(zeroed, 7)

                def split(bt):
                    for a in range(2):
                        pool.wait_ge(rest_ready, bt.b * 2 + a + 1)
                        wait(pool, parts_stored, bt.b * 16)
                        nc.gpsimd.tensor_tensor(parts[:, a, 1], rest[:, a], zero[:].unsqueeze(2).to_broadcast([P, DC, S]), ALU.add).then_inc(part1_ready, 1)
                        pool.wait_ge(part1_ready, bt.b * 2 + a + 1)
                        nc.gpsimd.tensor_tensor(parts[:, a, 2], rest[:, a], parts[:, a, 1], ALU.subtract).then_inc(parts_ready, 1)

                def split_max(bt, g):
                    m, p = nmax[:, g % 2], nparts[:, g % 2].rearrange("p n (h c) -> p n h c", h=GH)
                    at = (bt.b * NG + g) * 3
                    z = zero[:].unsqueeze(2).to_broadcast([P, GH, TB])
                    pool.wait_ge(nmax_ready, (bt.b * NG + g) * NSTEP + NSTEP)
                    nc.gpsimd.tensor_tensor(p[:, 0], m, z, ALU.add).then_inc(nstep, 1)
                    pool.wait_ge(nstep, at + 1)
                    nc.gpsimd.tensor_tensor(nrest[:], m, p[:, 0], ALU.subtract).then_inc(nstep, 1)
                    pool.wait_ge(nstep, at + 2)
                    nc.gpsimd.tensor_tensor(p[:, 1], nrest[:], z, ALU.add).then_inc(nstep, 1)
                    pool.wait_ge(nstep, at + 3)
                    nc.gpsimd.tensor_tensor(p[:, 2], nrest[:], p[:, 1], ALU.subtract).then_inc(nparts_ready, 1)

                def batch(bt, nxt):
                    for g in range(NG):
                        if g < NG - 1:
                            split_max(bt, g + 1)
                        elif nxt is not None:
                            split_max(nxt, 0)
                        if g == 0 and nxt is not None:
                            split(nxt)

                split(Batch(0, 0, 0))
                split_max(Batch(0, 0, 0), 0)
                all_batches(pool, batch)

            @block.tensor
            def _(pe):
                def prep(nxt, n, bank):
                    if n == 0:
                        pe.wait_ge(ctx_loaded[nxt.slot], nxt.earlier * 16 + 16)
                        pe.wait_ge(xn_ready, nxt.b * TB + TB)
                    if n < 2:
                        for c in range(DC):
                            for j in range(TB):
                                cols = slice(c * P, (c + 1) * P)
                                src = xn[:, j, cols] if n else cx[:, nxt.slot, j, cols]
                                last = nc.tensor.transpose(first[:, bank, c, j * P:(j + 1) * P], src, ident[:])
                    elif n < 4:
                        pe.wait_ge(turned_ready, nxt.b * 2 + n - 2 + 1)
                        w, src = ((wk, cT), (wq, xT))[n - 2]
                        for c in range(DC):
                            last = nc.tensor.matmul(first[:, bank, c, :], w[:], src[:, c, :], start=True, stop=True)
                    else:
                        for j in range(TB):
                            for c in range(DC):
                                at = (j % 2) * D + c * P
                                last = nc.tensor.matmul(first[:, bank, j // 2, at:at + P], cT[:, c, j * P:(j + 1) * P], wv[:],
                                                        start=True, stop=True)
                    last.then_inc(first_full, 1)

                def first_energies(bt, g, n, bank):
                    h = g * GH + n // 2
                    if g == 0 and n == 0:
                        pe.wait_ge(stack_loaded, (bt.b + 1) * NLOAD * 16)
                    for j in range(2):
                        qc = (n % 2) * 2 + j
                        last = nc.tensor.matmul(first[:, bank, j, :], q_stack[0:FIRST_ROWS, bt.slot, h, qc * P:(qc + 1) * P],
                                                k_stack[0:FIRST_ROWS, bt.slot, h, :], start=True, stop=True)
                    last.then_inc(first_full, 1)

                def second_energies(bt, g, u):
                    kc, h = u // GH, g * GH + u % GH
                    if u == 0:
                        pe.wait_ge(nrows_loaded[g % 2], (bt.b * (NG // 2) + g // 2 + 1) * 16)
                    pe.wait_ge(second_free, (bt.b * NG + g) * NUNIT + u + 1)
                    nc.tensor.matmul(second[:, u % 2, :], k_stack[:, bt.slot, h, kc * P:(kc + 1) * P], q_stack[:, bt.slot, h, :],
                                     start=True, stop=True).then_inc(second_full, 1)

                def values(bt, g, kc):
                    at = bt.b * NG + g
                    pe.wait_ge(second_free, at * NUNIT + (kc + 1) * GH + 2)
                    if kc == 0:
                        pe.wait_ge(pv_free, at + 1)
                    for j in range(GH):
                        last = nc.tensor.matmul(pv[32 * j:32 * j + 32, :], v[:, bt.slot, kc, g * GH + j, :],
                                                prob[:, (kc * GH + j) % NRING, :], start=(kc == 0), stop=(kc == TB - 1),
                                                skip_group_check=True)
                    last.then_inc(pv_done, 1)

                def rows(bt, g, uses):
                    pe.wait_ge(nparts_ready, bt.b * NG + g + 1)
                    pe.wait_ge(misc_free, uses + 1)
                    nc.tensor.transpose(misc[:, 0:P // 2].bitcast(BF16), nparts[:, g % 2].rearrange("p n m -> p (n m)"),
                                        ident_bf[:]).then_inc(misc_full, 1)

                def turn(groups, uses):
                    pe.wait_ge(pv_free, groups + 1)
                    pe.wait_ge(misc_free, uses + 1)
                    for qc in range(TB):
                        last = nc.tensor.transpose(misc[:, qc * P:(qc + 1) * P], oT[:, qc * P:(qc + 1) * P], ident[:])
                    last.then_inc(misc_full, 1)

                def finish(slot, n, uses):
                    pe.wait_ge(misc_free, uses + 1)
                    if n < 2:
                        for qc in range(TB):
                            last = nc.tensor.transpose(misc[:, qc * P:(qc + 1) * P], o[:, slot, qc, n * P:(n + 1) * P], ident[:])
                    else:
                        for j in range(2):
                            qc, out = 2 * (n - 2) + j, misc[:, j * D:(j + 1) * D]
                            for c in range(DC):
                                nc.tensor.matmul(out, oT2[:, c, qc * P:(qc + 1) * P], wo[:, c, :], start=(c == 0), stop=False)
                            last = nc.tensor.matmul(out, ones[:], bo[:], start=False, stop=True)
                    last.then_inc(misc_full, 1)

                def group(bt, nxt, g):
                    for n in range(NSTEP):
                        item = ahead(g, n)
                        fbt = nxt if item[1] else bt
                        if fbt is not None:
                            freed(pe, bt, item)
                            first_energies(fbt, item[2], n=item[3], bank=pair(bt, item))
                        second_energies(bt, g, 2 * n)
                        second_energies(bt, g, 2 * n + 1)
                        if g == 0 and n in PREP_AT and nxt is not None:
                            item = ("prep", 1, PREP_AT.index(n))
                            freed(pe, bt, item)
                            prep(nxt, item[2], pair(bt, item))
                        if n == TURN_AT and not (bt.first and g == 0):
                            turn(bt.b * NG + g, use_misc(bt, "turn", g))
                        if n == ROWS_AT and not (bt.last and g == NG - 1):
                            rows(*((bt, g + 1) if g < NG - 1 else (nxt, 0)), use_misc(bt, "rows", g))
                        if g in (1, 2) and n > ROWS_AT and not bt.first:
                            step = 2 * (g - 1) + n - ROWS_AT - 1
                            finish(1 - bt.slot, step, use_misc(bt, "fin", step))
                        if n >= 3 and n % 2 == 1:
                            values(bt, g, (n - 3) // 2)
                    values(bt, g, TB - 1)

                def batch(bt, nxt):
                    for g in range(NG):
                        group(bt, nxt, g)

                pe.wait_ge(loaded, (3 * (P // DH) + 3) * 16)
                b0 = Batch(0, 0, 0, first=True)
                for at, item in enumerate(BEFORE):
                    if at >= 2:
                        read(pe, b0, BEFORE[at - 2])
                    if item[0] == "prep":
                        prep(b0, item[2], at % 2)
                    else:
                        first_energies(b0, item[2], item[3], at % 2)
                rows(b0, 0, 0)
                all_batches(pe, batch)
                turn(B * NG, MISC_END)
                for n in range(NFIN):
                    finish(1, n, MISC_END + 1 + n)

            @block.scalar
            def _(act):
                act.sem_inc(second_free, 2)
                act.sem_inc(pv_free, 1)

                def copy_out(groups):
                    act.wait_ge(pv_done, groups * TB + 2)
                    nc.scalar.activation(oT[:], pv[:], ACT.Copy).then_inc(pv_free, 1)

                def prep(nxt, n, uses, bank):
                    act.wait_ge(first_full, uses + 1)
                    nc.scalar.activation((cT, xT)[n][:], first[:, bank], ACT.Copy).then_inc(turned_ready, 1)

                def batch(bt, nxt):
                    for g in range(NG):
                        at = bt.b * NG + g
                        for u in range(NUNIT):
                            if u % GH == 0:
                                act.wait_ge(pv_done, at * TB + u // GH + 1)
                            act.wait_ge(second_full, at * NUNIT + u + 1)
                            nc.scalar.activation(prob[:, u % NRING, :], second[:, u % 2, :], ACT.Exp, scale=D ** -0.5)\
                                .then_inc(second_free, 1)
                            if u == 1 and not (bt.first and g == 0):
                                copy_out(at)
                            if nxt is not None and g == 0 and u % 2 == 1 and u // 2 in PREP_AT[:2]:
                                item = ("prep", 1, PREP_AT.index(u // 2))
                                prep(nxt, item[2], use(bt, item), pair(bt, item))

                for n in range(2):
                    prep(Batch(0, 0, 0), n, n, n)
                all_batches(act, batch)
                copy_out(B * NG)

            @block.vector
            def _(dve):
                dve.sem_inc(misc_free, 1)
                dve.sem_inc(pv_done, 2)
                nc.vector.memset(ones[:], 1.0)
                nc.vector.memset(v[:], 0.0).then_inc(rsum_ready, 1)
                dve.wait_ge(rsum_ready, 1)
                nc.vector.memset(v[:, :, :, :, DH:DH + 1].rearrange("p a j h n -> p (a j h) n"), 1.0)
                dve.wait_ge(loaded, (3 * (P // DH) + 3) * 16)
                nc.vector.tensor_scalar(mask_bf[:], mask[:], 0.0, MASKED, ALU.is_equal, ALU.mult).then_inc(mask_ready, 1)

                def normed(bt):
                    for j in range(TB):
                        t = bt.b * TB + j
                        nc.vector.tensor_scalar(xn[:, j, :], x[:, t, :], mean[:, bass.ds(t, 1)], rstd[:, bass.ds(t, 1)],
                                                ALU.subtract, ALU.mult).then_inc(xn_ready, 1)

                def prep(nxt, n, uses, bank):
                    dve.wait_ge(first_full, uses + 1)
                    if n < 4:
                        a = n - 2
                        wait(dve, parts_stored, nxt.b * 16)
                        nc.vector.tensor_copy(parts[:, a, 0], first[:, bank]).then_inc(part0_ready, 1)
                        dve.wait_ge(part0_ready, nxt.b * 2 + a + 1)
                        nc.vector.tensor_tensor(rest[:, a], first[:, bank], parts[:, a, 0], ALU.subtract).then_inc(rest_ready, 1)
                    else:
                        nc.vector.tensor_copy(v[:, nxt.slot, :, :, 0:DH].rearrange("p j h e -> p (j h) e"),
                                              first[:, bank].rearrange("p a (m e) -> p (a m) e", e=DH)).then_inc(v_ready, 1)

                def maxima(g, n, uses, bank):
                    dve.wait_ge(first_full, uses + 1)
                    c = (n % 2) * 2
                    nc.vector.tensor_reduce(nmax[:, g % 2, n // 2, c:c + 2], first[:, bank], AX.X, ALU.max, negate=True)\
                        .then_inc(nmax_ready, 1)

                def rows(bt, g, uses):
                    dve.wait_ge(misc_full, uses + 1)
                    wait(dve, nrows_loaded[g % 2], (bt.b * (NG // 2) + g // 2) * 16)
                    nc.vector.tensor_copy(nrows[:, g % 2, :], misc[0:3 * GH * TB, 0:P // 2].bitcast(BF16))\
                        .then_inc(nrows_ready, 1)
                    dve.wait_ge(nrows_ready, bt.b * NG + g + 1)
                    dve.sem_inc(misc_free, 1)

                def turn(groups, slot, g, uses):
                    m = misc[:].rearrange("p (c h n) -> p c h n", c=TB, n=2 * DH)
                    dve.wait_ge(misc_full, uses + 1)
                    nc.vector.reciprocal(rsum[:], m[:, :, :, DH]).then_inc(rsum_ready, 1)
                    dve.wait_ge(rsum_ready, groups + 1)
                    nc.vector.tensor_tensor(o[:, slot, :, g * GH * DH:(g + 1) * GH * DH].rearrange("p c (h e) -> p c h e", e=DH),
                                            m[:, :, :, 0:DH], rsum[:].unsqueeze(3).to_broadcast([P, TB, GH, DH]), ALU.mult)\
                        .then_inc(misc_free, 1)

                def finish(b, n, uses):
                    dve.wait_ge(misc_full, uses + 1)
                    if n < 2:
                        nc.vector.tensor_copy(oT2[:, n, :], misc[:]).then_inc(misc_free, 1)
                    else:
                        xs = x[:, bass.ds(b * TB + 2 * (n - 2), 2), :].rearrange("p j n -> p (j n)")
                        nc.vector.tensor_tensor(xs, xs, misc[:], ALU.add).then_inc(misc_free, 1)

                def batch(bt, nxt):
                    for g in range(NG):
                        if g == 0 and nxt is not None:
                            normed(nxt)
                        for n in range(NSTEP):
                            item = ahead(g, n)
                            if not (bt.last and item[1]):
                                maxima(item[2], item[3], use(bt, item), pair(bt, item))
                            if g == 0 and n in PREP_AT[2:] and nxt is not None:
                                item = ("prep", 1, PREP_AT.index(n))
                                prep(nxt, item[2], use(bt, item), pair(bt, item))
                            if n == TURN_AT and not (bt.first and g == 0):
                                turn(bt.b * NG + g, bt.slot if g else 1 - bt.slot, (g - 1) % NG, use_misc(bt, "turn", g))
                            if n == ROWS_AT and not (bt.last and g == NG - 1):
                                rows(*((bt, g + 1) if g < NG - 1 else (nxt, 0)), use_misc(bt, "rows", g))
                            if g in (1, 2) and n > ROWS_AT and not bt.first:
                                step = 2 * (g - 1) + n - ROWS_AT - 1
                                finish(bt.b - 1, step, use_misc(bt, "fin", step))

                b0 = Batch(0, 0, 0, first=True)
                normed(b0)
                for at, item in enumerate(BEFORE):
                    if item[0] == "energy":
                        maxima(item[2], item[3], at, at % 2)
                    elif item[2] >= 2:
                        prep(b0, item[2], at, at % 2)
                rows(b0, 0, 0)
                all_batches(dve, batch)
                turn(B * NG, 1, NG - 1, MISC_END)
                for n in range(NFIN):
                    finish(B - 1, n, MISC_END + 1 + n)
                dve.wait_ge(misc_free, 1 + MISC_END + 1 + NFIN)
        s.clear()


def normed_and_logits(nc, ctx, name, x, ident, mean, rstd, w_gate, n_exp, xnT, logits, rows=None):
    with ExitStack() as own:
        k = Kit(nc, own, name + "_nl_")
        s = Kit(nc, own, name + "_nl_")
        xn = k.sb("xn", [P, 2, TB, D])
        wg = k.sb("wg", [P, DC, n_exp])
        lgT = k.sb("lgT", [P, 2, S])
        tp = k.ps("tp", [P, 2, DC, S])
        lp = k.ps("lp", [n_exp, 2, S])
        lt = k.ps("lt", [P, 2, S])
        loaded, xn_ready, xn_free = s.sem("loaded"), s.sem("xn_ready"), s.sem("xn_free")
        tp_full, tp_free, lp_full, lp_free = s.sem("tp_full"), s.sem("tp_free"), s.sem("lp_full"), s.sem("lp_free")
        lt_full, lt_free, stored = s.sem("lt_full"), s.sem("lt_free"), [s.sem("stored0"), s.sem("stored1")]

        with nc.Block() as block:
            @block.sync
            def _(sp):
                sp.dma_start(wg[:], w_gate.rearrange("(c p) n -> p c n", p=P)).then_inc(loaded, 16)
                if rows is not None:
                    for sem in stored:
                        sp.sem_inc(sem, 16)
                    with sp.Fori(0, TURNS) as i:
                        for sl in range(2):
                            b = i * 2 + sl
                            sp.wait_ge(xn_ready, b * TB + TB)
                            sp.dma_start(rows[bass.ds(b * S, S), 0:D].rearrange("(j p) d -> p j d", p=P), xn[:, sl])\
                                .then_inc(stored[sl], 16)
                    for sem in stored:
                        sp.wait_ge(sem, 16 * TURNS + 16)

            @block.tensor
            def _(pe):
                pe.sem_inc(xn_free, 2)
                pe.wait_ge(loaded, 16)
                with pe.Fori(0, TURNS) as i:
                    for sl in range(2):
                        b = i * 2 + sl
                        pe.wait_ge(xn_ready, b * TB + TB)
                        pe.wait_ge(tp_free, b + 1)
                        for c in range(DC):
                            for j in range(TB):
                                last = nc.tensor.transpose(tp[:, sl, c, j * P:(j + 1) * P],
                                                           xn[:, sl, j, c * P:(c + 1) * P], ident[:])
                        last.then_inc(tp_full, 1)
                        pe.wait_ge(tp_full, b + 1)
                        pe.sem_inc(xn_free, 1)
                    for sl in range(2):
                        b = i * 2 + sl
                        pe.wait_ge(tp_free, b + 1 + 2)
                        pe.wait_ge(lp_free, b + 1)
                        for c in range(DC):
                            last = nc.tensor.matmul(lp[:, sl, :], wg[:, c, :], xnT[:, c, bass.ds(b * S, S)],
                                                    start=(c == 0), stop=(c == DC - 1))
                        last.then_inc(lp_full, 1)
                    for sl in range(2):
                        b = i * 2 + sl
                        pe.wait_ge(lp_free, b + 1 + 2)
                        pe.wait_ge(lt_free, b + 1)
                        for j in range(TB):
                            last = nc.tensor.transpose(lt[:, sl, j * P:(j + 1) * P], lgT[:, sl, j * P:(j + 1) * P], ident[:])
                        last.then_inc(lt_full, 1)

            @block.scalar
            def _(act):
                act.sem_inc(tp_free, 2)
                with act.Fori(0, TURNS) as i:
                    for sl in range(2):
                        b = i * 2 + sl
                        act.wait_ge(tp_full, b + 1)
                        nc.scalar.activation(xnT[:, :, bass.ds(b * S, S)], tp[:, sl], ACT.Copy).then_inc(tp_free, 1)

            @block.vector
            def _(dve):
                nc.vector.memset(lgT[:], 0.0).then_inc(lp_free, 2)
                dve.wait_ge(lp_free, 2)
                dve.sem_inc(lt_free, 2)
                with dve.Fori(0, TURNS) as i:
                    for sl in range(2):
                        b = i * 2 + sl
                        dve.wait_ge(xn_free, b + 1)
                        if rows is not None:
                            dve.wait_ge(stored[sl], i * 16 + 16)
                        for j in range(TB):
                            t = b * TB + j
                            nc.vector.tensor_scalar(xn[:, sl, j, :], x[:, t, :], mean[:, bass.ds(t, 1)], rstd[:, bass.ds(t, 1)],
                                                    ALU.subtract, ALU.mult).then_inc(xn_ready, 1)
                    for sl in range(2):
                        b = i * 2 + sl
                        dve.wait_ge(lp_full, b + 1)
                        nc.vector.tensor_copy(lgT[0:n_exp, sl, :], lp[:, sl, :]).then_inc(lp_free, 1)
                    for sl in range(2):
                        b = i * 2 + sl
                        dve.wait_ge(lt_full, b + 1)
                        nc.vector.tensor_copy(logits[:, bass.ds(b * TB, TB), :],
                                              lt[:, sl, :].rearrange("p (j n) -> p j n", j=TB)[:, :, 0:n_exp]).then_inc(lt_free, 1)
                dve.wait_ge(lt_free, B + 2)
                dve.wait_ge(tp_free, B + 2)
        s.clear()


def softmax_scores(nc, dve, chain, logits, nmax, total, exp_ready, exp_go):
    n = logits.shape[2]
    chain.link(nc.vector.tensor_reduce(nmax[:], logits[:], AX.X, ALU.max))
    nc.vector.tensor_tensor(logits[:], logits[:], nmax[:].unsqueeze(2).to_broadcast([P, NT, n]), ALU.subtract).then_inc(exp_go, 1)
    dve.wait_ge(exp_ready, 1)
    chain.link(nc.vector.tensor_reduce(total[:], logits[:], AX.X, ALU.add))
    chain.link(nc.vector.reciprocal(total[:], total[:]))
    chain.link(nc.vector.tensor_tensor(logits[:], logits[:], total[:].unsqueeze(2).to_broadcast([P, NT, n]), ALU.mult))


def mix_experts_routed(nc, ctx, x, ident, mean, rstd, w_gate, w_in, w_out, places, outputs, scattered, gathered):
    with ExitStack() as own:
        k = Kit(nc, own, "mr_")
        s = Kit(nc, own, "mr_")
        E, TOP, CAP, F = 32, 4, 2048, 128
        T = B * S
        NS = w_in.shape[0] - E
        TILES = T * TOP // P + E
        UNROLL = 8
        LAG_H, LAG_Y, LAG_S = 1, 3, 4
        xnT = k.sb("xnT", [P, DC, T])
        place = k.sb("place", [P, NT, TOP], I32)
        weight = k.sb("weight", [P, NT, TOP])
        expert_h = k.sb("expert_h", [1, TILES + UNROLL], I32)
        expert_y = k.sb("expert_y", [1, TILES + UNROLL], I32)
        with ExitStack() as own2:
            k2 = Kit(nc, own2, "mr_r_")
            PAD, TAKEN = -2.0, -1.0
            logits = k2.sb("logits", [P, NT, E])
            normed_and_logits(nc, ctx, "mr", x, ident, mean, rstd, w_gate, E, xnT, logits)
            nmax = k2.sb("nmax", [P, NT])
            total = k2.sb("total", [P, NT])
            padded = k2.sb("padded", [P, NT, E + 8])
            left = k2.sb("left", [P, NT, E + 8])
            top = k2.sb("top", [P, NT, 8])
            before = k2.sb("before", [P, NT + 1, E])
            chosen = k2.sb("chosen", [P, NT, E])
            rank = k2.sb("rank", [P, NT, E])
            match = k2.sb("match", [P, NT, E])
            tri = k2.sb("tri", [P, P])
            ones = k2.sb("ones", [P, P])
            steps = k2.sb("steps", [P, CAP // P])
            over = k2.sb("over", [P, E, CAP // P])
            count = k2.sb("count", [P, E])
            tiles = k2.sb("tiles", [P, E])
            ends = k2.sb("ends", [P, E])
            starts = k2.sb("starts", [P, E])
            tile_no = k2.sb("tile_no", [1, TILES + 2 * UNROLL])
            past = k2.sb("past", [1, TILES + 2 * UNROLL, E])
            table = k2.sb("table", [1, TILES + 2 * UNROLL])
            spare = k2.sb("spare", [P, 1])
            place_f = k2.sb("place_f", [P, NT, TOP])
            none = k2.sb("none", [P, NT, TOP])
            ranks = k2.ps("ranks", [P, 2, 512])
            counts = k2.ps("counts", [P, 512])
            exp_go, exp_ready, chained = s.sem("exp_go"), s.sem("exp_ready"), s.sem("chained")
            top_done, tri_ready, sel_ready, rank_full = s.sem("top_done"), s.sem("tri_ready"), s.sem("sel_ready"), s.sem("rank_full")
            with nc.Block() as block:
                @block.gpsimd
                def _(pool):
                    nc.gpsimd.memset(ones[:], 1.0).then_inc(tri_ready, 1)
                    pool.wait_ge(tri_ready, 1)
                    nc.gpsimd.affine_select(out=tri[:], in_=ones[:], compare_op=ALU.is_ge, fill=0.0, base=0,
                                            pattern=[[1, P]], channel_multiplier=-1).then_inc(tri_ready, 1)
                    nc.gpsimd.iota(steps[:], pattern=[[P, CAP // P]], base=0, channel_multiplier=0,
                                   allow_small_or_imprecise_dtypes=True).then_inc(tri_ready, 1)
                    nc.gpsimd.iota(tile_no[:], pattern=[[1, TILES + 2 * UNROLL]], base=-LAG_Y, channel_multiplier=0,
                                   allow_small_or_imprecise_dtypes=True).then_inc(tri_ready, 1)
                    nc.gpsimd.iota(spare[:], pattern=[[0, 1]], base=TILES * P + 1, channel_multiplier=1,
                                   allow_small_or_imprecise_dtypes=True).then_inc(tri_ready, 1)

                @block.scalar
                def _(act):
                    act.wait_ge(exp_go, 1)
                    nc.scalar.activation(logits[:], logits[:], ACT.Exp).then_inc(exp_ready, 1)

                @block.tensor
                def _(pe):
                    pe.wait_ge(tri_ready, 2)
                    pe.wait_ge(sel_ready, 2)
                    nc.tensor.matmul(counts[:, 0:E], ones[:], before[:, NT, :], start=True, stop=True)
                    for t in range(NT):
                        o = ranks[:, t // 16, (t % 16) * E:(t % 16 + 1) * E]
                        nc.tensor.matmul(o, ones[:], before[:, t, :], start=True, stop=False)
                        last = nc.tensor.matmul(o, tri[:], chosen[:, t, :], start=False, stop=True)
                    last.then_inc(rank_full, 1)

                @block.vector
                def _(dve):
                    chain = Chain(dve, chained)
                    chain.tick(nc.vector.memset(padded[:], PAD))
                    chain.tick(nc.vector.memset(before[:, 0, :], 0.0))
                    softmax_scores(nc, dve, chain, logits, nmax, total, exp_ready, exp_go)
                    chain.tick(nc.vector.tensor_copy(padded[:, :, 0:E], logits[:]))
                    for t in range(NT):
                        nc.vector.max(top[:, t, :], logits[:, t, :]).then_inc(top_done, 1)
                    chain.wait()
                    dve.wait_ge(top_done, NT)
                    chain.link(nc.vector.memset(top[:, :, TOP:8], PAD))
                    for t in range(NT):
                        nc.vector.match_replace(left[:, t, :], top[:, t, :], padded[:, t, :], TAKEN).then_inc(top_done, 1)
                    dve.wait_ge(top_done, 2 * NT)
                    chain.link(nc.vector.tensor_scalar(chosen[:], left[:, :, 0:E], TAKEN, None, ALU.is_equal))
                    for t in range(NT):
                        chain.link(nc.vector.tensor_tensor(before[:, t + 1, :], before[:, t, :], chosen[:, t, :], ALU.add))
                    dve.sem_inc(sel_ready, 2)
                    dve.wait_ge(rank_full, 1)
                    dve.wait_ge(tri_ready, 5)
                    chain.link(nc.vector.tensor_scalar(count[:], counts[:, 0:E], float(CAP), None, ALU.min))
                    chain.link(nc.vector.tensor_tensor(over[:], count[:].unsqueeze(2).to_broadcast([P, E, CAP // P]),
                                                       steps[:].unsqueeze(1).to_broadcast([P, E, CAP // P]), ALU.is_gt))
                    chain.link(nc.vector.tensor_reduce(tiles[:], over[:], AX.X, ALU.add))
                    chain.link(nc.vector.tensor_tensor_scan(ends[:], ones[:, 0:E], tiles[:], 0.0, ALU.mult, ALU.add))
                    chain.link(nc.vector.tensor_tensor(starts[:], ends[:], tiles[:], ALU.subtract))
                    chain.link(nc.vector.tensor_scalar(starts[:], starts[:], float(P), None, ALU.mult))
                    chain.link(nc.vector.tensor_copy(rank[:], ranks[:].rearrange("p a (t e) -> p (a t) e", e=E)))
                    chain.link(nc.vector.tensor_scalar(match[:], rank[:], float(CAP), None, ALU.is_le))
                    chain.link(nc.vector.tensor_tensor(chosen[:], chosen[:], match[:], ALU.mult))
                    chain.link(nc.vector.tensor_tensor(rank[:], rank[:], starts[:].unsqueeze(1).to_broadcast([P, NT, E]), ALU.add))
                    chain.link(nc.vector.tensor_tensor(rank[:], rank[:], chosen[:], ALU.mult))
                    chain.link(nc.vector.tensor_tensor(logits[:], logits[:], chosen[:], ALU.mult))
                    for t in range(NT):
                        nc.vector.max(top[:, t, :], rank[:, t, :]).then_inc(top_done, 1)
                    dve.wait_ge(top_done, 3 * NT)
                    chain.link(nc.vector.tensor_scalar(none[:], top[:, :, 0:TOP], 0.0, spare[:], ALU.is_equal, ALU.mult))
                    chain.link(nc.vector.scalar_tensor_tensor(place_f[:], top[:, :, 0:TOP], -1.0, none[:], ALU.add, ALU.add))
                    chain.link(nc.vector.tensor_copy(place[:], place_f[:]))
                    for n in range(TOP):
                        chain.link(nc.vector.tensor_tensor(match[:], rank[:], top[:, :, n:n + 1].to_broadcast([P, NT, E]), ALU.is_equal))
                        chain.link(nc.vector.tensor_tensor(match[:], match[:], logits[:], ALU.mult))
                        chain.link(nc.vector.tensor_reduce(weight[:, :, n], match[:], AX.X, ALU.add))
                    chain.link(nc.vector.tensor_tensor(past[:], tile_no[:].unsqueeze(2).to_broadcast([1, TILES + 2 * UNROLL, E]),
                                                       ends[0:1, :].unsqueeze(1).to_broadcast([1, TILES + 2 * UNROLL, E]), ALU.is_ge))
                    chain.link(nc.vector.tensor_reduce(table[:], past[:], AX.X, ALU.add))
                    chain.link(nc.vector.tensor_scalar(table[:], table[:], float(E - 1), None, ALU.min))
                    chain.tick(nc.vector.tensor_copy(expert_y[:], table[:, 0:TILES + UNROLL]))
                    chain.tick(nc.vector.tensor_copy(expert_h[:], table[:, LAG_Y - LAG_H:LAG_Y - LAG_H + TILES + UNROLL]))
                    chain.wait()

        w1 = k.sb("w1", [P, E, DC, 2 * F])
        w2 = k.sb("w2", [P, E, D])
        w_loaded = s.sem("w_loaded")

        with ExitStack() as own2:
            k2 = Kit(nc, own2, "mr_s_")
            xn = k2.sb("xn", [P, TB, D])
            now = k2.sb("now", [P, TB, TOP], I32)
            sw1 = k2.sb("sw1", [P, NS, DC, 2 * F])
            sw2 = k2.sb("sw2", [P, NS, D])
            act_out = k2.sb("act_out", [P, NS, S])
            hid = k2.sb("hid", [P, NS, S])
            hp = k2.ps("hp", [P, NS, 2, S])
            yp = k2.ps("yp", [P, 2, 2, S])
            loaded, rows_ready, passed = s.sem("sh_loaded"), s.sem("rows_ready"), s.sem("passed")
            h_full, silu_done, h_free = s.sem("sh_h_full"), s.sem("sh_silu_done"), s.sem("sh_h_free")
            y_full, y_free = s.sem("sh_y_full"), s.sem("sh_y_free")
            with nc.Block() as block:
                @block.sync
                def _(sp):
                    for n in range(NS):
                        sp.dma_start(sw1[:, n].rearrange("p c n -> p (c n)"), w_in[E + n]).then_inc(loaded, 16)
                        sp.dma_start(sw2[:, n, :], w_out[E + n]).then_inc(loaded, 16)
                    for n in range(0, E, 8):
                        sp.dma_start(w1[:, n:n + 8].rearrange("p e c n -> p e (c n)"), w_in[n:n + 8].rearrange("e p n -> p e n"))\
                            .then_inc(w_loaded, 16)
                        sp.dma_start(w2[:, n:n + 8, :], w_out[n:n + 8].rearrange("e p n -> p e n")).then_inc(w_loaded, 16)
                    sp.wait_ge(w_loaded, 16 * 2 * (E // 8))

                @block.gpsimd
                def _(pool):
                    with pool.Fori(0, B) as b:
                        for j in range(TB):
                            pool.wait_ge(rows_ready, (b * TB + j) * 2 + 2)
                            pool.sem_inc(passed, 1)
                            for n in range(TOP):
                                nc.gpsimd.indirect_dma_start(out=places[:, :],
                                                             out_offset=bass.IndirectOffsetOnAxis(ap=now[:, j, n:n + 1], axis=0),
                                                             in_=xn[:, j, :], in_offset=None).then_inc(scattered[j], 16)
                    for sem in scattered:
                        pool.wait_ge(sem, 16 * TOP * B)

                @block.tensor
                def _(pe):
                    pe.wait_ge(loaded, 32 * NS)
                    with pe.Fori(0, TURNS) as i:
                        for sl in range(2):
                            b = i * 2 + sl
                            for n in range(NS):
                                pe.wait_ge(h_free, b * NS + n + 1)
                                for half in range(2):
                                    for c in range(DC):
                                        last = nc.tensor.matmul(hp[:, n, half, :], sw1[:, n, c, half * F:(half + 1) * F],
                                                                xnT[:, c, bass.ds(b * S, S)], start=(c == 0), stop=(c == DC - 1))
                                last.then_inc(h_full, 1)
                            pe.wait_ge(h_free, b * NS + NS + NS)
                            pe.wait_ge(y_free, b + 1)
                            for j in range(TB):
                                for n in range(NS):
                                    last = nc.tensor.matmul(yp[:, sl, j // 2, (j % 2) * D:(j % 2 + 1) * D],
                                                            hid[:, n, j * P:(j + 1) * P], sw2[:, n, :], start=(n == 0), stop=(n == NS - 1))
                            last.then_inc(y_full, 1)

                @block.scalar
                def _(act):
                    with act.Fori(0, B) as b:
                        for n in range(NS):
                            act.wait_ge(h_full, b * NS + n + 1)
                            nc.scalar.activation(act_out[:, n, :], hp[:, n, 0, :], ACT.Silu).then_inc(silu_done, 1)

                @block.vector
                def _(dve):
                    dve.sem_inc(h_free, NS)
                    dve.sem_inc(y_free, 2)

                    def batch(b, sl, first):
                        for j in range(TB):
                            t = b * TB + j
                            if not first:
                                dve.wait_ge(scattered[j], b * TOP * 16)
                            nc.vector.tensor_scalar(xn[:, j, :], x[:, t, :], mean[:, bass.ds(t, 1)], rstd[:, bass.ds(t, 1)],
                                                    ALU.subtract, ALU.mult).then_inc(rows_ready, 1)
                            nc.vector.tensor_copy(now[:, j, :], place[:, t, :]).then_inc(rows_ready, 1)
                        for n in range(NS):
                            dve.wait_ge(silu_done, b * NS + n + 1)
                            nc.vector.tensor_tensor(hid[:, n, :], act_out[:, n, :], hp[:, n, 1, :], ALU.mult).then_inc(h_free, 1)
                        dve.wait_ge(y_full, b + 1)
                        dve.wait_ge(rows_ready, b * 2 * TB + 2 * TB)
                        for m in range(2):
                            xs = x[:, bass.ds(b * TB + 2 * m, 2), :].rearrange("p j n -> p (j n)")
                            last = nc.vector.tensor_tensor(xs, xs, yp[:, sl, m, :], ALU.add)
                        last.then_inc(y_free, 1)

                    batch(0, 0, True)
                    batch(1, 1, False)
                    with dve.Fori(1, TURNS) as i:
                        for sl in range(2):
                            batch(i * 2 + sl, sl, False)
                    dve.wait_ge(y_free, B + 2)

        with ExitStack() as own2:
            k2 = Kit(nc, own2, "mr_e_")
            xt = k2.sb("xt", [P, UNROLL, D])
            xtT = k2.sb("xtT", [P, 2, DC, P])
            act_out = k2.sb("act_out", [P, 2, F])
            hid = k2.sb("hid", [P, 2, F])
            hidT = k2.sb("hidT", [P, 2, P])
            y = k2.sb("y", [P, UNROLL, D])
            xp = k2.ps("xp", [P, 2, S])
            hp = k2.ps("hp", [P, 2, S])
            hq = k2.ps("hq", [P, 2, S])
            yp = k2.ps("yp", [P, 2, S])
            x_loaded = [s.sem(f"x_loaded{j}") for j in range(UNROLL)]
            y_stored = [s.sem(f"y_stored{j}") for j in range(UNROLL)]
            xp_full, xt_ready = s.sem("xp_full"), s.sem("xt_ready")
            hp_full, silu_done, hid_ready = s.sem("hp_full"), s.sem("silu_done"), s.sem("hid_ready")
            hq_full, hidT_ready = s.sem("hq_full"), s.sem("hidT_ready")
            yp_full, y_ready = s.sem("yp_full"), s.sem("y_ready")
            LOOPS = TILES // UNROLL
            with nc.Block() as block:
                @block.sync
                def _(sp):
                    def load(n, u):
                        sp.dma_start(xt[:, u, :], places[bass.ds(n * P, P), :]).then_inc(x_loaded[u], 16)

                    def store(n, u):
                        sp.wait_ge(y_ready, n + 1 + 2)
                        sp.dma_start(outputs[bass.ds(n * P, P), :], y[:, u, :]).then_inc(y_stored[u], 16)

                    def steps(i, first, last):
                        for u in range(UNROLL):
                            n = i * UNROLL + u
                            if not last:
                                sp.wait_ge(xp_full, n + 1)
                                load(n + UNROLL, u)
                            if not (first and u < LAG_S):
                                store(n - LAG_S, (u - LAG_S) % UNROLL)

                    for u in range(UNROLL):
                        sp.sem_inc(y_stored[u], 16)
                        load(u, u)
                    steps(0, True, False)
                    with sp.Fori(1, LOOPS - 1) as i:
                        steps(i, False, False)
                    steps(LOOPS - 1, False, True)
                    for u in range(UNROLL - LAG_S, UNROLL):
                        store((LOOPS - 1) * UNROLL + u, u)
                    for u in range(UNROLL):
                        sp.wait_ge(y_stored[u], LOOPS * 16 + 16)

                @block.tensor
                def _(pe):
                    regs_h = [pe.alloc_register(f"expert_h{u}") for u in range(UNROLL)]
                    regs_y = [pe.alloc_register(f"expert_y{u}") for u in range(UNROLL)]

                    def steps(i, first, last_ones):
                        pe.load(regs_h, expert_h[0:1, bass.ds(i * UNROLL, UNROLL)])
                        pe.load(regs_y, expert_y[0:1, bass.ds(i * UNROLL, UNROLL)])
                        for u in range(UNROLL):
                            n = i * UNROLL + u
                            if not last_ones:
                                pe.wait_ge(x_loaded[u], i * 16 + 16)
                                for c in range(DC):
                                    last = nc.tensor.transpose(xp[:, u % 2, c * P:(c + 1) * P], xt[:, u, c * P:(c + 1) * P], ident[:])
                                last.then_inc(xp_full, 1)
                            if not (first and u < 1) and not (last_ones and u > 0):
                                e, v = pe.snap(regs_h[u], min_val=0, max_val=E - 1), (u - LAG_H) % 2
                                pe.wait_ge(xt_ready, n)
                                for c in range(DC):
                                    last = nc.tensor.matmul(hp[:, v, 0:2 * F], xtT[:, v, c, :],
                                                            w1[:, bass.ds(e, 1), c, :].rearrange("p a n -> p (a n)"),
                                                            start=(c == 0), stop=(c == DC - 1))
                                last.then_inc(hp_full, 1)
                            if not (first and u < 2) and not (last_ones and u > 1):
                                v = u % 2
                                pe.wait_ge(hid_ready, n - 1)
                                nc.tensor.transpose(hq[:, v, 0:P], hid[:, v, :], ident[:]).then_inc(hq_full, 1)
                            if not (first and u < 3) and not (last_ones and u > 2):
                                e, v = pe.snap(regs_y[u], min_val=0, max_val=E - 1), (u - LAG_Y) % 2
                                pe.wait_ge(hidT_ready, n - LAG_Y + 1)
                                pe.wait_ge(y_ready, n - LAG_Y + 1)
                                nc.tensor.matmul(yp[:, v, 0:D], hidT[:, v, :], w2[:, bass.ds(e, 1), :].rearrange("p a n -> p (a n)"),
                                                 start=True, stop=True).then_inc(yp_full, 1)

                    steps(0, True, False)
                    with pe.Fori(1, LOOPS) as i:
                        steps(i, False, False)
                    steps(LOOPS, False, True)

                @block.scalar
                def _(act):
                    def steps(i, first, last_ones):
                        for u in range(UNROLL):
                            n = i * UNROLL + u
                            if not last_ones:
                                act.wait_ge(xp_full, n + 1)
                                nc.scalar.activation(xtT[:, u % 2].rearrange("p c n -> p (c n)"), xp[:, u % 2, 0:D], ACT.Copy)\
                                    .then_inc(xt_ready, 1)
                            if not (first and u < 1) and not (last_ones and u > 0):
                                v = (u - 1) % 2
                                act.wait_ge(hp_full, n)
                                nc.scalar.activation(act_out[:, v, :], hp[:, v, 0:F], ACT.Silu).then_inc(silu_done, 1)
                            if not (first and u < 2) and not (last_ones and u > 1):
                                v = u % 2
                                act.wait_ge(hq_full, n - 1)
                                nc.scalar.activation(hidT[:, v, :], hq[:, v, 0:P], ACT.Copy).then_inc(hidT_ready, 1)

                    steps(0, True, False)
                    with act.Fori(1, LOOPS) as i:
                        steps(i, False, False)
                    steps(LOOPS, False, True)

                @block.vector
                def _(dve):
                    dve.sem_inc(y_ready, 2)

                    def steps(i, first, last_ones):
                        for u in range(UNROLL):
                            n = i * UNROLL + u
                            if not (first and u < 1) and not (last_ones and u > 0):
                                v = (u - 1) % 2
                                dve.wait_ge(silu_done, n)
                                nc.vector.tensor_tensor(hid[:, v, :], act_out[:, v, :], hp[:, v, F:2 * F], ALU.mult).then_inc(hid_ready, 1)
                            if not (first and u < 3) and not (last_ones and u > 2):
                                v = (u - LAG_Y) % UNROLL
                                dve.wait_ge(yp_full, n - LAG_Y + 1)
                                dve.wait_ge(y_stored[v], i * 16 + (16 if u >= LAG_Y else 0))
                                nc.vector.tensor_copy(y[:, v, :], yp[:, v % 2, 0:D]).then_inc(y_ready, 1)

                    steps(0, True, False)
                    with dve.Fori(1, LOOPS) as i:
                        steps(i, False, False)
                    steps(LOOPS, False, True)

        with ExitStack() as own2:
            k2 = Kit(nc, own2, "mr_c_")
            SLOTS = 4
            row = k2.sb("row", [P, SLOTS, TOP, D])
            now = k2.sb("now", [P, SLOTS, TOP], I32)
            wait_ready, taken, passed2 = s.sem("now_ready"), s.sem("taken"), s.sem("passed2")
            with nc.Block() as block:
                @block.gpsimd
                def _(pool):
                    with pool.Fori(0, NT // SLOTS) as i:
                        for j in range(SLOTS):
                            pool.wait_ge(wait_ready, i * SLOTS + j + 1)
                            pool.sem_inc(passed2, 1)
                            for n in range(TOP):
                                nc.gpsimd.indirect_dma_start(out=row[:, j, n, :], out_offset=None, in_=outputs[:, :],
                                                             in_offset=bass.IndirectOffsetOnAxis(ap=now[:, j, n:n + 1], axis=0))\
                                    .then_inc(gathered[j], 16)

                @block.vector
                def _(dve):
                    for j in range(SLOTS):
                        nc.vector.tensor_copy(now[:, j, :], place[:, j, :]).then_inc(wait_ready, 1)

                    def add(i, more):
                        for j in range(SLOTS):
                            t = i * SLOTS + j
                            dve.wait_ge(gathered[j], i * 16 * TOP + 16 * TOP)
                            for n in range(TOP):
                                nc.vector.scalar_tensor_tensor(x[:, bass.ds(t, 1), :].rearrange("p a n -> p (a n)"), row[:, j, n, :],
                                                               weight[:, bass.ds(t, 1), n], x[:, bass.ds(t, 1), :].rearrange("p a n -> p (a n)"),
                                                               ALU.mult, ALU.add).then_inc(taken, 1)
                                dve.wait_ge(taken, (i * SLOTS + j) * TOP + n + 1)
                            if more:
                                nc.vector.tensor_copy(now[:, j, :], place[:, t + SLOTS, :]).then_inc(wait_ready, 1)

                    with dve.Fori(0, NT // SLOTS - 1) as i:
                        add(i, True)
                    add(NT // SLOTS - 1, False)
        s.clear()


def experts_in_turn(eng, n, one):
    one(0, 0, 0, True)
    with eng.Fori(0, n // 2 - 1) as i:
        one(i * 2 + 1, 1, i, False)
        one(i * 2 + 2, 0, i + 1, False)
    one(n - 1, 1, n // 2 - 1, False)


def mix_experts_sparse(nc, ctx, x, ident, mean, rstd, w_gate, w_exp, sw_in, sw_out, rows, y_dram, out):
    with ExitStack() as own:
        k = Kit(nc, own, "me_")
        s = Kit(nc, own, "me_")
        E, TOP, CAP, F = 64, 8, 160, 768
        T = B * S
        FC = F // P
        HALF = NT // 2
        TH = T // 2
        TAIL = CAP - P
        ROUNDS = CAP // 8
        passed = s.sem("passed")
        lists = k.sb("lists", [P, CAP])
        index_a = k.sb("index_a", [P, E], I32)
        index_b = k.sb("index_b", [TAIL, E], I32)
        with ExitStack() as own2:
            k2 = Kit(nc, own2, "me_r_")
            xnT = k2.sb("xnT", [P, DC, T])
            key = k2.sb("key", [P, TH])
            with ExitStack() as own3:
                k3 = Kit(nc, own3, "me_g_")
                gates = k3.sb("gates", [P, NT, E])
                normed_and_logits(nc, ctx, "me", x, ident, mean, rstd, w_gate, E, xnT, gates, rows)
                left = k3.sb("left", [P, NT, E])
                sel = k3.sb("sel", [P, HALF, 2, E])
                top = k3.sb("top", [P, NT, 8])
                nmax = k3.sb("nmax", [P, NT])
                total = k3.sb("total", [P, NT])
                ones = k3.sb("ones", [P, TH])
                selT = k3.sb("selT", [P, TH])
                count = k3.sb("count", [P, TH])
                before = k3.sb("before", [P, 1])
                order = k3.sb("order", [P, TH])
                zero = k3.sb("zero", [P, D + E])
                sp4 = k3.ps("sp4", [P, TH])
                exp_go, exp_ready, chained, top_done = s.sem("exp_go"), s.sem("exp_ready"), s.sem("chained"), s.sem("top_done")
                sel_ready, selT_full, counted, moved = s.sem("sel_ready"), s.sem("selT_full"), s.sem("counted"), s.sem("moved")
                gates_ready, stored, order_ready, zero_ready = s.sem("gates_ready"), s.sem("stored"), s.sem("order_ready"), s.sem("zero_ready")
                with nc.Block() as block:
                    @block.gpsimd
                    def _(pool):
                        nc.gpsimd.iota(order[:], pattern=[[-1, TH]], base=TH, channel_multiplier=0,
                                       allow_small_or_imprecise_dtypes=True).then_inc(order_ready, 1)

                    @block.sync
                    def _(sp):
                        sp.wait_ge(zero_ready, 1)
                        sp.dma_start(rows[T:T + P, :], zero[:]).then_inc(stored, 16)
                        sp.dma_start(rows[T + P:T + CAP, :], zero[0:TAIL, :]).then_inc(stored, 16)
                        sp.dma_start(y_dram[T:T + P, :], zero[:, 0:D]).then_inc(stored, 16)
                        sp.dma_start(y_dram[T + P:T + CAP, :], zero[0:TAIL, 0:D]).then_inc(stored, 16)
                        sp.wait_ge(counted, 1)
                        sp.dma_start(before[P // 2:P, :], count[0:P // 2, TH - 1:TH]).then_inc(moved, 16)
                        sp.wait_ge(gates_ready, 1)
                        sp.dma_start(rows[0:T, D:D + E].rearrange("(j p) e -> p j e", p=P), gates[:]).then_inc(stored, 16)
                        sp.wait_ge(stored, 80)
                        sp.wait_ge(moved, 16)

                    @block.scalar
                    def _(act):
                        act.wait_ge(exp_go, 1)
                        nc.scalar.activation(gates[:], gates[:], ACT.Exp).then_inc(exp_ready, 1)

                    @block.tensor
                    def _(pe):
                        pe.wait_ge(sel_ready, 1)
                        for j in range(HALF):
                            last = nc.tensor.transpose(sp4[:, j * P:(j + 1) * P], sel[:, j].rearrange("p a e -> p (a e)"), ident[:])
                        last.then_inc(selT_full, 1)

                    @block.vector
                    def _(dve):
                        chain = Chain(dve, chained)
                        nc.vector.memset(zero[:], 0.0).then_inc(zero_ready, 1)
                        chain.link(nc.vector.memset(before[:], 0.0))
                        chain.link(nc.vector.memset(ones[:], 1.0))
                        softmax_scores(nc, dve, chain, gates, nmax, total, exp_ready, exp_go)
                        for t in range(NT):
                            nc.vector.max(top[:, t, :], gates[:, t, :]).then_inc(top_done, 1)
                        dve.wait_ge(top_done, NT)
                        for t in range(NT):
                            nc.vector.match_replace(left[:, t, :], top[:, t, :], gates[:, t, :], -1.0).then_inc(top_done, 1)
                        dve.wait_ge(top_done, 2 * NT)
                        chain.link(nc.vector.tensor_scalar(left[:], left[:], -1.0, None, ALU.is_equal))
                        for a in range(2):
                            last = nc.vector.tensor_copy(sel[:, :, a, :], left[:, a * HALF:(a + 1) * HALF, :])
                            chain.tick(last)
                        chain.wait()
                        dve.sem_inc(sel_ready, 1)
                        chain.link(nc.vector.tensor_reduce(total[:], top[:], AX.X, ALU.add))
                        chain.link(nc.vector.tensor_scalar(total[:], total[:], float(np.finfo(np.float32).eps), None, ALU.max))
                        chain.link(nc.vector.reciprocal(total[:], total[:]))
                        chain.link(nc.vector.tensor_tensor(gates[:], gates[:], left[:], ALU.mult))
                        nc.vector.tensor_tensor(gates[:], gates[:], total[:].unsqueeze(2).to_broadcast([P, NT, E]), ALU.mult)\
                            .then_inc(gates_ready, 1)
                        dve.wait_ge(selT_full, 1)
                        chain.link(nc.vector.tensor_copy(selT[:], sp4[:]))
                        nc.vector.tensor_tensor_scan(count[:], ones[:], selT[:], 0.0, ALU.mult, ALU.add).then_inc(counted, 1)
                        dve.wait_ge(moved, 16)
                        chain.link(nc.vector.tensor_scalar(count[:], count[:], before[:], float(CAP), ALU.add, ALU.is_le))
                        chain.link(nc.vector.tensor_tensor(selT[:], selT[:], count[:], ALU.mult))
                        dve.wait_ge(order_ready, 1)
                        chain.link(nc.vector.tensor_tensor(key[:], selT[:], order[:], ALU.mult))

            sw1 = k2.sb("sw1", [P, DC, 2 * F])
            sw2 = k2.sb("sw2", [P, FC, D])
            act_out = k2.sb("act_out", [P, 2, S])
            hid = k2.sb("hid", [P, FC, S])
            best = k2.sb("best", [P, ROUNDS // TURNS, 8])
            hp = k2.ps("hp", [P, 2, 2, S])
            yp = k2.ps("yp", [P, 4, S])
            loaded, h_full, silu_done, h_free = s.sem("sh_loaded"), s.sem("sh_h_full"), s.sem("sh_silu_done"), s.sem("sh_h_free")
            y_full, y_free, listed, y_stored, x_ready = s.sem("sh_y_full"), s.sem("sh_y_free"), s.sem("listed"), s.sem("y_stored"), s.sem("x_ready")
            lists_ready = s.sem("lists_ready")
            with nc.Block() as block:
                @block.sync
                def _(sp):
                    sp.dma_start(sw1[:], sw_in.rearrange("(c p) n -> p c n", p=P)).then_inc(loaded, 16)
                    sp.dma_start(sw2[:], sw_out.rearrange("(c p) n -> p c n", p=P)).then_inc(loaded, 16)
                    sp.wait_ge(x_ready, B)
                    sp.dma_start(y_dram[0:T, :].rearrange("(j p) d -> p j d", p=P), x[:]).then_inc(y_stored, 16)
                    sp.wait_ge(y_stored, 16)

                @block.tensor
                def _(pe):
                    pe.wait_ge(loaded, 32)
                    with pe.Fori(0, TURNS) as i:
                        for sl in range(2):
                            b = i * 2 + sl
                            for f in range(FC):
                                pe.wait_ge(h_free, b * FC + f + 1)
                                for half in range(2):
                                    for c in range(DC):
                                        at = half * F + f * P
                                        last = nc.tensor.matmul(hp[:, f % 2, half, :], sw1[:, c, at:at + P],
                                                                xnT[:, c, bass.ds(b * S, S)], start=(c == 0), stop=(c == DC - 1))
                                last.then_inc(h_full, 1)
                            pe.wait_ge(h_free, b * FC + FC + 2)
                            pe.wait_ge(y_free, b + 1)
                            for j in range(TB):
                                for f in range(FC):
                                    last = nc.tensor.matmul(yp[:, 2 * sl + j // 2, (j % 2) * D:(j % 2 + 1) * D],
                                                            hid[:, f, j * P:(j + 1) * P], sw2[:, f, :],
                                                            start=(f == 0), stop=(f == FC - 1))
                            last.then_inc(y_full, 1)

                @block.scalar
                def _(act):
                    with act.Fori(0, TURNS) as i:
                        for sl in range(2):
                            for f in range(FC):
                                at = (i * 2 + sl) * FC + f
                                act.wait_ge(h_full, at + 1)
                                act.wait_ge(h_free, at + 1)
                                nc.scalar.activation(act_out[:, f % 2, :], hp[:, f % 2, 1, :], ACT.Silu).then_inc(silu_done, 1)

                @block.vector
                def _(dve):
                    dve.sem_inc(h_free, 2)
                    dve.sem_inc(y_free, 2)
                    with dve.Fori(0, TURNS) as i:
                        for sl in range(2):
                            b = i * 2 + sl
                            for f in range(FC):
                                dve.wait_ge(silu_done, b * FC + f + 1)
                                nc.vector.tensor_tensor(hid[:, f, :], act_out[:, f % 2, :], hp[:, f % 2, 0, :], ALU.mult)\
                                    .then_inc(h_free, 1)
                                r = sl * 3 + f - 1
                                if 1 <= f < 4 and r < ROUNDS // TURNS:
                                    at = (i * (ROUNDS // TURNS) + r) * 2
                                    nc.vector.max(best[:, r, :], key[:]).then_inc(listed, 1)
                                    dve.wait_ge(listed, at + 1)
                                    dve.sem_inc(passed, 1)
                                    nc.vector.match_replace(key[:], best[:, r, :], key[:], 0.0).then_inc(listed, 1)
                                    dve.wait_ge(listed, at + 2)
                            dve.wait_ge(y_full, b + 1)
                            for m in range(2):
                                xs = x[:, bass.ds(b * TB + 2 * m, 2), :].rearrange("p j n -> p (j n)")
                                last = nc.vector.tensor_tensor(xs, xs, yp[:, 2 * sl + m, :], ALU.add)
                            last.then_inc(x_ready, 1)
                            dve.wait_ge(x_ready, b + 1)
                            dve.sem_inc(y_free, 1)
                        nc.vector.tensor_copy(lists[:, bass.ds(i * (CAP // TURNS), CAP // TURNS)],
                                              best[:].rearrange("p r n -> p (r n)")).then_inc(lists_ready, 1)
                        dve.wait_ge(lists_ready, i + 1)

        with ExitStack() as own2:
            k2 = Kit(nc, own2, "me_i_")
            start = k2.sb("start", [P, 1])
            found = k2.sb("found", [P, CAP])
            token = k2.sb("token", [P, CAP])
            flipped = k2.sb("flipped", [P, CAP])
            place = k2.sb("place", [P, 1])
            spare = k2.sb("spare", [P, 2, 1])
            both = k2.sb("both", [P, 2, E])
            empty = k2.sb("empty", [P, 2, E])
            tT = k2.ps("tT", [P, 2, P])
            chained, ready, turned, iota_done = s.sem("i_chained"), s.sem("i_ready"), s.sem("i_turned"), s.sem("i_iota_done")
            with nc.Block() as block:
                @block.gpsimd
                def _(pool):
                    nc.gpsimd.iota(place[:], pattern=[[0, 1]], base=T + 1, channel_multiplier=1,
                                   allow_small_or_imprecise_dtypes=True).then_inc(iota_done, 1)

                @block.tensor
                def _(pe):
                    pe.wait_ge(ready, 1)
                    nc.tensor.transpose(tT[:, 0, :], flipped[:, 0:P], ident[:])
                    nc.tensor.transpose(tT[0:TAIL, 1, :], flipped[:, P:CAP], ident[:]).then_inc(turned, 1)

                @block.vector
                def _(dve):
                    chain = Chain(dve, chained)
                    chain.tick(nc.vector.memset(start[0:P // 2, :], float(TH + 1)))
                    chain.link(nc.vector.memset(start[P // 2:P, :], float(T + 1)))
                    chain.link(nc.vector.tensor_scalar(found[:], lists[:], 0.0, None, ALU.is_gt))
                    chain.link(nc.vector.tensor_scalar(token[:], lists[:], -1.0, start[:], ALU.mult, ALU.add))
                    chain.link(nc.vector.tensor_tensor(token[:], token[:], found[:], ALU.mult))
                    chain.tick(nc.vector.tensor_copy(flipped[0:P // 2, :], token[0:P // 2, :]))
                    chain.tick(nc.vector.tensor_copy(flipped[P // 2:P, :], token[P // 2:P, ::-1]))
                    chain.wait()
                    dve.sem_inc(ready, 1)
                    dve.wait_ge(iota_done, 1)
                    chain.tick(nc.vector.tensor_copy(spare[:, 0, :], place[:]))
                    chain.tick(nc.vector.tensor_scalar(spare[:, 1, :], place[:], float(P), None, ALU.add))
                    chain.wait()
                    dve.wait_ge(turned, 1)
                    for a, (n, index) in enumerate(((P, index_a), (TAIL, index_b))):
                        t, e = both[0:n, a, :], empty[0:n, a, :]
                        chain.link(nc.vector.tensor_copy(t, tT[0:n, a, 0:E]))
                        chain.link(nc.vector.tensor_tensor(t, t, tT[0:n, a, E:2 * E], ALU.add))
                        chain.link(nc.vector.tensor_scalar(e, t, 0.0, spare[0:n, a, :], ALU.is_equal, ALU.mult))
                        chain.link(nc.vector.scalar_tensor_tensor(t, t, -1.0, e, ALU.add, ALU.add))
                        chain.link(nc.vector.tensor_copy(index[:], t))

        w = k.sb("w", [P, 2, DC * 2 * F + FC * D])
        w1 = w[:, :, 0:DC * 2 * F].rearrange("p a (c n) -> p a c n", c=DC)
        w2 = w[:, :, DC * 2 * F:].rearrange("p a (c n) -> p a c n", c=FC)
        xa = k.sb("xa", [P, 2, D + E])
        xb = k.sb("xb", [TAIL, 2, D + E])
        now_a = k.sb("now_a", [P, 2, 1], I32)
        now_b = k.sb("now_b", [TAIL, 2, 1], I32)
        index_ready = s.sem("index_ready")
        xgT = k.sb("xgT", [P, DC, CAP])
        act_out = k.sb("act_out", [P, 2, CAP])
        hid = k.sb("hid", [P, 2, FC, CAP])
        oT = k.sb("oT", [P, DC, CAP])
        oa = k.sb("oa", [P, 2, D])
        ob = k.sb("ob", [TAIL, 2, D])
        xp = k.ps("xp", [P, S])
        hp = k.ps("hp", [P, 3, S])
        op = k.ps("op", [P, DC, S])
        tp = k.ps("tp", [P, 2, S // 2])
        w_loaded, g_loaded = [s.sem("w_loaded0"), s.sem("w_loaded1")], [s.sem("g_loaded0"), s.sem("g_loaded1")]
        e_done, xp_full, xp_free = s.sem("e_done"), s.sem("xp_full"), s.sem("xp_free")
        h_full, silu_done, h_free = s.sem("h_full"), s.sem("silu_done"), s.sem("h_free")
        o_full, o_free, t_full, t_free, added = s.sem("o_full"), s.sem("o_free"), s.sem("t_full"), s.sem("t_free"), s.sem("added")
        rows_free = s.sem("rows_free")
        o_ready, final = s.sem("o_ready"), s.sem("final")

        with nc.Block() as block:
            @block.sync
            def _(sp):
                with sp.Fori(0, E // 2) as i:
                    for sl in range(2):
                        sp.wait_ge(e_done, i * 2 + sl + 1)
                        sp.dma_start(w[:, sl, :], w_exp[bass.ds(i * 2 + sl, 1)].rearrange("a p n -> p (a n)")).then_inc(w_loaded[sl], 16)
                sp.wait_ge(added, 32 * E)
                sp.dma_start(out[:, :], y_dram[0:T, :]).then_inc(final, 16)
                sp.wait_ge(final, 16)

            @block.gpsimd
            def _(pool):
                def gather(e, sl):
                    nc.gpsimd.tensor_copy(now_a[:, sl, :], index_a[:, bass.ds(e, 1)]).then_inc(index_ready, 1)
                    nc.gpsimd.tensor_copy(now_b[:, sl, :], index_b[:, bass.ds(e, 1)]).then_inc(index_ready, 1)
                    pool.wait_ge(index_ready, e * 2 + 2)
                    pool.sem_inc(passed, 1)
                    for dst, index in ((xa, now_a), (xb, now_b)):
                        nc.gpsimd.indirect_dma_start(out=dst[:, sl, :], out_offset=None, in_=rows[:, :],
                                                     in_offset=bass.IndirectOffsetOnAxis(ap=index[:, sl, :], axis=0))\
                            .then_inc(g_loaded[sl], 16)

                def scatter(e, sl):
                    pool.wait_ge(o_ready, e + 1)
                    pool.sem_inc(passed, 1)
                    for src, index in ((oa, now_a), (ob, now_b)):
                        nc.gpsimd.indirect_dma_start(out=y_dram[:, :],
                                                     out_offset=bass.IndirectOffsetOnAxis(ap=index[:, sl, :], axis=0),
                                                     in_=src[:, sl, :], in_offset=None, compute_op=ALU.add).then_inc(added, 16)
                    pool.wait_ge(added, e * 32 + 32)
                    pool.sem_inc(rows_free, 1)

                pool.sem_inc(rows_free, 2)
                gather(0, 0)
                gather(1, 1)
                with pool.Fori(0, E // 2 - 1) as i:
                    for sl in range(2):
                        scatter(i * 2 + sl, sl)
                        gather(i * 2 + sl + 2, sl)
                scatter(E - 2, 0)
                scatter(E - 1, 1)

            @block.tensor
            def _(pe):
                pe.sem_inc(e_done, 2)

                def turn_in(e, sl, earlier):
                    pe.wait_ge(g_loaded[sl], earlier * 32 + 32)
                    pe.wait_ge(xp_free, e + 1)
                    for c in range(DC):
                        cols = slice(c * P, (c + 1) * P)
                        nc.tensor.transpose(xp[:, c * CAP:c * CAP + P], xa[:, sl, cols], ident[:])
                        last = nc.tensor.transpose(xp[:, c * CAP + P:(c + 1) * CAP], xb[:, sl, cols], ident[0:TAIL, 0:TAIL])
                    last.then_inc(xp_full, 1)

                def turn_out(e):
                    pe.wait_ge(o_free, e + 2)
                    pe.wait_ge(t_free, e + 1)
                    for c in range(DC):
                        cols = slice(c * P, (c + 1) * P)
                        nc.tensor.transpose(tp[:, 0, cols], oT[:, c, 0:P], ident[:])
                        last = nc.tensor.transpose(tp[0:TAIL, 1, cols], oT[:, c, P:CAP], ident[:])
                    last.then_inc(t_full, 1)

                def one(e, sl, earlier, first):
                    turn_in(e, sl, earlier)
                    pe.wait_ge(xp_free, e + 2)
                    pe.wait_ge(w_loaded[sl], earlier * 16 + 16)
                    for f in range(FC):
                        at = e * FC + f
                        pe.wait_ge(h_free, at + 1)
                        for half in range(2):
                            for c in range(DC):
                                cols = slice(half * F + f * P, half * F + (f + 1) * P)
                                last = nc.tensor.matmul(hp[:, f % 3, half * CAP:(half + 1) * CAP], w1[:, sl, c, cols], xgT[:, c, :],
                                                        start=(c == 0), stop=(c == DC - 1))
                        last.then_inc(h_full, 1)
                        if f == 1 and not first:
                            turn_out(e - 1)
                    pe.wait_ge(o_free, e + 1)
                    for f in range(FC):
                        pe.wait_ge(h_free, e * FC + f + 1 + 3)
                        for c in range(DC):
                            last = nc.tensor.matmul(op[:, c, 0:CAP], w2[:, sl, f, c * P:(c + 1) * P], hid[:, sl, f, :],
                                                    start=(f == 0), stop=(f == FC - 1))
                    last.then_inc(o_full, 1)
                    pe.wait_ge(o_full, e + 1)
                    pe.sem_inc(e_done, 1)

                experts_in_turn(pe, E, one)
                turn_out(E - 1)

            @block.scalar
            def _(act):
                act.sem_inc(o_free, 1)

                def one(e, sl, earlier, first):
                    for f in range(FC):
                        at = e * FC + f
                        act.wait_ge(h_full, at + 1)
                        act.wait_ge(h_free, at + 2)
                        nc.scalar.activation(act_out[:, f % 2, :], hp[:, f % 3, CAP:2 * CAP], ACT.Silu).then_inc(silu_done, 1)
                    act.wait_ge(o_full, e + 1)
                    nc.scalar.activation(oT[:], op[:, :, 0:CAP], ACT.Copy).then_inc(o_free, 1)

                experts_in_turn(act, E, one)

            @block.vector
            def _(dve):
                dve.sem_inc(xp_free, 1)
                dve.sem_inc(h_free, 3)
                dve.sem_inc(t_free, 1)

                def weigh(e, sl):
                    dve.wait_ge(t_full, e + 1)
                    dve.wait_ge(rows_free, e + 1)
                    nc.vector.tensor_scalar(oa[:, sl, :], tp[:, 0, :], xa[:, sl, bass.ds(e + D, 1)], None, ALU.mult).then_inc(t_free, 1)
                    nc.vector.tensor_scalar(ob[:, sl, :], tp[0:TAIL, 1, :], xb[:, sl, bass.ds(e + D, 1)], None, ALU.mult)\
                        .then_inc(o_ready, 1)

                def one(e, sl, earlier, first):
                    dve.wait_ge(xp_full, e + 1)
                    nc.vector.tensor_copy(xgT[:], xp[:, 0:DC * CAP].rearrange("p (c n) -> p c n", c=DC)).then_inc(xp_free, 1)
                    for f in range(FC):
                        dve.wait_ge(silu_done, e * FC + f + 1)
                        nc.vector.tensor_tensor(hid[:, sl, f, :], act_out[:, f % 2, :], hp[:, f % 3, 0:CAP], ALU.mult).then_inc(h_free, 1)
                        if f == 1 and not first:
                            weigh(e - 1, 1 - sl)

                experts_in_turn(dve, E, one)
                weigh(E - 1, 1)
        s.clear()


def program(nc, a, out):
    scratch = {name: nc.dram_tensor(name, shape, dtype).ap() for name, shape, dtype in (
        ("lag_products", [P, 2 * S], F32), ("lag_weights", [1, 3 * S], F32),
        ("part_rows", [2, 3, D, S], BF16), ("mask_rows", [B, S], BF16),
        ("places", [161 * P, D], F32), ("outputs", [161 * P, D], F32),
        ("token_rows", [B * S + 160, D + 64], F32), ("sums", [B * S + 160, D], F32))}
    with ExitStack() as ctx:
        k = Kit(nc, ctx, "all_")
        x = k.sb("x", [P, NT, D])
        ident = k.sb("ident", [P, P])
        ident_bf = k.sb("ident_bf", [P, P], BF16)
        mean = k.sb("mean", [P, NT])
        rstd = k.sb("rstd", [P, NT])
        x_loaded = k.sem("x_loaded")
        scattered = [k.sem(f"scattered{j}") for j in range(TB)]
        gathered = [k.sem(f"gathered{j}") for j in range(TB)]
        identity_stage(nc, ctx, ident, ident_bf)
        with ExitStack() as early:
            ROWS = 7
            zero = Kit(nc, early, "z_").sb("zero", [P, ROWS, D])
            zero_ready, cleared = k.sem("zero_ready"), k.sem("cleared")
            places, outputs = scratch["places"], scratch["outputs"]
            n_tiles = places.shape[0] // P
            with nc.Block() as block:
                @block.gpsimd
                def _(pool):
                    nc.gpsimd.memset(zero[:], 0.0).then_inc(zero_ready, 1)

                @block.sync
                def _(sp):
                    sp.dma_start(x[:], a["x"].rearrange("b (j p) d -> p (b j) d", p=P)).then_inc(x_loaded, 16)
                    sp.wait_ge(x_loaded, 16)
                    sp.wait_ge(zero_ready, 1)
                    with sp.Fori(0, n_tiles // ROWS) as i:
                        sp.dma_start(places[bass.ds(i * (ROWS * P), ROWS * P), :].rearrange("(j p) d -> p j d", p=P), zero[:])\
                            .then_inc(cleared, 16)
                    sp.dma_start(outputs[(n_tiles - 1) * P:n_tiles * P, :], zero[:, 0, :]).then_inc(cleared, 16)
            norm_stats(nc, ctx, "l0a", x, mean, rstd)
            mix_attention(nc, ctx, x, ident, ident_bf, mean, rstd, a["L0_attn_weight_qkv"], a["L0_attn_out_wT"], a["L0_attn_out_b"])
            norm_stats(nc, ctx, "l0x", x, mean, rstd)
            mix_correlation(nc, ctx, x, ident, mean, rstd, a["ctx_1024"], a["L0_xattn_Wq"], a["L0_xattn_bq"], a["L0_xattn_Wout"],
                            a["L0_xattn_bout"], scratch["lag_products"], scratch["lag_weights"])
            with nc.Block() as block:
                @block.sync
                def _(sp):
                    sp.wait_ge(cleared, 16 * (n_tiles // ROWS) + 16)
        norm_stats(nc, ctx, "l0f", x, mean, rstd)
        mix_experts_routed(nc, ctx, x, ident, mean, rstd, a["L0_ffn_Wg"], a["L0_ffn_w_in"], a["L0_ffn_w_out"], places, outputs,
                           scattered, gathered)
        norm_stats(nc, ctx, "l1a", x, mean, rstd)
        mix_recurrence(nc, ctx, x, ident, mean, rstd, a["L1_attn_A"], a["L1_attn_BC"])
        norm_stats(nc, ctx, "l1x", x, mean, rstd)
        mix_heads(nc, ctx, x, ident, ident_bf, mean, rstd, a["ctx_1024"], a["mask"], a["L1_xattn_WvT"], a["L1_xattn_WkT"],
                  a["L1_xattn_WqT"], a["L1_xattn_WoT"], a["L1_xattn_bo"], scratch["part_rows"], scratch["mask_rows"])
        norm_stats(nc, ctx, "l1f", x, mean, rstd)
        mix_experts_sparse(nc, ctx, x, ident, mean, rstd, a["L1_ffn_wgT"], a["L1_ffn_w_exp"], a["L1_ffn_shared_w1T"],
                           a["L1_ffn_shared_w2T"], scratch["token_rows"], scratch["sums"], out)


def laid_out(i):
    i = {name: np.asarray(v) for name, v in i.items()}

    def by_partition(w):
        n, c, m = w.shape[0], w.shape[1] // P, w.shape[2]
        return w.reshape(n, c, P, m).transpose(0, 2, 1, 3).reshape(n, P, c * m)

    def slices(w, axis):
        return np.stack(np.split(w, w.shape[axis] // P, axis=axis))

    w1, w3, w2 = (np.concatenate([i[f"L0_ffn_W{n}"], slices(i[f"L0_ffn_Ws{n}"], axis)]) for n, axis in ((1, 1), (3, 1), (2, 0)))
    a = {name: i[name] for name in ("x", "ctx_1024", "L0_attn_weight_qkv", "L0_attn_out_b", "L0_xattn_Wq", "L0_xattn_bq",
                                    "L0_xattn_Wout", "L0_xattn_bout", "L0_ffn_Wg", "L1_attn_A", "L1_attn_BC", "L1_xattn_bo")}
    a["mask"] = i["mask_Bx1x1xS2_if1"]
    a["L0_ffn_w_in"] = by_partition(np.concatenate([w1, w3], axis=2))
    a["L0_ffn_w_out"] = w2
    a["L1_ffn_w_exp"] = np.concatenate([by_partition(i["L1_ffn_expert_w1"].transpose(0, 2, 1)),
                                        by_partition(i["L1_ffn_expert_w2"].transpose(0, 2, 1))], axis=2)
    for name in ("L0_attn_out_w", "L1_xattn_Wv", "L1_xattn_Wk", "L1_xattn_Wq", "L1_xattn_Wo", "L1_ffn_wg",
                 "L1_ffn_shared_w1", "L1_ffn_shared_w2"):
        a[name + "T"] = i[name].T
    return {name: np.ascontiguousarray(v) for name, v in a.items()}


def kernel(**inputs):
    import concourse.bacc as bacc
    from concourse.bass_utils import run_bass_kernel_spmd

    nc = bacc.Bacc("TRN2", target_bir_lowering=False, num_devices=1)
    arrays = laid_out(inputs)
    aps = {name: nc.dram_tensor("in_" + name, v.shape, mybir.dt.from_np(v.dtype), kind="ExternalInput").ap()
           for name, v in arrays.items()}
    out = nc.dram_tensor("out_x", (B * S, D), F32, kind="ExternalOutput").ap()
    program(nc, aps, out)
    r = run_bass_kernel_spmd(nc, [{"in_" + name: v for name, v in arrays.items()}], core_ids=[0])
    return r.results[0]["out_x"].reshape(B, S, D)
```
